# Optimizing a Trainium2 kernel written in Bass

```python
import numpy as np
import jax
import jax.numpy as jnp

def _softmax(x, axis=-1):
    return jax.nn.softmax(x, axis=axis)

def _gelu(x):
    return jax.nn.gelu(x, approximate=True)

def _silu(x):
    return jax.nn.silu(x)

def _sigmoid(x):
    return jax.nn.sigmoid(x)

def _layernorm(x, axis=-1, eps=1e-05):
    m = jnp.mean(x, axis=axis, keepdims=True)
    v = jnp.var(x, axis=axis, keepdims=True)
    return (x - m) / jnp.sqrt(v + eps)

def _scatter_add(tgt, idx, src, axis=0):
    return tgt.at[idx].add(src)

def _segment_sum(src, seg, n):
    return jax.ops.segment_sum(src, seg, n)
kernel_name = 'mk_gnn_ffn_d1_gnn_r8_753b46'

def setup_inputs(seed: int=0):
    np.random.seed(seed)
    _w = jnp.asarray

    def _rec_inputs():
        import jax
        import jax.numpy as jnp
        _gk = jax.random.key(seed)
        x = -0.0002117 + 1 * jax.random.normal(jax.random.fold_in(_gk, 1), (6250, 256), jnp.float32)
        src = jax.random.randint(jax.random.fold_in(_gk, 2), (200000,), 0, 6250, jnp.int32)
        dst = jnp.minimum((6250 * jax.random.uniform(jax.random.fold_in(_gk, 3), (200000,)) ** 2.0).astype(jnp.int32), 49999)
        _o = jnp.argsort(dst, stable=True)
        src = src[_o]
        dst = dst[_o]
        return (x, src, dst)
    x, src, dst = _rec_inputs()

    def _L0_gnn_setup():
        import jax, jax.numpy as jnp
        import numpy as np
        N = 12500
        D = 256
        E = 400000
        key = jax.random.key(seed)
        ks = jax.random.split(key, 8)
        x = jax.random.normal(ks[0], (N, D), dtype=jnp.float32)
        edge_index = jax.random.randint(ks[1], (2, E), 0, N, dtype=jnp.int64)
        s = 1.0 / np.sqrt(D)
        W_l = jax.random.uniform(ks[2], (D, D), dtype=jnp.float32, minval=-s, maxval=s)
        b_l = jax.random.uniform(ks[3], (D,), dtype=jnp.float32, minval=-s, maxval=s)
        W_r = jax.random.uniform(ks[4], (D, D), dtype=jnp.float32, minval=-s, maxval=s)
        ln_gamma = jnp.ones((D,), dtype=jnp.float32)
        ln_beta = jnp.zeros((D,), dtype=jnp.float32)
        return {'x': x, 'edge_index': edge_index, 'W_l': W_l, 'b_l': b_l, 'W_r': W_r, 'ln_gamma': ln_gamma, 'ln_beta': ln_beta}
    _L0_gnn_all = _L0_gnn_setup()
    _L0_gnn_in = {k: v for k, v in _L0_gnn_all.items() if k in ('W_l', 'b_l', 'W_r', 'ln_gamma', 'ln_beta')}
    del _L0_gnn_all

    def _L0_ffn_setup():
        import math
        import jax, jax.numpy as jnp
        import numpy as np
        CAPACITY_FACTOR = 1.25
        key = jax.random.key(seed)
        ks = jax.random.split(key, 5)
        B, L, D, F, E = (8, 1024, 256, 1024, 8)
        h = jax.random.normal(ks[0], (B, L, D), dtype=jnp.float32)
        gate_w = jax.random.normal(ks[1], (D, E), dtype=jnp.float32) * 0.02
        gate_b = jnp.zeros((E,), dtype=jnp.float32)
        w1 = jax.random.normal(ks[2], (E, D, F), dtype=jnp.float32) * (1.0 / math.sqrt(D))
        b1 = jnp.zeros((E, F), dtype=jnp.float32)
        w2 = jax.random.normal(ks[3], (E, F, D), dtype=jnp.float32) * (1.0 / math.sqrt(F))
        b2 = jnp.zeros((E, D), dtype=jnp.float32)
        return {'h': h, 'gate_w': gate_w, 'gate_b': gate_b, 'w1': w1, 'b1': b1, 'w2': w2, 'b2': b2}
    _L0_ffn_all = _L0_ffn_setup()
    _L0_ffn_in = {k: v for k, v in _L0_ffn_all.items() if k in ('gate_w', 'gate_b', 'w1', 'b1', 'w2', 'b2')}
    del _L0_ffn_all
    return {'x': x, 'src': src, 'dst': dst, 'L0_gnn_W_l': _L0_gnn_in['W_l'], 'L0_gnn_b_l': _L0_gnn_in['b_l'], 'L0_gnn_W_r': _L0_gnn_in['W_r'], 'L0_gnn_ln_gamma': _L0_gnn_in['ln_gamma'], 'L0_gnn_ln_beta': _L0_gnn_in['ln_beta'], 'L0_ffn_gate_w': _L0_ffn_in['gate_w'], 'L0_ffn_gate_b': _L0_ffn_in['gate_b'], 'L0_ffn_w1': _L0_ffn_in['w1'], 'L0_ffn_b1': _L0_ffn_in['b1'], 'L0_ffn_w2': _L0_ffn_in['w2'], 'L0_ffn_b2': _L0_ffn_in['b2']}

def reference(x, src, dst, L0_gnn_W_l, L0_gnn_b_l, L0_gnn_W_r, L0_gnn_ln_gamma, L0_gnn_ln_beta, L0_ffn_gate_w, L0_ffn_gate_b, L0_ffn_w1, L0_ffn_b1, L0_ffn_w2, L0_ffn_b2):
    import jax
    import jax.numpy as jnp

    def _L0_gnn_ref(x, edge_index, W_l, b_l, W_r, ln_gamma, ln_beta):
        import jax, jax.numpy as jnp
        import numpy as np
        N = 12500
        D = 256
        E = 400000
        src, dst = (edge_index[0], edge_index[1])
        n = x.shape[0]
        msg_sum = jax.ops.segment_sum(x[src], dst, num_segments=n)
        deg = jax.ops.segment_sum(jnp.ones((src.shape[0],), x.dtype), dst, num_segments=n)
        agg = msg_sum / jnp.maximum(deg, 1.0)[:, None]
        f = agg @ W_l.T + b_l + x @ W_r.T
        f = jax.nn.gelu(f, approximate=False)
        mu = jnp.mean(f, axis=-1, keepdims=True)
        var = jnp.var(f, axis=-1, keepdims=True)
        f = (f - mu) * jax.lax.rsqrt(var + 1e-05) * ln_gamma + ln_beta
        return f + x

    def _L0_ffn_ref(h, gate_w, gate_b, w1, b1, w2, b2):
        import math
        import jax, jax.numpy as jnp
        import numpy as np
        CAPACITY_FACTOR = 1.25
        B, L, D = h.shape
        E = gate_w.shape[1]
        T = B * L
        C = max(1, math.ceil(CAPACITY_FACTOR * T / E))
        x = h.reshape(T, D)
        logits = x @ gate_w + gate_b
        probs = jax.nn.softmax(logits, axis=-1)
        idx = jnp.argmax(probs, axis=-1)
        prb = jnp.take_along_axis(probs, idx[:, None], axis=1)[:, 0]
        one_hot = jax.nn.one_hot(idx, E, dtype=jnp.float32)
        pos = (jnp.cumsum(one_hot, axis=0) * one_hot).sum(-1).astype(jnp.int32) - 1
        kept = pos < C
        pos_safe = jnp.where(kept, pos, C)
        buf = jnp.zeros((E, C, D), dtype=h.dtype).at[idx, pos_safe].set(x, mode='drop')
        hmid = jax.nn.relu(jnp.einsum('ecd,edf->ecf', buf, w1) + b1[:, None, :])
        ybuf = jnp.einsum('ecf,efd->ecd', hmid, w2) + b2[:, None, :]
        pos_g = jnp.minimum(pos, C - 1)
        y_tok = ybuf[idx, pos_g] * (prb * kept)[:, None]
        y = y_tok.reshape(B, L, D)
        y = jnp.nan_to_num(y, nan=0.0, posinf=10000.0, neginf=-10000.0)
        return y
    edge_index = jnp.stack([src, dst])
    x = x + _L0_gnn_ref(_layernorm(x, axis=-1), edge_index, L0_gnn_W_l, L0_gnn_b_l, L0_gnn_W_r, L0_gnn_ln_gamma, L0_gnn_ln_beta)
    x = x + _L0_ffn_ref(_layernorm(x, axis=-1)[None], L0_ffn_gate_w, L0_ffn_gate_b, L0_ffn_w1, L0_ffn_b1, L0_ffn_w2, L0_ffn_b2)[0]
    return x

_drawn_inputs = setup_inputs


def setup_inputs(seed=0):
    import zlib

    import numpy as np

    out = dict(_drawn_inputs(seed))
    spreads = {'L0_gnn_ln_gamma': (1.0, 0.2),
     'L0_gnn_ln_beta': (0.0, 0.1),
     'L0_ffn_gate_b': (0.0, 0.1),
     'L0_ffn_b1': (0.0, 0.8),
     'L0_ffn_b2': (0.0, 0.8)}
    factors = {}
    for name, (base, spread) in spreads.items():
        noise = np.random.default_rng([zlib.crc32(name.encode()), seed]).standard_normal(out[name].shape)
        drawn = base * np.exp(spread * noise) if base else spread * noise
        out[name] = jnp.asarray(drawn.astype(out[name].dtype))
    for name, factor in factors.items():
        out[name] = (out[name] * factor).astype(out[name].dtype)
    return out
```

```python
from contextlib import ExitStack

import concourse.bass as bass
from concourse import mybir

F32 = mybir.dt.float32
I32 = mybir.dt.int32
ALU = mybir.AluOpType
ACT = mybir.ActivationFunctionType
AX = mybir.AxisListType

P = 128
N, D = 6250, 256
E = 200000
X, F = 8, 1024
CAP = -(-5 * N // (4 * X))
EPS = 1e-5
NT = -(-N // P)
LAST = N - (NT - 1) * P
DK = D // P
FK = F // P
ROW = D + 4
PROB, TOKEN, RSTD, NMR = D, D + 1, D + 2, D + 3
NOBODY = 1 << 20

G = 8
PAIRS = (NT - 1) // (2 * G)
assert NT == PAIRS * 2 * G + 1

COLS = 8
BLOCK = P * COLS
SLOTS = 3
BLOCKS = E // BLOCK
RUNS = BLOCKS // SLOTS
REST = E - BLOCKS * BLOCK
REST_COLS = 5
REST_ROWS = REST // REST_COLS
assert BLOCKS == RUNS * SLOTS and REST == REST_ROWS * REST_COLS and REST_ROWS <= P
CNT = D + 1
BP = 65
BPN = BLOCKS // BP
assert BLOCKS == BP * BPN

TOK_TILES = -(-CAP // P)
TOK_LAST = CAP - (TOK_TILES - 1) * P
HALVES = [(0, 512), (512, CAP - 512)]
RSQRT_GUESS = 0x5F3759DF


class Own:

    def __init__(self, eng, sem):
        self.eng, self.sem, self.n, self.off, self.per = eng, sem, 0, None, None

    def __call__(self, ins):
        ins.then_inc(self.sem, 1)
        self.n += 1
        return ins

    def wait(self):
        self.eng.wait_ge(self.sem, self.n if self.off is None else self.off + self.n)

    def wait_apart(self, passed):
        self.wait()
        self.eng.sem_inc(passed, 1)

    def enter(self, i, per):
        self.start, self.off, self.per = self.n, i * per, per

    def leave(self, trips):
        assert self.n - self.start == self.per, (self.n - self.start, self.per)
        self.n, self.off = self.start + self.per * trips, None


def groups(eng, body, own=None, per=0):
    with eng.Fori(0, PAIRS) as i:
        if own:
            own.enter(i, per)
        for b in range(2):
            body(i * (2 * G) + b * G, G, b, i * 2 + b)
    if own:
        own.leave(PAIRS)
    body(NT - 1, 1, 0, 2 * PAIRS)


def gnn_moe(nc, x, src, dst, w_l, b_l, w_r, gamma, beta, gate_w, gate_b, w1, b1, w2, b2, out):
    ctx = ExitStack()
    with ctx:
        def sb(name, shape, dt=F32):
            return ctx.enter_context(nc.sbuf_tensor(name, shape, dt))

        def ps(name, shape):
            return ctx.enter_context(nc.psum_tensor(name, shape, F32))

        def sem(name):
            return ctx.enter_context(nc.semaphore(name))

        xn_table = nc.dram_tensor("xn_table", (N, D), F32).ap()
        slot_table = nc.dram_tensor("slot_table", (X * CAP, ROW), F32).ap()
        range_table = nc.dram_tensor("range_table", (2 * (BLOCKS + 1),), I32).ap()

        rows = sb("rows", [P, NT, ROW])
        res = sb("res", [P, NT * D])
        resid = res[:, :].rearrange("p (t d) -> p t d", t=NT)
        sums_flat = sb("sums", [P, NT * CNT])
        sums = sums_flat[:, :].rearrange("p (t d) -> p t d", t=NT)
        gath_flat = sb("gath", [P, SLOTS * COLS * CNT])
        gath = gath_flat[:, :].rearrange("p (s k d) -> p s k d", s=SLOTS, k=COLS)
        stage = sb("stage", [P, 2, G, ROW])
        onehot = sb("onehot", [P, COLS, P])

        ident = sb("ident", [P, P])
        upper = sb("upper", [P, P])
        ones = sb("ones", [P, P])
        lane = sb("lane", [P, P])
        tile_base = sb("tile_base", [P, NT])
        w_l_sb = sb("w_l_sb", [P, DK, D])
        gamma_sb = sb("gamma_sb", [P, D])
        gate_w_sb = sb("gate_w_sb", [P, DK, X])
        gate_b_sb = sb("gate_b_sb", [P, X])
        b1_rows = sb("b1_rows", [X * FK, P])
        b1_sb = sb("b1_sb", [P, X * FK])
        b1_now = sb("b1_now", [P, 2, FK])
        xT = sb("xT", [P, 2, D])
        src_ix = sb("src_ix", [P, SLOTS, COLS], I32)
        dst_ix = sb("dst_ix", [P, SLOTS, COLS], I32)
        dst_rel = sb("dst_rel", [P, COLS])
        block_range = sb("block_range", [BP, BPN, 2], I32)
        rest_range = sb("rest_range", [1, 2], I32)
        range_row = sb("range_row", [1, 2 * (BLOCKS + 1)], I32)
        bn = sb("bn", [P, G, 6])
        mv = sb("mv", [P, G, 2])
        var = sb("var", [P, G])
        rs = sb("rs", [P, G])
        nt_ = sb("nt_", [P, G])
        nmr = sb("nmr", [P, G])
        rdeg = sb("rdeg", [P, NT])
        logits = sb("logits", [P, NT, X])
        fill = sb("fill", [P, ROW])

        dst_all = sums_flat[0:BP, 0:BPN * BLOCK].bitcast(I32).rearrange("p (b e) -> p b e", b=BPN)
        o = BPN * BLOCK
        rest_dst = sums_flat[0:1, o:o + REST].bitcast(I32)
        o += REST
        w_r_sb = sums_flat[:, o:o + DK * D].rearrange("p (k d) -> p k d", k=DK)
        o += DK * D
        b_l_sb = sums_flat[:, o:o + D]
        beta_sb = sums_flat[:, o + D:o + 2 * D]
        n8 = NT * X

        def route(k):
            return stage[:, :, :, :].rearrange("p a g r -> p (a g r)")[:, k * n8:(k + 1) * n8].rearrange(
                "p (t e) -> p t e", e=X)

        picked, score, descend, before, place = (route(k) for k in range(5))
        notfirst = route(5).rearrange("p t e -> p (t e)").rearrange("p (e t) -> p e t", e=X)
        small = sb("small", [P, 6, NT])
        slot_ix = sb("slot_ix", [P, NT], I32)
        token_ix = sb("token_ix", [P, NT], I32)
        hidden = sums_flat[:, 0:FK * CAP].rearrange("p (f c) -> p f c", f=FK)
        inT = sums_flat[:, FK * CAP:FK * CAP + DK * CAP].rearrange("p (k c) -> p k c", k=DK)
        w1_sb = [gath_flat[:, 0:DK * F], res[:, 0:DK * F]]
        w2_sb = [gath_flat[:, DK * F:DK * F + FK * D], res[:, DK * F:DK * F + FK * D]]
        w1_sb = [w.rearrange("p (k f) -> p k f", k=DK) for w in w1_sb]
        w2_sb = [w.rearrange("p (k d) -> p k d", k=FK) for w in w2_sb]
        o = DK * F + FK * D
        b2_sb = [res[:, o + b * D:o + (b + 1) * D] for b in range(2)]
        o += 2 * D
        normed = [res[:, o + b * D:o + (b + 1) * D] for b in range(2)]
        o += 2 * D
        mask = [res[:, o + b * D:o + (b + 1) * D].bitcast(I32) for b in range(3)]
        o += 3 * D
        big, neg, zero = (res[:, o + b * D:o + (b + 1) * D] for b in range(3))
        o += 3 * D
        final = [res[:, o + b * D:o + (b + 1) * D] for b in range(2)]
        o += 2 * D
        slot_rows = [stage[:, b, :, :] for b in range(2)]

        pT = [ps(f"pT{b}", [P, 512]) for b in range(2)]
        pR = [ps(f"pR{b}", [P, 512]) for b in range(2)]
        pS = ps("pS", [P, 512])
        pG = ps("pG", [P, 512])
        pH = [ps(f"pH{b}", [P, 512]) for b in range(2)]

        x_in, consts_in, b1_in, dst_in, table_filled = (sem(s) for s in (
            "x_in", "consts_in", "b1_in", "dst_in", "table_filled"))
        pe_passed, dve_passed = sem("pe_passed"), sem("dve_passed")
        pool_consts = sem("pool_consts")
        pool_step = sem("pool_step")
        dve_step = sem("dve_step")
        xn_ready, xn_stored, stage_free, xs_ready, transposed0, xT_sb0, r_ps0, r_sb0, r_biased, b1T_ps, b1T_sb = (
            sem(s) for s in ("xn_ready", "xn_stored", "stage_free", "xs_ready", "transposed0", "xT_sb0", "r_ps0",
                             "r_sb0", "r_biased", "b1T_ps", "b1T_sb"))
        ranges_found, ranges_stored, ranges_in, fill_ready = (sem(s) for s in (
            "ranges_found", "ranges_stored", "ranges_in", "fill_ready"))
        index_in = [sem(f"index_in{s}") for s in range(SLOTS)]
        gathered = [sem(f"gathered{s}") for s in range(SLOTS)]
        slot_claimed, block_done, onehot_ready, rel_ready, sum_ps, sum_added = (sem(s) for s in (
            "slot_claimed", "block_done", "onehot_ready", "rel_ready", "sum_ps", "sum_added"))
        sums_ready, mean_ready, xT_ps2, xT_sb2, f_ps, f_sb, g_sb, x1_ready, x1_stored, x2_ready, gT_ps, gT_sb, gate_ps, gate_sb = (
            sem(s) for s in ("sums_ready", "mean_ready", "xT_ps2", "xT_sb2", "f_ps", "f_sb", "g_sb", "x1_ready", "x1_stored",
                             "x2_ready", "gT_ps", "gT_sb", "gate_ps", "gate_sb"))
        shifted, exped, picked_ready, counts_ps, slots_ready, dispatched = (sem(s) for s in (
            "shifted", "exped", "picked_ready", "counts_ps", "slots_ready", "dispatched"))
        weights_in = [sem(f"weights_in{b}") for b in range(2)]
        rows_in = [sem(f"rows_in{b}") for b in range(2)]
        in_normed, inT_ps, inT_sb, hid_ps, hid_sb, y_ps, y_taken, y_ready = (sem(s) for s in (
            "in_normed", "inT_ps", "inT_sb", "hid_ps", "hid_sb", "y_ps", "y_taken", "y_ready"))
        b1_set = sem("b1_set")
        scattered = [sem(f"scattered{b}") for b in range(2)]
        scatter_claimed, final_free, tail_cleared = (sem(s) for s in ("scatter_claimed", "final_free", "tail_cleared"))

        CONSTS = 7 * 16
        block = ctx.enter_context(nc.Block())

        @block.sync
        def _(sp):
            for c in range(6):
                sp.dma_start(rows[:, c * G:(c + 1) * G, 0:D],
                             x[c * G * P:(c + 1) * G * P, :].rearrange("(t p) d -> p t d", p=P)).then_inc(x_in, 16)
            sp.wait_ge(tail_cleared, 1)
            sp.dma_start(rows[0:LAST, NT - 1, 0:D], x[(NT - 1) * P:N, :]).then_inc(x_in, 16)
            sp.dma_start(dst_all, dst[0:BLOCKS * BLOCK].rearrange("(p b e) -> p b e", p=BP, b=BPN)).then_inc(dst_in, 16)
            sp.dma_start(rest_dst[:, :], dst[BLOCKS * BLOCK:E].rearrange("(a e) -> a e", a=1)).then_inc(dst_in, 16)
            sp.wait_ge(ranges_found, 2)
            sp.dma_start(range_table[0:2 * BLOCKS].rearrange("(p b c) -> p b c", p=BP, b=BPN),
                         block_range[:, :, :]).then_inc(ranges_stored, 16)
            sp.dma_start(range_table[2 * BLOCKS:2 * BLOCKS + 2].rearrange("(a c) -> a c", a=1),
                         rest_range[:, :]).then_inc(ranges_stored, 16)
            sp.wait_ge(ranges_stored, 32)
            sp.dma_start(range_row[:, :], range_table.rearrange("(a c) -> a c", a=1)).then_inc(ranges_in, 16)

            def store_xn(t0, nt, b, g):
                sp.wait_ge(xn_ready, t0 + nt)
                if nt == G:
                    sp.dma_start(xn_table[bass.ds(t0 * P, G * P), :].rearrange("(t p) d -> p t d", p=P),
                                 stage[:, b, :, 0:D]).then_inc(xn_stored, 16)
                else:
                    sp.dma_start(xn_table[t0 * P:N, :], stage[0:LAST, b, 0, 0:D]).then_inc(xn_stored, 16)
                sp.wait_ge(xn_stored, g * 16 + 16)
                sp.wait_ge(transposed0, t0 + nt)
                sp.sem_inc(stage_free, 1)

            groups(sp, store_xn)

            def load_indices(s, first, rows_, cols, turn):
                sp.wait_ge(block_done, turn)
                for at, of in ((src_ix, src), (dst_ix, dst)):
                    sp.dma_start(at[0:rows_, s, 0:cols],
                                 of[bass.ds(first, rows_ * cols)].rearrange("(p k) -> p k", k=cols)
                                 ).then_inc(index_in[s], 16)

            with sp.Fori(0, RUNS) as i:
                for s in range(SLOTS):
                    load_indices(s, i * (SLOTS * BLOCK) + s * BLOCK, P, COLS, i * SLOTS + s + 1)
            load_indices(0, BLOCKS * BLOCK, REST_ROWS, REST_COLS, BLOCKS + 1)

            def store_x1(t0, nt, b, g):
                sp.wait_ge(x1_ready, g + 1)
                if nt == G:
                    sp.dma_start(out[bass.ds(t0 * P, G * P), :].rearrange("(t p) d -> p t d", p=P),
                                 rows[:, bass.ds(t0, G), 0:D]).then_inc(x1_stored, 16)
                else:
                    sp.dma_start(out[t0 * P:N, :], rows[0:LAST, t0, 0:D]).then_inc(x1_stored, 16)

            groups(sp, store_x1)

            def load_weights(e, b):
                sp.dma_start(w1_sb[b], w1[e, :, :].rearrange("(k p) f -> p k f", p=P)).then_inc(weights_in[b], 16)
                sp.dma_start(w2_sb[b], w2[e, :, :].rearrange("(k p) d -> p k d", p=P)).then_inc(weights_in[b], 16)
                sp.dma_start(b2_sb[b], b2[e, :].rearrange("(a d) -> a d", a=1).to_broadcast([P, D])
                             ).then_inc(weights_in[b], 16)

            def load_rows(e, b):
                first = e * CAP
                full = (TOK_TILES - 1) * P
                sp.dma_start(slot_rows[b][:, 0:TOK_TILES - 1, :],
                             slot_table[bass.ds(first, full), :].rearrange("(t p) d -> p t d", p=P)
                             ).then_inc(rows_in[b], 16)
                sp.dma_start(slot_rows[b][0:TOK_LAST, TOK_TILES - 1, :],
                             slot_table[bass.ds(first + full, TOK_LAST), :]).then_inc(rows_in[b], 16)

            sp.wait_ge(slots_ready, 2)
            for b in range(2):
                load_weights(b, b)
            sp.wait_ge(dispatched, 16 * NT)
            for b in range(2):
                load_rows(b, b)
            with sp.Fori(1, X // 2) as i:
                for b in range(2):
                    sp.wait_ge(final_free, i * (2 * TOK_TILES) + (b - 1) * TOK_TILES + 2)
                    load_weights(i * 2 + b, b)
                    load_rows(i * 2 + b, b)

            sp.wait_ge(x1_stored, 16 * (2 * PAIRS + 1))
            for b in range(2):
                sp.wait_ge(scattered[b], 16 * X * TOK_TILES // 2)

        @block.gpsimd
        def _(pool):
            own = Own(pool, pool_step)
            nc.gpsimd.memset(rows[:, NT - 1, :], 0.0).then_inc(tail_cleared, 1)
            own(nc.gpsimd.memset(ones[:, :], 1.0))
            own(nc.gpsimd.memset(ident[:, :], 0.0))
            own.wait()
            nc.gpsimd.affine_select(out=ident[:, :], in_=ident[:, :], compare_op=ALU.not_equal, fill=1.0, base=0,
                                    pattern=[[-1, P]], channel_multiplier=1).then_inc(pool_consts, 1)
            nc.gpsimd.affine_select(out=upper[:, :], in_=ones[:, :], compare_op=ALU.is_ge, fill=0.0, base=0,
                                    pattern=[[1, P]], channel_multiplier=-1).then_inc(pool_consts, 1)
            nc.gpsimd.iota(lane[:, :], [[1, P]], base=0, channel_multiplier=0,
                           allow_small_or_imprecise_dtypes=True).then_inc(pool_consts, 1)
            nc.gpsimd.iota(tile_base[:, :], [[P, NT]], base=0, channel_multiplier=0,
                           allow_small_or_imprecise_dtypes=True).then_inc(pool_consts, 1)
            nc.gpsimd.iota(token_ix[:, :], [[P, NT]], base=0, channel_multiplier=1).then_inc(pool_consts, 1)
            own(nc.gpsimd.memset(fill[:, :], 0.0))
            own.wait()
            nc.gpsimd.memset(fill[:, TOKEN:TOKEN + 1].bitcast(I32), NOBODY).then_inc(fill_ready, 1)
            for s in range(SLOTS):
                nc.gpsimd.memset(gath[:, s, :, D:CNT], 1.0).then_inc(fill_ready, 1)

            def biases(t0, nt, b, g):
                pool.wait_ge(xs_ready, g + 1)
                v = rows[:, bass.ds(t0, nt), 0:D]
                nc.gpsimd.tensor_tensor(v, v, beta_sb[:, :].unsqueeze(1).to_broadcast([P, nt, D]),
                                        ALU.add).then_inc(r_biased, 1)
                pool.wait_ge(r_sb0, t0 + nt + 2)
                v = resid[:, bass.ds(t0, nt), :]
                nc.gpsimd.tensor_tensor(v, v, b_l_sb[:, :].unsqueeze(1).to_broadcast([P, nt, D]),
                                        ALU.add).then_inc(r_biased, 1)

            pool.wait_ge(consts_in, CONSTS)
            groups(pool, biases)

            def gather_block(s, rows_, cols, turn):
                pool.wait_ge(index_in[s], turn)
                pool.sem_inc(slot_claimed, 1)
                for k in range(cols):
                    nc.gpsimd.indirect_dma_start(
                        gath[0:rows_, s, k, 0:D], None, xn_table,
                        bass.IndirectOffsetOnAxis(ap=src_ix[0:rows_, s, k:k + 1], axis=0)).then_inc(gathered[s], 16)

            pool.wait_ge(stage_free, 2 + 2 * PAIRS + 1)
            with pool.Fori(0, RUNS) as i:
                for s in range(SLOTS):
                    gather_block(s, P, COLS, i * 32 + 32)
            gather_block(0, REST_ROWS, REST_COLS, RUNS * 32 + 32)

            pool.wait_ge(slots_ready, 2)
            pool.wait_ge(table_filled, 32)
            for t in range(NT):
                n = P if t < NT - 1 else LAST
                nc.gpsimd.indirect_dma_start(
                    slot_table, bass.IndirectOffsetOnAxis(ap=slot_ix[0:n, t:t + 1], axis=0), rows[0:n, t, :], None,
                    bounds_check=X * CAP - 1, oob_is_err=False).then_inc(dispatched, 16)

            pool.wait_ge(x1_stored, 16 * (2 * PAIRS + 1))
            with pool.Fori(0, X // 2) as i:
                for b in range(2):
                    for m in range(TOK_TILES):
                        n = P if m < TOK_TILES - 1 else TOK_LAST
                        c = m % 2
                        k = b * TOK_TILES + m
                        pool.wait_ge(y_ready, i * (2 * TOK_TILES) + k + 1)
                        pool.sem_inc(scatter_claimed, 1)
                        nc.gpsimd.indirect_dma_start(
                            out, bass.IndirectOffsetOnAxis(ap=slot_rows[b][0:n, m, TOKEN:TOKEN + 1].bitcast(I32), axis=0),
                            final[c][0:n, :], None, bounds_check=N - 1, oob_is_err=False).then_inc(scattered[c], 16)
                        pool.wait_ge(scattered[c], i * (16 * TOK_TILES) + 16 * (k // 2 + 1))
                        pool.sem_inc(final_free, 1)

        @block.tensor
        def _(pe):
            def transpose_rows(at, of, n, ready, at_rows=P):
                for k in range(DK):
                    last = nc.tensor.transpose(at[:, k * P:k * P + n], of[0:n, k * P:(k + 1) * P], ident[0:n, 0:n])
                return last.then_inc(ready, 1)

            def linear(at, of, w, ready):
                for k in range(DK):
                    last = nc.tensor.matmul(at[:, 0:D], of[:, k * P:(k + 1) * P], w[:, k, :],
                                            start=(k == 0), stop=(k == DK - 1))
                return last.then_inc(ready, 1)

            pe.wait_ge(pool_consts, 5)
            pe.wait_ge(b1_in, 16)
            nc.tensor.transpose(pG[:, 0:X * FK], b1_rows[:, :], ident[0:X * FK, 0:X * FK]).then_inc(b1T_ps, 1)
            pe.wait_ge(consts_in, CONSTS)

            def transposes0(t0, j, b):
                pe.wait_ge(xn_ready, t0 + j + 1)
                pe.wait_ge(xT_sb0, t0 + j + 1)
                transpose_rows(pT[j % 2], stage[:, b, j, 0:D], P, transposed0)

            def linear0(t0, j):
                pe.wait_ge(xT_sb0, t0 + j + 3)
                pe.wait_ge(r_sb0, t0 + j + 1)
                linear(pR[j % 2], xT[:, j % 2, :], w_r_sb, r_ps0)

            def group0(t0, nt, b, g):
                for j in range(nt + 1):
                    if j < nt:
                        transposes0(t0, j, b)
                    if j > 0:
                        linear0(t0, j - 1)

            groups(pe, group0)

            item = pe.alloc_register("pe_item")
            pe.reg_mov(item, 0)
            pe.wait_ge(ranges_in, 16)

            def sum_block(s, number, rows_, cols, turn):
                lo = pe.value_load(range_row[0:1, bass.ds(number * 2, 1)], min_val=0, max_val=NT - 1)
                hi = pe.value_load(range_row[0:1, bass.ds(number * 2 + 1, 1)], min_val=1, max_val=NT)
                pe.wait_ge(gathered[s], turn)
                pe.sem_inc(pe_passed, 1)
                with pe.Fori(lo, hi):
                    pe.reg_add(item, item, 1)
                    pe.wait_ge(onehot_ready, pe.snap(item))
                    for k in range(cols):
                        last = nc.tensor.matmul(pS[:, 0:CNT], onehot[0:rows_, k, :], gath[0:rows_, s, k, :],
                                                start=(k == 0), stop=(k == cols - 1))
                    last.then_inc(sum_ps, 1)

            with pe.Fori(0, RUNS) as i:
                for s in range(SLOTS):
                    sum_block(s, i * SLOTS + s, P, COLS, i * (16 * COLS) + 16 * COLS)
            sum_block(0, BLOCKS, REST_ROWS, REST_COLS, RUNS * 16 * COLS + 16 * REST_COLS)

            def group2(t0, nt, b, g):
                for j in range(nt + 1):
                    if j < nt:
                        pe.wait_ge(xT_sb2, t0 + j + 1)
                        if j < 2:
                            pe.wait_ge(gT_sb, t0 + 2)
                        pe.wait_ge(mean_ready, t0 + j + 1)
                        transpose_rows(pT[j % 2], stage[:, b, j, 0:D], P, xT_ps2)
                    if j > 0:
                        pe.wait_ge(xT_sb2, t0 + j + 2)
                        pe.wait_ge(f_sb, t0 + j)
                        linear(pR[(j - 1) % 2], xT[:, (j - 1) % 2, :], w_l_sb, f_ps)
                for j in range(nt + 1):
                    if j < nt:
                        pe.wait_ge(x2_ready, t0 + j + 1)
                        pe.wait_ge(gT_sb, t0 + j + 1)
                        transpose_rows(pT[j % 2], stage[:, b, j, 0:D], P, gT_ps)
                    if j > 0:
                        pe.wait_ge(gT_sb, t0 + j + 2)
                        if j == 1:
                            pe.wait_ge(gate_sb, g + 1)
                        for k in range(DK):
                            last = nc.tensor.matmul(pG[:, (j - 1) * X:j * X], xT[:, (j - 1) % 2, k * P:(k + 1) * P],
                                                    gate_w_sb[:, k, :], start=(k == 0), stop=(k == DK - 1))
                        last.then_inc(gate_ps, 1)

            groups(pe, group2)

            pe.wait_ge(picked_ready, 1)
            flat = picked.rearrange("p t e -> p (t e)")
            nc.tensor.matmul(pR[0][:, 0:n8], upper[:, :], flat, start=True, stop=True).then_inc(counts_ps, 1)
            nc.tensor.matmul(pR[1][:, 0:n8], ones[:, :], flat, start=True, stop=True).then_inc(counts_ps, 1)

            with pe.Fori(0, X // 2) as i:
                for b in range(2):
                    tok0 = i * (2 * TOK_TILES) + b * TOK_TILES
                    for m in range(TOK_TILES):
                        n = P if m < TOK_TILES - 1 else TOK_LAST
                        pe.wait_ge(in_normed, tok0 + m + 1)
                        pe.wait_ge(inT_sb, tok0 + m + 1)
                        transpose_rows(pT[m % 2], normed[m % 2], n, inT_ps)
                    pe.wait_ge(inT_sb, tok0 + TOK_TILES + 2)
                    pe.wait_ge(weights_in[b], i * 48 + 48)
                    for h, (c0, cn) in enumerate(HALVES):
                        for f in range(FK):
                            u = h * FK + f
                            pe.wait_ge(hid_sb, i * (4 * FK) + b * 2 * FK + u + 1)
                            for k in range(DK):
                                last = nc.tensor.matmul(pH[u % 2][:, 0:cn], w1_sb[b][:, k, f * P:(f + 1) * P],
                                                        inT[:, k, c0:c0 + cn], start=(k == 0), stop=(k == DK - 1))
                            last.then_inc(hid_ps, 1)
                    for m in range(TOK_TILES):
                        n = P if m < TOK_TILES - 1 else TOK_LAST
                        if m == 0:
                            pe.wait_ge(hid_sb, i * (4 * FK) + b * 2 * FK + FK + 2)
                        if m * P + n > HALVES[0][1] and m * P < HALVES[0][1] + P:
                            pe.wait_ge(hid_sb, i * (4 * FK) + b * 2 * FK + 2 * FK + 2)
                        pe.wait_ge(y_taken, tok0 + m + 1)
                        for f in range(FK):
                            last = nc.tensor.matmul(pR[m % 2][0:n, 0:D], hidden[:, f, m * P:m * P + n],
                                                    w2_sb[b][:, f, :], start=(f == 0), stop=(f == FK - 1))
                        last.then_inc(y_ps, 1)

        @block.scalar
        def _(act):
            for at, of in ((w_l_sb, w_l), (w_r_sb, w_r)):
                act.dma_start(at[:, :, :], of.rearrange("(k p) n -> p k n", p=P)).then_inc(consts_in, 16)
            for at, of in ((b_l_sb, b_l), (gamma_sb, gamma), (beta_sb, beta), (gate_b_sb, gate_b)):
                act.dma_start(at[:, :], of.rearrange("(a d) -> a d", a=1).to_broadcast([P, at.shape[1]])
                              ).then_inc(consts_in, 16)
            act.dma_start(gate_w_sb[:, :, :], gate_w.rearrange("(k p) n -> p k n", p=P)).then_inc(consts_in, 16)
            act.dma_start(b1_rows[:, :], b1.rearrange("e (k p) -> (e k) p", p=P)).then_inc(b1_in, 16)
            act.wait_ge(fill_ready, 1)
            full = X * CAP // P
            act.dma_start(slot_table[0:full * P, :].rearrange("(p t) d -> p t d", p=P),
                          fill[:, :].unsqueeze(1).to_broadcast([P, full, ROW])).then_inc(table_filled, 16)
            act.dma_start(slot_table[full * P:X * CAP, :], fill[0:X * CAP - full * P, :]).then_inc(table_filled, 16)
            for free, n in ((xT_sb0, 2), (r_sb0, 2), (xT_sb2, 2), (gT_sb, 2), (gate_sb, 1), (inT_sb, 2), (hid_sb, 2)):
                act.sem_inc(free, n)
            act.wait_ge(b1T_ps, 1)
            nc.scalar.copy(b1_sb[:, :], pG[:, 0:X * FK]).then_inc(b1T_sb, 1)

            def group0(t0, nt, b, g):
                for j in range(nt + 1):
                    if j < nt:
                        act.wait_ge(transposed0, t0 + j + 1)
                        act.wait_ge(r_ps0, t0 + j + 1)
                        nc.scalar.copy(xT[:, j % 2, :], pT[j % 2][:, 0:D]).then_inc(xT_sb0, 1)
                    if j > 0:
                        act.wait_ge(r_ps0, t0 + j + 2)
                        nc.scalar.copy(resid[:, bass.ds(t0 + j - 1, 1), :].rearrange("p a d -> p (a d)"),
                                       pR[(j - 1) % 2][:, 0:D]).then_inc(r_sb0, 1)

            act.sem_inc(r_ps0, 2)
            groups(act, group0)

            act.sem_inc(f_ps, 2)
            act.sem_inc(gate_ps, 2)
            act.wait_ge(sums_ready, 1)

            def group2(t0, nt, b, g):
                def mean(j):
                    nc.scalar.activation(stage[:, b, j, 0:D],
                                         sums[:, bass.ds(t0 + j, 1), 0:D].rearrange("p a d -> p (a d)"), ACT.Copy,
                                         scale=rdeg[:, bass.ds(t0 + j, 1)]).then_inc(mean_ready, 1)

                mean(0)
                for j in range(nt + 2):
                    if j + 1 < nt:
                        mean(j + 1)
                    if j < nt:
                        act.wait_ge(xT_ps2, t0 + j + 1)
                        act.wait_ge(f_ps, t0 + j + 1)
                        if j < 2:
                            act.wait_ge(gate_ps, t0 + 2)
                        nc.scalar.copy(xT[:, j % 2, :], pT[j % 2][:, 0:D]).then_inc(xT_sb2, 1)
                    if j > 1:
                        act.wait_ge(f_sb, t0 + j + 1)
                        v = resid[:, bass.ds(t0 + j - 2, 1), :].rearrange("p a d -> p (a d)")
                        nc.scalar.activation(v, v, ACT.Gelu).then_inc(g_sb, 1)
                for j in range(nt):
                    act.wait_ge(gT_ps, t0 + j + 1)
                    act.wait_ge(gate_ps, t0 + j + 1)
                    nc.scalar.copy(xT[:, j % 2, :], pT[j % 2][:, 0:D]).then_inc(gT_sb, 1)
                act.wait_ge(gate_ps, t0 + nt + 2)
                nc.scalar.copy(logits[:, bass.ds(t0, nt), :],
                               pG[:, 0:nt * X].rearrange("p (t e) -> p t e", e=X)).then_inc(gate_sb, 1)

            groups(act, group2)

            act.wait_ge(shifted, 1)
            nc.scalar.activation(before[:, :, :], before[:, :, :], ACT.Exp).then_inc(exped, 1)

            act.wait_ge(b1T_sb, 1)
            act.wait_ge(counts_ps, 2)
            act.sem_inc(hid_ps, 2)
            with act.Fori(0, X // 2) as i:
                for b in range(2):
                    tok0 = i * (2 * TOK_TILES) + b * TOK_TILES
                    for m in range(TOK_TILES):
                        n = P if m < TOK_TILES - 1 else TOK_LAST
                        act.wait_ge(inT_ps, tok0 + m + 1)
                        if m == 0:
                            act.wait_ge(hid_ps, i * (4 * FK) + b * 2 * FK + 2)
                        nc.scalar.copy(inT[:, :, m * P:m * P + n],
                                       pT[m % 2][:, 0:D].rearrange("p (k c) -> p k c", k=DK)[:, :, 0:n]
                                       ).then_inc(inT_sb, 1)
                    nc.scalar.copy(b1_now[:, b, :], b1_sb[:, bass.ds(i * (2 * FK) + b * FK, FK)]).then_inc(b1_set, 1)
                    act.wait_ge(b1_set, i * 2 + b + 1)
                    for h, (c0, cn) in enumerate(HALVES):
                        for f in range(FK):
                            u = h * FK + f
                            act.wait_ge(hid_ps, i * (4 * FK) + b * 2 * FK + u + 3)
                            if u == 0:
                                act.wait_ge(y_ps, tok0 + 1)
                            nc.scalar.activation(hidden[:, f, c0:c0 + cn], pH[u % 2][:, 0:cn], ACT.Relu,
                                                 bias=b1_now[:, b, f:f + 1]).then_inc(hid_sb, 1)

        @block.vector
        def _(dve):
            own = Own(dve, dve_step)
            for free, n in ((stage_free, 2), (block_done, SLOTS), (sum_added, 1), (f_sb, 2), (y_taken, 2), (y_ps, 1),
                            (final_free, 2)):
                dve.sem_inc(free, n)

            def rsqrt(nt):
                v, y, w = var[:, 0:nt], rs[:, 0:nt], nt_[:, 0:nt]
                own(nc.vector.tensor_scalar(v, mv[:, 0:nt, 1], EPS, None, ALU.add))
                own.wait()
                own(nc.vector.tensor_scalar(w.bitcast(I32), v.bitcast(I32), 1, None, ALU.logical_shift_right))
                own.wait()
                own(nc.vector.tensor_scalar(y.bitcast(I32), w.bitcast(I32), -1.0, float(RSQRT_GUESS), ALU.mult, ALU.add))
                for _ in range(4):
                    own.wait()
                    own(nc.vector.scalar_tensor_tensor(w, y, -0.5, y, ALU.mult, ALU.mult))
                    own.wait()
                    own(nc.vector.tensor_tensor(w, w, v, ALU.mult))
                    own.wait()
                    own(nc.vector.scalar_tensor_tensor(y, w, 1.5, y, ALU.add, ALU.mult))
                own.wait()
                own(nc.vector.scalar_tensor_tensor(nmr[:, 0:nt], mv[:, 0:nt, 0], -1.0, y, ALU.mult, ALU.mult))
                own.wait()

            RSQRT_STEPS = 3 + 4 * 3 + 1

            def moments(views):
                dve.sem_inc(dve_passed, 1)
                for j, v in enumerate(views):
                    own(nc.vector.bn_stats(bn[:, j, :], v))
                own.wait_apart(dve_passed)
                for j in range(len(views)):
                    own(nc.vector.bn_aggr(mv[:, j, :], bn[:, j, :]))
                own.wait()

            def tile_rows(t):
                return rows[:, bass.ds(t, 1), 0:D].rearrange("p a d -> p (a d)")

            def tile_res(t):
                return resid[:, bass.ds(t, 1), :].rearrange("p a d -> p (a d)")

            dve.wait_ge(x_in, 16 * 7)
            dve.wait_ge(dst_in, 32)
            for at, of in ((block_range[:, :, :], dst_all), (rest_range[:, :].unsqueeze(1), rest_dst[:, :].unsqueeze(1))):
                own(nc.vector.tensor_reduce(at[:, :, 0], of, AX.X, ALU.min))
                own(nc.vector.tensor_reduce(at[:, :, 1], of, AX.X, ALU.max))
                own.wait()
                own(nc.vector.tensor_scalar(at, at, 7, None, ALU.logical_shift_right))
                own.wait()
                nc.vector.tensor_scalar(at[:, :, 1], at[:, :, 1], 1.0, None, ALU.add).then_inc(ranges_found, 1)

            def group0(t0, nt, b, g):
                moments([tile_rows(t0 + j) for j in range(nt)])
                rsqrt(nt)
                dve.wait_ge(stage_free, g + 1)
                for j in range(nt):
                    nc.vector.tensor_scalar(stage[:, b, j, 0:D], tile_rows(t0 + j), rs[:, j:j + 1], nmr[:, j:j + 1],
                                            ALU.mult, ALU.add).then_inc(xn_ready, 1)
                dve.wait_ge(xn_ready, t0 + nt)
                v = rows[:, bass.ds(t0, nt), 0:D]
                nc.vector.tensor_tensor(v, v, stage[:, b, 0:nt, 0:D], ALU.add).then_inc(xs_ready, 1)

            groups(dve, group0, own, 2 * (2 * G + RSQRT_STEPS))

            dve.wait_ge(r_biased, 2 * (2 * PAIRS + 1))
            own(nc.vector.memset(sums_flat[:, :], 0.0))
            own.wait()
            item = dve.alloc_register("dve_item")
            dve.reg_mov(item, 0)
            dve.wait_ge(ranges_in, 16)
            dve.wait_ge(pool_consts, 5)
            dve.wait_ge(fill_ready, 1 + SLOTS)

            def sum_block(s, number, rows_, cols, turn):
                lo = dve.value_load(range_row[0:1, bass.ds(number * 2, 1)], min_val=0, max_val=NT - 1)
                hi = dve.value_load(range_row[0:1, bass.ds(number * 2 + 1, 1)], min_val=1, max_val=NT)
                dve.wait_ge(index_in[s], turn)
                dve.sem_inc(dve_passed, 1)
                with dve.Fori(lo, hi) as t:
                    dve.reg_add(item, item, 1)
                    n = dve.snap(item)
                    nc.vector.tensor_scalar(dst_rel[0:rows_, 0:cols], dst_ix[0:rows_, s, 0:cols],
                                            tile_base[0:rows_, bass.ds(t, 1)], None, ALU.subtract).then_inc(rel_ready, 1)
                    dve.wait_ge(rel_ready, n)
                    nc.vector.tensor_tensor(onehot[0:rows_, 0:cols, :],
                                            lane[0:rows_, :].unsqueeze(1).to_broadcast([rows_, cols, P]),
                                            dst_rel[0:rows_, 0:cols].unsqueeze(2).to_broadcast([rows_, cols, P]),
                                            ALU.is_equal).then_inc(onehot_ready, 1)
                    dve.wait_ge(sum_added, n)
                    dve.wait_ge(sum_ps, n)
                    v = sums[:, bass.ds(t, 1), :].rearrange("p a d -> p (a d)")
                    nc.vector.tensor_tensor(v, v, pS[:, 0:CNT], ALU.add).then_inc(sum_added, 1)
                nc.vector.engine_nop().then_inc(block_done, 1)

            with dve.Fori(0, RUNS) as i:
                for s in range(SLOTS):
                    sum_block(s, i * SLOTS + s, P, COLS, i * 32 + 32)
            sum_block(0, BLOCKS, REST_ROWS, REST_COLS, RUNS * 32 + 32)
            dve.wait_ge(block_done, SLOTS + BLOCKS + 1)

            own(nc.vector.tensor_scalar(rdeg[:, :], sums[:, :, D], 1.0, None, ALU.max))
            own.wait()
            nc.vector.reciprocal(rdeg[:, :], rdeg[:, :]).then_inc(sums_ready, 1)
            dve.wait_ge(sums_ready, 1)

            def group2(t0, nt, b, g):
                for j in range(nt):
                    dve.wait_ge(f_ps, t0 + j + 3)
                    nc.vector.tensor_tensor(tile_res(t0 + j), pR[j % 2][:, 0:D], tile_res(t0 + j),
                                            ALU.add).then_inc(f_sb, 1)
                dve.wait_ge(g_sb, t0 + nt)
                moments([tile_res(t0 + j) for j in range(nt)])
                rsqrt(nt)
                for j in range(nt):
                    own(nc.vector.scalar_tensor_tensor(stage[:, b, j, 0:D], tile_res(t0 + j), mv[:, j, 0:1],
                                                       gamma_sb[:, :], ALU.subtract, ALU.mult))
                own.wait()
                for j in range(nt):
                    own(nc.vector.scalar_tensor_tensor(tile_rows(t0 + j), stage[:, b, j, 0:D], rs[:, j:j + 1],
                                                       tile_rows(t0 + j), ALU.mult, ALU.add))
                own.wait()
                moments([tile_rows(t0 + j) for j in range(nt)])
                rsqrt(nt)
                own(nc.vector.tensor_copy(rows[:, bass.ds(t0, nt), RSTD], rs[:, 0:nt]))
                own(nc.vector.tensor_copy(rows[:, bass.ds(t0, nt), NMR], nmr[:, 0:nt]))
                for j in range(nt):
                    nc.vector.tensor_scalar(stage[:, b, j, 0:D], tile_rows(t0 + j), rs[:, j:j + 1], nmr[:, j:j + 1],
                                            ALU.mult, ALU.add).then_inc(x2_ready, 1)
                nc.vector.engine_nop().then_inc(x1_ready, 1)

            groups(dve, group2, own, 2 * (2 * (2 * G + RSQRT_STEPS) + 2 * G + 2))

            dve.wait_ge(gate_sb, 1 + 2 * PAIRS + 1)
            def wide(v):
                return v.unsqueeze(2).to_broadcast([P, NT, X])

            largest, best, total, where, over, keep = (small[:, k, :] for k in range(6))
            gate_b_wide = gate_b_sb[:, :].unsqueeze(1).to_broadcast([P, NT, X])
            own(nc.vector.tensor_tensor(logits[:, :, :], logits[:, :, :], gate_b_wide, ALU.add))
            own(nc.vector.tensor_scalar(descend, lane[:, 0:X].unsqueeze(1).to_broadcast([P, NT, X]), -1.0, float(X),
                                        ALU.mult, ALU.add))
            own.wait()
            own(nc.vector.tensor_reduce(largest, logits[:, :, :], AX.X, ALU.max))
            own.wait()
            nc.vector.tensor_tensor(before, logits[:, :, :], wide(largest), ALU.subtract).then_inc(shifted, 1)
            own(nc.vector.tensor_tensor(score, logits[:, :, :], wide(largest), ALU.is_equal))
            own.wait()
            own(nc.vector.tensor_tensor(score, score, descend, ALU.mult))
            own.wait()
            own(nc.vector.tensor_reduce(best, score, AX.X, ALU.max))
            own.wait()
            nc.vector.tensor_tensor(picked, descend, wide(best), ALU.is_equal).then_inc(picked_ready, 1)
            dve.wait_ge(exped, 1)
            own(nc.vector.tensor_reduce(total, before, AX.X, ALU.add))
            own.wait()
            own(nc.vector.reciprocal(rows[:, :, PROB:PROB + 1], total.unsqueeze(2)))
            own(nc.vector.tensor_copy(rows[:, :, TOKEN:TOKEN + 1].bitcast(I32), token_ix[:, :].unsqueeze(2)))
            own(nc.vector.memset(notfirst[:, :, :], 1.0))
            own.wait()
            own(nc.vector.memset(notfirst[:, :, 0:1], 0.0))
            dve.wait_ge(counts_ps, 2)
            own(nc.vector.tensor_copy(score.rearrange("p t e -> p (t e)").rearrange("p (e t) -> p e t", e=X),
                                      pR[1][:, 0:n8].rearrange("p (t e) -> p e t", e=X)))
            own.wait()
            own(nc.vector.tensor_tensor_scan(descend.rearrange("p t e -> p (t e)"),
                                             notfirst[:, :, :].rearrange("p e t -> p (e t)"),
                                             score.rearrange("p t e -> p (t e)"), 0.0, ALU.mult, ALU.add))
            own.wait()
            own(nc.vector.tensor_tensor(descend.rearrange("p t e -> p (t e)"), descend.rearrange("p t e -> p (t e)"),
                                        score.rearrange("p t e -> p (t e)"), ALU.subtract))
            own.wait()
            own(nc.vector.tensor_tensor(place, descend.rearrange("p t e -> p (t e)").rearrange("p (e t) -> p t e", e=X),
                                        pR[0][:, 0:n8].rearrange("p (t e) -> p t e", e=X), ALU.add))
            own.wait()
            own(nc.vector.tensor_tensor(place, place, picked, ALU.mult))
            own.wait()
            own(nc.vector.tensor_reduce(where, place, AX.X, ALU.add))
            own.wait()
            own(nc.vector.tensor_scalar(over, where, float(CAP), float(NOBODY), ALU.is_gt, ALU.mult))
            own(nc.vector.tensor_scalar(keep, best, -float(CAP), float(X * CAP - 1), ALU.mult, ALU.add))
            own.wait()
            own(nc.vector.tensor_tensor(keep, keep, where, ALU.add))
            own.wait()
            own(nc.vector.tensor_tensor(keep, keep, over, ALU.add))
            own.wait()
            nc.vector.tensor_copy(slot_ix[:, :], keep).then_inc(slots_ready, 1)
            own(nc.vector.memset(big, 1e4))
            own(nc.vector.memset(neg, -1e4))
            own(nc.vector.memset(zero, 0.0))
            own.wait()
            nc.vector.engine_nop().then_inc(slots_ready, 1)

            HUGE = 3.4028234e38

            def norm_rows(i, b):
                tok0 = i * (2 * TOK_TILES) + b * TOK_TILES
                dve.wait_ge(rows_in[b], i * 32 + 32)
                for m in range(TOK_TILES):
                    n = P if m < TOK_TILES - 1 else TOK_LAST
                    r = slot_rows[b]
                    dve.wait_ge(inT_sb, tok0 + m + 1)
                    nc.vector.tensor_scalar(normed[m % 2][0:n, :], r[0:n, m, 0:D], r[0:n, m, RSTD:RSTD + 1],
                                            r[0:n, m, NMR:NMR + 1], ALU.mult, ALU.add).then_inc(in_normed, 1)

            with dve.Fori(0, X // 2) as i:
                own.enter(i, 2 * TOK_TILES * 7)
                for b in range(2):
                    norm_rows(i, b)
                    tok0 = i * (2 * TOK_TILES) + b * TOK_TILES
                    dve.wait_ge(weights_in[b], i * 48 + 48)
                    for m in range(TOK_TILES):
                        n = P if m < TOK_TILES - 1 else TOK_LAST
                        r, y = slot_rows[b], final[m % 2][0:n, :]
                        dve.wait_ge(y_ps, tok0 + m + 2)
                        dve.wait_ge(final_free, tok0 + m + 1)
                        nc.vector.tensor_tensor(y, pR[m % 2][0:n, 0:D], b2_sb[b][0:n, :], ALU.add).then_inc(y_taken, 1)
                        dve.wait_ge(y_taken, tok0 + m + 3)
                        own(nc.vector.tensor_scalar(y, y, r[0:n, m, PROB:PROB + 1], None, ALU.mult))
                        own.wait()
                        own(nc.vector.tensor_tensor(mask[0][0:n, :], y, y, ALU.not_equal))
                        own(nc.vector.tensor_scalar(mask[1][0:n, :], y, HUGE, None, ALU.is_gt))
                        own(nc.vector.tensor_scalar(mask[2][0:n, :], y, -HUGE, None, ALU.is_lt))
                        for k, v in enumerate((zero, big, neg)):
                            own.wait_apart(dve_passed)
                            own(nc.vector.copy_predicated(y, mask[k][0:n, :], v[0:n, :]))
                        own.wait()
                        nc.vector.tensor_tensor(y, y, r[0:n, m, 0:D], ALU.add).then_inc(y_ready, 1)
            own.leave(X // 2)


_INS = ["x", "src", "dst", "L0_gnn_W_l", "L0_gnn_b_l", "L0_gnn_W_r", "L0_gnn_ln_gamma", "L0_gnn_ln_beta",
        "L0_ffn_gate_w", "L0_ffn_gate_b", "L0_ffn_w1", "L0_ffn_b1", "L0_ffn_w2", "L0_ffn_b2"]


def kernel(**inputs):
    import concourse.bacc as _bacc
    import numpy as _np
    from concourse import mybir as _mybir
    from concourse.bass_utils import run_bass_kernel_spmd as _run

    nc = _bacc.Bacc("TRN2", target_bir_lowering=False, num_devices=1)
    arrays, args = {}, []
    for name in _INS:
        a = _np.asarray(inputs[name])
        if name in ("L0_gnn_W_l", "L0_gnn_W_r"):
            a = a.T
        a = _np.ascontiguousarray(a)
        arrays[f"in_{name}"] = a
        args.append(nc.dram_tensor(f"in_{name}", a.shape, _mybir.dt.from_np(a.dtype), kind="ExternalInput").ap())
    args.append(nc.dram_tensor("out_rows", (N, D), F32, kind="ExternalOutput").ap())
    gnn_moe(nc, *args)
    r = _run(nc, [arrays], core_ids=[0])
    return r.results[0]["out_rows"]
```

```python
from contextlib import ExitStack

import concourse.bass as bass
from concourse import mybir

F32 = mybir.dt.float32
I32 = mybir.dt.int32
F16 = mybir.dt.float16
ALU = mybir.AluOpType
ACT = mybir.ActivationFunctionType
AX = mybir.AxisListType

P = 128
N, D = 6250, 256
E = 200000
X, F = 8, 1024
CAP = -(-5 * N // (4 * X))
EPS = 1e-5
NT = -(-N // P)
LAST = N - (NT - 1) * P
DK = D // P
FK = F // P
ROW = D + 4
PROB, TOKEN, RSTD, NMR = D, D + 1, D + 2, D + 3
NOBODY = 1 << 20

G = 8
PAIRS = (NT - 1) // (2 * G)
assert NT == PAIRS * 2 * G + 1

T = 8
assert T % 2 == 0
COLS = 6
BLOCK = P * COLS
SLOTS = 4
RUNS = -(-E // (BLOCK * SLOTS))
HEAVY = 2
HEAVY_BLOCKS = 2
HEAVY_RUNS = HEAVY * HEAVY_BLOCKS * (P // 8) // SLOTS
EARLY_RUNS = HEAVY_RUNS + (T - HEAVY) * (P // 8) // SLOTS
PAD_RUNS = RUNS + EARLY_RUNS
PADDED = PAD_RUNS * SLOTS * BLOCK
NO_EDGE = 1 << 20
PAD_P = 64
assert (PADDED - E) % PAD_P == 0
PAD_N = (PADDED - E) // PAD_P
CT = -(-E // (P * P))
NC = CT * P
GD = 8
NG = T * P // GD
TG = P // GD
GW = GD * NT
ROUNDS = -(-NG // P)
GP = NG // ROUNDS
assert NT * P + SLOTS * 2 * (P + GW) <= NT * ROW
MOST = 2048.0
assert NG == ROUNDS * GP and NC * P <= PADDED and GW <= 512
COUNT_SCALE = 16.0
CNT = D + 1
SCALE = 4096.0
GROW = 2 * D + 2

TOK_TILES = -(-CAP // P)
TOK_LAST = CAP - (TOK_TILES - 1) * P
HALVES = [(0, 512), (512, CAP - 512)]
RSQRT_GUESS = 0x5F3759DF
COL_COPIES = -(-2 * CT // 4)
SOURCES = [range(NT * u // TG, NT * (u + 1) // TG) for u in range(TG)]
assert TG == 4 * SLOTS


class Own:

    def __init__(self, eng, sem):
        self.eng, self.sem, self.n, self.off, self.per = eng, sem, 0, None, None

    def __call__(self, ins):
        ins.then_inc(self.sem, 1)
        self.n += 1
        return ins

    def wait(self):
        self.eng.wait_ge(self.sem, self.n if self.off is None else self.off + self.n)

    def wait_apart(self, passed):
        self.wait()
        self.eng.sem_inc(passed, 1)

    def enter(self, i, per):
        self.start, self.off, self.per = self.n, i * per, per

    def leave(self, trips):
        assert self.n - self.start == self.per, (self.n - self.start, self.per)
        self.n, self.off = self.start + self.per * trips, None


def groups(eng, body, own=None, per=0):
    with eng.Fori(0, PAIRS) as i:
        if own:
            own.enter(i, per)
        for b in range(2):
            body(i * (2 * G) + b * G, G, b, i * 2 + b)
    if own:
        own.leave(PAIRS)
    body(NT - 1, 1, 0, 2 * PAIRS)


class Ranges:

    def __init__(self, eng, name, count, highest):
        self.eng, self.highest = eng, highest
        self.regs = [eng.alloc_register(f"{name}{k}") for k in range(2 * count)]

    def load(self, row, first):
        self.eng.load(self.regs, row[0:1, bass.ds(first * 2, len(self.regs))])

    def __getitem__(self, k):
        lo, hi = self.regs[2 * k:2 * k + 2]
        return (self.eng.snap(lo, min_val=0, max_val=self.highest - 1),
                self.eng.snap(hi, min_val=1, max_val=self.highest))


def block_of(nc, first_block, j):
    return nc.s_assert_within(first_block + j, 0, PAD_RUNS * SLOTS - 1, skip_runtime_bounds_check_because=(
        "either the last of all blocks alone or the blocks from 0 to SLOTS * RUNS - 1"))


def run_of(nc, first_run, k):
    return nc.s_assert_within(first_run + k, 0, PAD_RUNS - 1, skip_runtime_bounds_check_because=(
        "the runs are first_run + at most max(RUNS - first_run, EARLY_RUNS + 1) - 1, with first_run < RUNS"))


def gnn_moe(nc, x, src, dst, w_l, b_l, w_r, gamma, beta, gate_w, gate_b, w1, b1, w2, b2, out):
    ctx = ExitStack()
    with ctx:
        def sb(name, shape, dt=F32):
            return ctx.enter_context(nc.sbuf_tensor(name, shape, dt))

        def ps(name, shape):
            return ctx.enter_context(nc.psum_tensor(name, shape, F32))

        def sem(name):
            return ctx.enter_context(nc.semaphore(name))

        xn_table = nc.dram_tensor("xn_table", (N, 2 * D), F16).ap()
        slot_table = nc.dram_tensor("slot_table", (X * CAP, ROW), F32).ap()
        src_table = nc.dram_tensor("src_table", (PADDED,), I32).ap()
        dst_table = nc.dram_tensor("dst_table", (PADDED,), I32).ap()
        chunk_table = nc.dram_tensor("chunk_table", (2 * NC,), F32).ap()
        four_table = nc.dram_tensor("four_table", (NG * 2,), I32).ap()
        range_table = nc.dram_tensor("range_table", (2 * SLOTS * PAD_RUNS,), I32).ap()
        rows_table = nc.dram_tensor("rows_table", (P, NT, D), F32).ap()
        res_table = nc.dram_tensor("res_table", (P, NT, D), F32).ap()

        rows_flat = sb("rows", [P, NT * ROW])
        rows = rows_flat[:, :].rearrange("p (t d) -> p t d", t=NT)
        counts = rows_flat[:, 0:NT * P].bitcast(F16).rearrange("p (b h d) -> p b h d", b=2, h=NT)
        hot = rows_flat[:, NT * P:NT * P + SLOTS * 2 * (P + GW)].bitcast(F16).rearrange(
            "p (r h w) -> p r h w", r=SLOTS, h=4)
        res = sb("res", [P, NT * D])
        resid = res[:, :].rearrange("p (t d) -> p t d", t=NT)
        pieces = res[:, :].bitcast(F16).rearrange("p (t d) -> p t d", t=NT)
        sums_flat = sb("sums", [P, (NT + 1) * CNT])
        sums_from_one = sums_flat[:, :].rearrange("p (t d) -> p t d", t=NT + 1)
        sums = sums_from_one[:, 1:NT + 1, :]
        gath_flat = sb("gath", [P, SLOTS * COLS * GROW // 2])
        gath = gath_flat[:, :].bitcast(F16).rearrange("p (s k d) -> p s k d", s=SLOTS, k=COLS)
        chunk_ranges = gath_flat[:, 0:2 * NC].rearrange("p (q w t) -> p w t q", w=2, q=P)
        reached = gath_flat[:, 2 * NC:3 * NC]
        res_stage = gath_flat[:, 0:2 * G * D].rearrange("p (b g d) -> p b g d", b=2, g=G)
        stage_flat = sb("stage", [P, 2 * G * ROW])
        stage = stage_flat[:, :].rearrange("p (b g d) -> p b g d", b=2, g=G)
        edge_cols = stage_flat[:, 0:2 * NC]
        lane_col, key_col = edge_cols[:, 0:NC], edge_cols[:, NC:2 * NC]

        pad_ix = stage_flat[0:PAD_P, 0:2 * PAD_N].bitcast(I32).rearrange("p (w n) -> p w n", w=2)
        onehot = sb("onehot", [P, COLS, P], F16)

        lane16 = sb("lane16", [P, GW], F16)
        ones16 = sb("ones16", [P, 2], F16)
        zeros16 = sb("zeros16", [P, P], F16)
        group_base = sb("group_base", [P, NG])
        group_edges = sb("group_edges", [P, 2, ROUNDS])
        group_span = sb("group_span", [P, 2, ROUNDS])
        four_span = sb("four_span", [P, ROUNDS, 2], I32)
        chunk_span = sb("chunk_span", [P, 2, CT])
        meta = sb("meta", [1, 4], I32)
        again = sb("again", [1, 2], I32)
        lane_edges = sb("lane_edges", [P, NG])
        lanes_now = sb("lanes_now", [P, 2, TG])
        over_sb = sb("over", [P, 6])
        ident = sb("ident", [P, P])
        upper = sb("upper", [P, P])
        ones = sb("ones", [P, P])
        lane = sb("lane", [P, P])
        tile_base = sb("tile_base", [P, NT])
        w_l_gamma = sb("w_l_gamma", [P, max(DK * D + D, 2 * SLOTS * PAD_RUNS)])
        w_l_sb = w_l_gamma[:, 0:DK * D].rearrange("p (k d) -> p k d", k=DK)
        gamma_sb = w_l_gamma[:, DK * D:DK * D + D]
        range_row = w_l_gamma[0:1, 0:2 * SLOTS * PAD_RUNS].bitcast(I32)
        gate_w_sb = sb("gate_w_sb", [P, DK, X])
        gate_b_sb = sb("gate_b_sb", [P, X])
        b1_rows = sb("b1_rows", [X * FK, P])
        b1_sb = sb("b1_sb", [P, X * FK])
        b1_now = sb("b1_now", [P, 2, FK])
        xT = sb("xT", [P, 2, D])
        src_ix = sb("src_ix", [P, SLOTS, COLS], I32)
        dst_ix = sb("dst_ix", [P, SLOTS, COLS], I32)
        dst_rel = sb("dst_rel", [P, COLS])
        bn = sb("bn", [P, G, 6])
        mv = sb("mv", [P, G, 2])
        var = sb("var", [P, G])
        rs = sb("rs", [P, G])
        nt_ = sb("nt_", [P, G])
        nmr = sb("nmr", [P, G])
        rdeg = sb("rdeg", [P, NT])
        routing = sb("routing", [P, NT * X + 6 * NT])
        logits = routing[:, 0:NT * X].rearrange("p (t e) -> p t e", e=X)
        small = routing[:, NT * X:].rearrange("p (k t) -> p k t", k=6)
        four_row = routing[0:1, 0:NG * 2].bitcast(I32)
        fill = sb("fill", [P, ROW])

        dst_chunks, src_chunks, dst_f, lane_f, key_f, count_up = (
            sums_flat[:, k * NC:(k + 1) * NC] for k in range(6))
        lane_key_f = sums_flat[:, 3 * NC:5 * NC]
        o = 6 * NC
        w_r_sb = sums_flat[:, o:o + DK * D].rearrange("p (k d) -> p k d", k=DK)
        o += DK * D
        b_l_sb = sums_flat[:, o:o + D]
        beta_sb = sums_flat[:, o + D:o + 2 * D]
        n8 = NT * X

        def route(k):
            return stage_flat[:, k * n8:(k + 1) * n8].rearrange(
                "p (t e) -> p t e", e=X)

        picked, score, descend, before, place = (route(k) for k in range(5))
        notfirst = route(5).rearrange("p t e -> p (t e)").rearrange("p (e t) -> p e t", e=X)
        slot_ix = sb("slot_ix", [P, NT], I32)
        token_ix = sb("token_ix", [P, NT], I32)
        hidden = sums_flat[:, 0:FK * CAP].rearrange("p (f c) -> p f c", f=FK)
        inT = sums_flat[:, FK * CAP:FK * CAP + DK * CAP].rearrange("p (k c) -> p k c", k=DK)
        w1_sb = [gath_flat[:, 0:DK * F], res[:, 0:DK * F]]
        w2_sb = [gath_flat[:, DK * F:DK * F + FK * D], res[:, DK * F:DK * F + FK * D]]
        w1_sb = [w.rearrange("p (k f) -> p k f", k=DK) for w in w1_sb]
        w2_sb = [w.rearrange("p (k d) -> p k d", k=FK) for w in w2_sb]
        o = DK * F + FK * D
        b2_sb = [res[:, o + b * D:o + (b + 1) * D] for b in range(2)]
        o += 2 * D
        normed = [res[:, o + b * D:o + (b + 1) * D] for b in range(2)]
        o += 2 * D
        mask = [res[:, o + b * D:o + (b + 1) * D].bitcast(I32) for b in range(3)]
        o += 3 * D
        big, neg, zero = (res[:, o + b * D:o + (b + 1) * D] for b in range(3))
        o += 3 * D
        final = [res[:, o + b * D:o + (b + 1) * D] for b in range(2)]
        o += 2 * D
        slot_rows = [stage[:, b, :, :] for b in range(2)]

        pT = [ps(f"pT{b}", [P, 512]) for b in range(2)]
        pR = [ps(f"pR{b}", [P, 512]) for b in range(2)]
        pS = ps("pS", [P, 512])
        pG = ps("pG", [P, 512])
        pD = pR[0]
        pH = [ps(f"pH{b}", [P, 512]) for b in range(2)]

        x_in, consts_in, b1_in, table_filled = (sem(s) for s in (
            "x_in", "consts_in", "b1_in", "table_filled"))
        pe_passed, dve_passed = sem("pe_passed"), sem("dve_passed")
        pool_consts = sem("pool_consts")
        pool_step = sem("pool_step")
        dve_step = sem("dve_step")
        high_ready, pieces_ready = sem("high_ready"), sem("pieces_ready")
        xn_ready, xn_stored, stage_free, xs_ready, transposed0, xT_sb0, r_ps0, r_sb0, r_biased, b1T_ps, b1T_sb = (
            sem(s) for s in ("xn_ready", "xn_stored", "stage_free", "xs_ready", "transposed0", "xT_sb0", "r_ps0",
                             "r_sb0", "r_biased", "b1T_ps", "b1T_sb"))
        pads_set, padded, chunks_in, spans_found, spans_stored, spans_in, fours_found, fours_stored, fours_in = (
            sem(s) for s in ("pads_set", "padded", "chunks_in", "spans_found", "spans_stored", "spans_in", "fours_found",
                             "fours_stored", "fours_in"))
        fill_ready, rows_spilled, res_spilled, res_biased, ranges_ready, tail_xs = (sem(s) for s in (
            "fill_ready", "rows_spilled", "res_spilled", "res_biased", "ranges_ready", "tail_xs"))
        cols_ps, cols_sb,  counts_ps1, counts_taken, tile_summed, sums_taken = (
            sem(s) for s in ("cols_ps", "cols_sb",  "counts_ps1",
                             "counts_taken", "tile_summed", "sums_taken"))
        lanes_kept = sem("lanes_kept")
        sp_passed, ranges_found = sem("sp_passed"), sem("ranges_found")
        res_free, all_added, w_l_in = sem("res_free"), sem("all_added"), sem("w_l_in")
        ranges_saved, ranges_back, over_found, over_ps, again_ready = (sem(s) for s in (
            "ranges_saved", "ranges_back", "over_found", "over_ps", "again_ready"))
        hots_ready = [sem(f"hots_ready{r}") for r in range(SLOTS)]
        hots_used = [sem(f"hots_used{r}") for r in range(SLOTS)]
        empty_counts, back, sums_cleared, act_passed = (sem(s) for s in (
            "empty_counts", "back", "sums_cleared", "act_passed"))
        index_in = [sem(f"index_in{s}") for s in range(SLOTS)]
        gathered = [sem(f"gathered{s}") for s in range(SLOTS)]
        slot_claimed, block_done, onehot_ready, rel_ready, sum_ps, sum_added = (sem(s) for s in (
            "slot_claimed", "block_done", "onehot_ready", "rel_ready", "sum_ps", "sum_added"))
        sums_ready, mean_ready, xT_ps2, xT_sb2, f_ps, f_sb, g_sb, x1_ready, x1_stored, x2_ready, gT_ps, gT_sb, gate_ps, gate_sb = (
            sem(s) for s in ("sums_ready", "mean_ready", "xT_ps2", "xT_sb2", "f_ps", "f_sb", "g_sb", "x1_ready", "x1_stored",
                             "x2_ready", "gT_ps", "gT_sb", "gate_ps", "gate_sb"))
        shifted, exped, picked_ready, counts_ps, slots_ready, dispatched = (sem(s) for s in (
            "shifted", "exped", "picked_ready", "counts_ps", "slots_ready", "dispatched"))
        weights_in = [sem(f"weights_in{b}") for b in range(2)]
        rows_in = [sem(f"rows_in{b}") for b in range(2)]
        in_normed, inT_ps, inT_sb, hid_ps, hid_sb, y_ps, y_taken, y_ready = (sem(s) for s in (
            "in_normed", "inT_ps", "inT_sb", "hid_ps", "hid_sb", "y_ps", "y_taken", "y_ready"))
        b1_set = sem("b1_set")
        scattered = [sem(f"scattered{b}") for b in range(2)]
        scatter_claimed, final_free, tail_cleared = (sem(s) for s in ("scatter_claimed", "final_free", "tail_cleared"))

        CONSTS = 5 * 16
        block = ctx.enter_context(nc.Block())

        @block.sync
        def _(sp):
            sp.dma_start(dst_table[0:E].rearrange("(p n) -> p n", p=PAD_P), dst.rearrange("(p n) -> p n", p=PAD_P)
                         ).then_inc(padded, 16)
            sp.dma_start(src_table[0:E].rearrange("(p n) -> p n", p=PAD_P), src.rearrange("(p n) -> p n", p=PAD_P)
                         ).then_inc(padded, 16)
            sp.wait_ge(pads_set, 2)
            for w, at in enumerate((src_table, dst_table)):
                sp.dma_start(at[E:PADDED].rearrange("(p n) -> p n", p=PAD_P), pad_ix[:, w, :]).then_inc(padded, 16)
            sp.wait_ge(padded, 64)
            for at, of in ((dst_chunks, dst_table), (src_chunks, src_table)):
                sp.dma_start(at.bitcast(I32).rearrange("p (t e) -> p t e", t=CT),
                             of[0:NC * P].rearrange("(t p e) -> p t e", t=CT, p=P)).then_inc(chunks_in, 16)
            for c in range(6):
                sp.dma_start(rows[:, c * G:(c + 1) * G, 0:D],
                             x[c * G * P:(c + 1) * G * P, :].rearrange("(t p) d -> p t d", p=P)).then_inc(x_in, 16)
            sp.wait_ge(tail_cleared, 1)
            sp.dma_start(rows[0:LAST, NT - 1, 0:D], x[(NT - 1) * P:N, :]).then_inc(x_in, 16)
            sp.wait_ge(spans_found, 1)
            sp.dma_start(chunk_table.rearrange("(p w t) -> p w t", w=2, p=P), chunk_span[:, :, :]
                         ).then_inc(spans_stored, 16)
            sp.wait_ge(spans_stored, 16)
            sp.dma_start(gath_flat[:, 0:2 * NC], chunk_table.rearrange("(a c) -> a c", a=1).to_broadcast([P, 2 * NC])
                         ).then_inc(spans_in, 16)
            sp.wait_ge(fours_found, 1)
            sp.dma_start(four_table.rearrange("(r p c) -> p r c", r=ROUNDS, p=GP), four_span[0:GP, :, :]
                         ).then_inc(fours_stored, 16)
            sp.wait_ge(fours_stored, 16)
            sp.dma_start(four_row[:, :], four_table.rearrange("(a c) -> a c", a=1)).then_inc(fours_in, 16)

            sp.wait_ge(ranges_found, 1)
            sp.dma_start(range_table.rearrange("(a c) -> a c", a=1), range_row).then_inc(ranges_saved, 16)

            def store_xn(t0, nt, b, g):
                sp.wait_ge(pieces_ready, t0 + nt)
                if nt == G:
                    sp.dma_start(xn_table[bass.ds(t0 * P, G * P), :].rearrange("(t p) d -> p t d", p=P),
                                 pieces[:, bass.ds(t0, G), :]).then_inc(xn_stored, 16)
                else:
                    sp.dma_start(xn_table[t0 * P:N, :], pieces[0:LAST, t0, :]).then_inc(xn_stored, 16)
                sp.wait_ge(transposed0, t0 + nt)
                sp.sem_inc(stage_free, 1)
                sp.wait_ge(r_biased, t0 + nt)
                sp.dma_start(rows_table[:, bass.ds(t0, nt), :], rows[:, bass.ds(t0, nt), 0:D]).then_inc(rows_spilled, 16)
                sp.wait_ge(res_biased, t0 + nt)
                sp.dma_start(res_table[:, bass.ds(t0, nt), :], res_stage[:, b, 0:nt, :]).then_inc(res_spilled, 16)
                sp.wait_ge(res_spilled, g * 16 + 16)
                sp.sem_inc(res_free, 1)

            groups(sp, store_xn)

            sp.wait_ge(ranges_saved, 16)
            sp.wait_ge(ranges_ready, 1)
            first_run = sp.value_load(meta[0:1, 0:1], min_val=0, max_val=RUNS - 1)
            all_runs = sp.value_load(meta[0:1, 2:3], min_val=1, max_val=PAD_RUNS)
            with sp.Fori(0, all_runs) as k:
                for s in range(SLOTS):
                    sp.wait_ge(block_done, k * SLOTS + s + 1)
                    for at, of in ((src_ix, src_table), (dst_ix, dst_table)):
                        sp.dma_start(at[:, s, :],
                                     of[bass.ds(run_of(nc, first_run, k) * (SLOTS * BLOCK) + s * BLOCK, BLOCK)
                                        ].rearrange("(p k) -> p k", k=COLS)).then_inc(index_in[s], 16)
            sp.wait_ge(block_done, all_runs * SLOTS + SLOTS)
            sp.sem_inc(sp_passed, 1)
            sp.dma_start(range_row, range_table.rearrange("(a c) -> a c", a=1)).then_inc(ranges_back, 16)
            sp.wait_ge(again_ready, 1)
            first_block = sp.value_load(again[0:1, 0:1], min_val=0, max_val=PAD_RUNS * SLOTS - 1)
            blocks_again = sp.value_load(again[0:1, 1:2], min_val=1, max_val=SLOTS * RUNS)
            with sp.Fori(0, blocks_again) as j:
                sp.wait_ge(block_done, all_runs * SLOTS + SLOTS + j)
                for at, of in ((src_ix, src_table), (dst_ix, dst_table)):
                    sp.dma_start(at[:, 0, :], of[bass.ds(block_of(nc, first_block, j) * BLOCK, BLOCK)
                                                 ].rearrange("(p k) -> p k", k=COLS)).then_inc(index_in[0], 16)

            def store_x1(t0, nt, b, g):
                sp.wait_ge(x1_ready, g + 1)
                if nt == G:
                    sp.dma_start(out[bass.ds(t0 * P, G * P), :].rearrange("(t p) d -> p t d", p=P),
                                 rows[:, bass.ds(t0, G), 0:D]).then_inc(x1_stored, 16)
                else:
                    sp.dma_start(out[t0 * P:N, :], rows[0:LAST, t0, 0:D]).then_inc(x1_stored, 16)

            groups(sp, store_x1)

            def load_weights(e, b):
                sp.dma_start(w1_sb[b], w1[e, :, :].rearrange("(k p) f -> p k f", p=P)).then_inc(weights_in[b], 16)
                sp.dma_start(w2_sb[b], w2[e, :, :].rearrange("(k p) d -> p k d", p=P)).then_inc(weights_in[b], 16)
                sp.dma_start(b2_sb[b], b2[e, :].rearrange("(a d) -> a d", a=1).to_broadcast([P, D])
                             ).then_inc(weights_in[b], 16)

            def load_rows(e, b):
                first = e * CAP
                full = (TOK_TILES - 1) * P
                sp.dma_start(slot_rows[b][:, 0:TOK_TILES - 1, :],
                             slot_table[bass.ds(first, full), :].rearrange("(t p) d -> p t d", p=P)
                             ).then_inc(rows_in[b], 16)
                sp.dma_start(slot_rows[b][0:TOK_LAST, TOK_TILES - 1, :],
                             slot_table[bass.ds(first + full, TOK_LAST), :]).then_inc(rows_in[b], 16)

            sp.wait_ge(slots_ready, 2)
            for b in range(2):
                load_weights(b, b)
            sp.wait_ge(dispatched, 16 * NT)
            for b in range(2):
                load_rows(b, b)
            with sp.Fori(1, X // 2) as i:
                for b in range(2):
                    sp.wait_ge(final_free, i * (2 * TOK_TILES) + (b - 1) * TOK_TILES + 2)
                    load_weights(i * 2 + b, b)
                    load_rows(i * 2 + b, b)

            sp.wait_ge(x1_stored, 16 * (2 * PAIRS + 1))
            for b in range(2):
                sp.wait_ge(scattered[b], 16 * X * TOK_TILES // 2)

        @block.gpsimd
        def _(pool):
            own = Own(pool, pool_step)
            nc.gpsimd.memset(rows[:, NT - 1, :], 0.0).then_inc(tail_cleared, 1)
            own(nc.gpsimd.memset(ones[:, :], 1.0))
            own(nc.gpsimd.memset(ident[:, :], 0.0))
            own.wait()
            nc.gpsimd.affine_select(out=ident[:, :], in_=ident[:, :], compare_op=ALU.not_equal, fill=1.0, base=0,
                                    pattern=[[-1, P]], channel_multiplier=1).then_inc(pool_consts, 1)
            nc.gpsimd.affine_select(out=upper[:, :], in_=ones[:, :], compare_op=ALU.is_ge, fill=0.0, base=0,
                                    pattern=[[1, P]], channel_multiplier=-1).then_inc(pool_consts, 1)
            own(nc.gpsimd.memset(ones16[:, :], 1.0))
            own(nc.gpsimd.memset(zeros16[:, :], 0.0))
            nc.gpsimd.iota(group_base[:, :], [[-GW, NG]], base=0, channel_multiplier=0,
                           allow_small_or_imprecise_dtypes=True).then_inc(pool_consts, 1)
            nc.gpsimd.iota(lane16[:, :], [[1, GW]], base=0, channel_multiplier=0,
                           allow_small_or_imprecise_dtypes=True).then_inc(pool_consts, 1)
            for w in range(2):
                nc.gpsimd.iota(group_edges[:, w, :], [[GD * GP, ROUNDS]], base=GD * w, channel_multiplier=GD,
                               allow_small_or_imprecise_dtypes=True).then_inc(pool_consts, 1)
            nc.gpsimd.iota(count_up, [[1, NC]], base=1, channel_multiplier=0,
                           allow_small_or_imprecise_dtypes=True).then_inc(pool_consts, 1)
            nc.gpsimd.iota(lane[:, :], [[1, P]], base=0, channel_multiplier=0,
                           allow_small_or_imprecise_dtypes=True).then_inc(pool_consts, 1)
            nc.gpsimd.iota(tile_base[:, :], [[P, NT]], base=0, channel_multiplier=0,
                           allow_small_or_imprecise_dtypes=True).then_inc(pool_consts, 1)
            nc.gpsimd.iota(token_ix[:, :], [[P, NT]], base=0, channel_multiplier=1).then_inc(pool_consts, 1)
            own(nc.gpsimd.memset(fill[:, :], 0.0))
            own.wait()
            nc.gpsimd.memset(fill[:, TOKEN:TOKEN + 1].bitcast(I32), NOBODY).then_inc(fill_ready, 1)

            def biases(t0, nt, b, g):
                pool.wait_ge(xs_ready, g + 1)
                v = rows[:, bass.ds(t0, nt), 0:D]
                nc.gpsimd.tensor_tensor(v, v, beta_sb[:, :].unsqueeze(1).to_broadcast([P, nt, D]),
                                        ALU.add).then_inc(r_biased, nt)
                pool.wait_ge(r_sb0, t0 + nt + 2)
                v = res_stage[:, b, 0:nt, :]
                nc.gpsimd.tensor_tensor(v, v, b_l_sb[:, :].unsqueeze(1).to_broadcast([P, nt, D]),
                                        ALU.add).then_inc(res_biased, nt)

            pool.wait_ge(consts_in, CONSTS)
            groups(pool, biases)

            pool.wait_ge(res_spilled, 16 * (2 * PAIRS + 1))
            for s in range(SLOTS):
                nc.gpsimd.memset(gath[:, s, :, 2 * D:2 * D + 1], 1.0).then_inc(fill_ready, 1)
            pool.wait_ge(xn_stored, 16 * (2 * PAIRS + 1))
            pool.wait_ge(ranges_ready, 1)
            all_runs = pool.value_load(meta[0:1, 2:3], min_val=1, max_val=PAD_RUNS)
            with pool.Fori(0, all_runs) as k:
                for s in range(SLOTS):
                    pool.wait_ge(index_in[s], k * 32 + 32)
                    pool.sem_inc(slot_claimed, 1)
                    for c in range(COLS):
                        nc.gpsimd.indirect_dma_start(
                            gath[:, s, c, 0:2 * D], None, xn_table,
                            bass.IndirectOffsetOnAxis(ap=src_ix[:, s, c:c + 1], axis=0)).then_inc(gathered[s], 16)
            pool.wait_ge(again_ready, 1)
            blocks_again = pool.value_load(again[0:1, 1:2], min_val=1, max_val=SLOTS * RUNS)
            with pool.Fori(0, blocks_again) as j:
                pool.wait_ge(index_in[0], all_runs * 32 + j * 32 + 32)
                pool.sem_inc(slot_claimed, 1)
                for c in range(COLS):
                    nc.gpsimd.indirect_dma_start(
                        gath[:, 0, c, 0:2 * D], None, xn_table,
                        bass.IndirectOffsetOnAxis(ap=src_ix[:, 0, c:c + 1], axis=0)).then_inc(gathered[0], 16)

            pool.wait_ge(slots_ready, 2)
            pool.wait_ge(table_filled, 32)
            for t in range(NT):
                n = P if t < NT - 1 else LAST
                nc.gpsimd.indirect_dma_start(
                    slot_table, bass.IndirectOffsetOnAxis(ap=slot_ix[0:n, t:t + 1], axis=0), rows[0:n, t, :], None,
                    bounds_check=X * CAP - 1, oob_is_err=False).then_inc(dispatched, 16)

            pool.wait_ge(x1_stored, 16 * (2 * PAIRS + 1))
            with pool.Fori(0, X // 2) as i:
                for b in range(2):
                    for m in range(TOK_TILES):
                        n = P if m < TOK_TILES - 1 else TOK_LAST
                        c = m % 2
                        k = b * TOK_TILES + m
                        pool.wait_ge(y_ready, i * (2 * TOK_TILES) + k + 1)
                        pool.sem_inc(scatter_claimed, 1)
                        nc.gpsimd.indirect_dma_start(
                            out, bass.IndirectOffsetOnAxis(ap=slot_rows[b][0:n, m, TOKEN:TOKEN + 1].bitcast(I32), axis=0),
                            final[c][0:n, :], None, bounds_check=N - 1, oob_is_err=False).then_inc(scattered[c], 16)
                        pool.wait_ge(scattered[c], i * (16 * TOK_TILES) + 16 * (k // 2 + 1))
                        pool.sem_inc(final_free, 1)

        @block.tensor
        def _(pe):
            def transpose_rows(at, of, n, ready, at_rows=P):
                for k in range(DK):
                    last = nc.tensor.transpose(at[:, k * P:k * P + n], of[0:n, k * P:(k + 1) * P], ident[0:n, 0:n])
                return last.then_inc(ready, 1)

            def linear(at, of, w, ready):
                for k in range(DK):
                    last = nc.tensor.matmul(at[:, 0:D], of[:, k * P:(k + 1) * P], w[:, k, :],
                                            start=(k == 0), stop=(k == DK - 1))
                return last.then_inc(ready, 1)

            pe.wait_ge(pool_consts, 10)
            pe.wait_ge(b1_in, 16)
            nc.tensor.transpose(pG[:, 0:X * FK], b1_rows[:, :], ident[0:X * FK, 0:X * FK]).then_inc(b1T_ps, 1)
            pe.wait_ge(consts_in, CONSTS)

            def transposes0(t0, j, b):
                pe.wait_ge(xn_ready, t0 + j + 1)
                pe.wait_ge(xT_sb0, t0 + j + 1)
                transpose_rows(pT[j % 2], stage[:, b, j, 0:D], P, transposed0)

            def linear0(t0, j):
                pe.wait_ge(xT_sb0, t0 + j + 3)
                pe.wait_ge(r_sb0, t0 + j + 1)
                linear(pR[j % 2], xT[:, j % 2, :], w_r_sb, r_ps0)

            def group0(t0, nt, b, g):
                for j in range(nt + 1):
                    if j < nt:
                        transposes0(t0, j, b)
                    if j > 0:
                        linear0(t0, j - 1)

            groups(pe, group0)

            for q in range(COL_COPIES):
                if q >= 2:
                    pe.wait_ge(cols_sb, q - 1)
                elif q == 0:
                    pe.wait_ge(xT_sb0, NT + 2)
                for k in range(4 * q, min(4 * q + 4, 2 * CT)):
                    last = nc.tensor.transpose(pT[q % 2][:, (k % 4) * P:(k % 4 + 1) * P],
                                               lane_key_f[:, k * P:(k + 1) * P], ident[:, :])
                last.then_inc(cols_ps, 1)

            item = pe.alloc_register("pe_item")
            chunk = [pe.alloc_register(f"pe_chunk{r}") for r in range(SLOTS)]
            for r in chunk:
                pe.reg_mov(r, 0)
            pe.reg_mov(item, 0)
            pe.wait_ge(fours_in, 16)
            pe.wait_ge(r_sb0, NT + 2)
            pe.wait_ge(empty_counts, 1)
            first_run = pe.value_load(meta[0:1, 0:1], min_val=0, max_val=RUNS - 1)
            more_runs = pe.value_load(meta[0:1, 1:2], min_val=1, max_val=RUNS)
            group_fours = Ranges(pe, "pe_fours", TG // 2, NC // 4)
            block_tiles = Ranges(pe, "pe_tiles", SLOTS, NT)

            def count_group(g, q):
                c, r = q % 2, q % SLOTS
                pe.wait_ge(counts_taken, g + 1)
                nc.tensor.matmul(pH[c][:, 0:GW], zeros16[:, :], lane16[:, :], start=True, stop=False)
                with pe.Fori(*group_fours[q % (TG // 2)]):
                    for h in range(4):
                        pe.reg_add(chunk[r], chunk[r], 1)
                        pe.wait_ge(hots_ready[r], pe.snap(chunk[r]))
                        nc.tensor.matmul(pH[c][:, 0:GW], hot[:, r, h, 0:P], hot[:, r, h, P:P + GW],
                                         start=False, stop=False).then_inc(hots_used[r], 1)
                nc.tensor.matmul(pH[c][:, 0:GW], zeros16[:, :], lane16[:, :], start=False, stop=True
                                 ).then_inc(counts_ps1, 1)

            def sum_sources(b, sources):
                for h in sources:
                    first, last = h == 0, h == NT - 1
                    of = counts[:, b, h, :]
                    nc.tensor.matmul(pG[:, 0:1], of, ones16[:, 0:1], start=first, stop=last)
                    nc.tensor.matmul(pD[:, 0:D], of, pieces[:, h, D:2 * D], start=first, stop=False)
                    done = nc.tensor.matmul(pD[:, 0:D], of, pieces[:, h, 0:D], start=False, stop=last)
                if h == NT - 1:
                    done.then_inc(tile_summed, 1)

            def sum_block(s, k, tiles):
                pe.wait_ge(gathered[s], k * (16 * COLS) + 16 * COLS)
                pe.sem_inc(pe_passed, 1)
                with pe.Fori(*tiles):
                    pe.reg_add(item, item, 1)
                    pe.wait_ge(onehot_ready, pe.snap(item))
                    for c in range(COLS):
                        nc.tensor.matmul(pS[:, 0:CNT], onehot[:, c, :], gath[:, s, c, D:D + CNT],
                                         start=(c == 0), stop=False)
                        last = nc.tensor.matmul(pS[:, 0:D], onehot[:, c, :], gath[:, s, c, 0:D],
                                                start=False, stop=(c == COLS - 1))
                    last.then_inc(sum_ps, 1)
                nc.tensor.matmul(pT[0][:, 0:1], zeros16[:, :], ones16[:, 0:1], start=True, stop=True
                                 ).then_inc(block_done, 1)

            nc.tensor.matmul(pS[:, 0:CNT], zeros16[:, :], lane16[:, 0:CNT], start=True, stop=True).then_inc(sum_ps, 1)
            def two_tiles(i, blocks, first):
                for tb in range(2):
                    for q in range(TG):
                        g = i * (2 * TG) + tb * TG + q
                        if q % (TG // 2) == 0:
                            group_fours.load(four_row, g)
                        count_group(g, q)
                        if q == 0:
                            pe.wait_ge(counts_taken, i * (2 * TG) + tb * TG + 2)
                            pe.wait_ge(sums_taken, i * 2 + tb + 1)
                        sum_sources(1 - tb, SOURCES[q])
                        for n in range((tb * TG + q) * blocks, (tb * TG + q + 1) * blocks):
                            k = first + n // SLOTS
                            if n % SLOTS == 0:
                                block_tiles.load(range_row, run_of(nc, first_run, k) * SLOTS)
                            sum_block(n % SLOTS, k, block_tiles[n % SLOTS])

            two_tiles(0, HEAVY_BLOCKS, 0)
            with pe.Fori(1, T // 2) as i:
                two_tiles(i, 1, i * (2 * TG // SLOTS) + (HEAVY_RUNS - 2 * TG // SLOTS))
            pe.wait_ge(counts_taken, NG + 2)
            pe.wait_ge(sums_taken, T + 1)
            sum_sources(1, range(NT))
            with pe.Fori(0, more_runs) as k:
                block_tiles.load(range_row, run_of(nc, first_run, k + EARLY_RUNS) * SLOTS)
                for s in range(SLOTS):
                    sum_block(s, k + EARLY_RUNS, block_tiles[s])

            pe.wait_ge(over_found, 1)
            nc.tensor.matmul(pG[:, 0:1], ones[:, :], over_sb[:, 0:1], start=True, stop=True).then_inc(over_ps, 1)
            pe.wait_ge(again_ready, 1)
            all_runs = pe.value_load(meta[0:1, 2:3], min_val=1, max_val=PAD_RUNS)
            first_block = pe.value_load(again[0:1, 0:1], min_val=0, max_val=PAD_RUNS * SLOTS - 1)
            blocks_again = pe.value_load(again[0:1, 1:2], min_val=1, max_val=SLOTS * RUNS)
            one_block = Ranges(pe, "pe_again", 1, NT)
            with pe.Fori(0, blocks_again) as j:
                one_block.load(range_row, block_of(nc, first_block, j))
                sum_block(0, all_runs + j, one_block[0])

            pe.wait_ge(w_l_in, 32)

            def group2(t0, nt, b, g):
                for j in range(nt + 1):
                    if j < nt:
                        pe.wait_ge(xT_sb2, t0 + j + 1)
                        if j < 2:
                            pe.wait_ge(gT_sb, t0 + 2)
                        pe.wait_ge(mean_ready, t0 + j + 1)
                        transpose_rows(pT[j % 2], stage[:, b, j, 0:D], P, xT_ps2)
                    if j > 0:
                        pe.wait_ge(xT_sb2, t0 + j + 2)
                        pe.wait_ge(f_sb, t0 + j)
                        linear(pR[(j - 1) % 2], xT[:, (j - 1) % 2, :], w_l_sb, f_ps)
                for j in range(nt + 1):
                    if j < nt:
                        pe.wait_ge(x2_ready, t0 + j + 1)
                        pe.wait_ge(gT_sb, t0 + j + 1)
                        transpose_rows(pT[j % 2], stage[:, b, j, 0:D], P, gT_ps)
                    if j > 0:
                        pe.wait_ge(gT_sb, t0 + j + 2)
                        if j == 1:
                            pe.wait_ge(gate_sb, g + 1)
                        for k in range(DK):
                            last = nc.tensor.matmul(pG[:, (j - 1) * X:j * X], xT[:, (j - 1) % 2, k * P:(k + 1) * P],
                                                    gate_w_sb[:, k, :], start=(k == 0), stop=(k == DK - 1))
                        last.then_inc(gate_ps, 1)

            groups(pe, group2)

            pe.wait_ge(picked_ready, 1)
            flat = picked.rearrange("p t e -> p (t e)")
            nc.tensor.matmul(pR[0][:, 0:n8], upper[:, :], flat, start=True, stop=True).then_inc(counts_ps, 1)
            nc.tensor.matmul(pR[1][:, 0:n8], ones[:, :], flat, start=True, stop=True).then_inc(counts_ps, 1)

            with pe.Fori(0, X // 2) as i:
                for b in range(2):
                    tok0 = i * (2 * TOK_TILES) + b * TOK_TILES
                    for m in range(TOK_TILES):
                        n = P if m < TOK_TILES - 1 else TOK_LAST
                        pe.wait_ge(in_normed, tok0 + m + 1)
                        pe.wait_ge(inT_sb, tok0 + m + 1)
                        transpose_rows(pT[m % 2], normed[m % 2], n, inT_ps)
                    pe.wait_ge(inT_sb, tok0 + TOK_TILES + 2)
                    pe.wait_ge(weights_in[b], i * 48 + 48)
                    for h, (c0, cn) in enumerate(HALVES):
                        for f in range(FK):
                            u = h * FK + f
                            pe.wait_ge(hid_sb, i * (4 * FK) + b * 2 * FK + u + 1)
                            for k in range(DK):
                                last = nc.tensor.matmul(pH[u % 2][:, 0:cn], w1_sb[b][:, k, f * P:(f + 1) * P],
                                                        inT[:, k, c0:c0 + cn], start=(k == 0), stop=(k == DK - 1))
                            last.then_inc(hid_ps, 1)
                    for m in range(TOK_TILES):
                        n = P if m < TOK_TILES - 1 else TOK_LAST
                        if m == 0:
                            pe.wait_ge(hid_sb, i * (4 * FK) + b * 2 * FK + FK + 2)
                        if m * P + n > HALVES[0][1] and m * P < HALVES[0][1] + P:
                            pe.wait_ge(hid_sb, i * (4 * FK) + b * 2 * FK + 2 * FK + 2)
                        pe.wait_ge(y_taken, tok0 + m + 1)
                        for f in range(FK):
                            last = nc.tensor.matmul(pR[m % 2][0:n, 0:D], hidden[:, f, m * P:m * P + n],
                                                    w2_sb[b][:, f, :], start=(f == 0), stop=(f == FK - 1))
                        last.then_inc(y_ps, 1)

        @block.scalar
        def _(act):
            act.dma_start(w_r_sb, w_r.rearrange("(k p) n -> p k n", p=P)).then_inc(consts_in, 16)
            for at, of in ((b_l_sb, b_l), (beta_sb, beta), (gate_b_sb, gate_b)):
                act.dma_start(at[:, :], of.rearrange("(a d) -> a d", a=1).to_broadcast([P, at.shape[1]])
                              ).then_inc(consts_in, 16)
            act.dma_start(gate_w_sb[:, :, :], gate_w.rearrange("(k p) n -> p k n", p=P)).then_inc(consts_in, 16)
            act.dma_start(b1_rows[:, :], b1.rearrange("e (k p) -> (e k) p", p=P)).then_inc(b1_in, 16)
            for free, n in ((res_free, 2), (tile_summed, 1), (sums_taken, 1), (xT_sb0, 2), (r_sb0, 2), (xT_sb2, 2), (gT_sb, 2), (gate_sb, 1), (inT_sb, 2), (hid_sb, 2)):
                act.sem_inc(free, n)
            act.wait_ge(b1T_ps, 1)
            nc.scalar.copy(b1_sb[:, :], pG[:, 0:X * FK]).then_inc(b1T_sb, 1)

            def group0(t0, nt, b, g):
                act.wait_ge(xn_ready, t0 + nt)
                act.sem_inc(act_passed, 1)
                nc.scalar.activation(pieces[:, bass.ds(t0, nt), 0:D], stage[:, b, 0:nt, 0:D], ACT.Copy,
                                     scale=SCALE).then_inc(high_ready, 1)
                for j in range(nt + 1):
                    if j < nt:
                        act.wait_ge(transposed0, t0 + j + 1)
                        act.wait_ge(r_ps0, t0 + j + 1)
                        nc.scalar.copy(xT[:, j % 2, :], pT[j % 2][:, 0:D]).then_inc(xT_sb0, 1)
                    if j > 0:
                        act.wait_ge(r_ps0, t0 + j + 2)
                        if j == 1:
                            act.wait_ge(res_free, g + 1)
                        nc.scalar.copy(res_stage[:, b, j - 1, :],
                                       pR[(j - 1) % 2][:, 0:D]).then_inc(r_sb0, 1)

            act.sem_inc(r_ps0, 2)
            groups(act, group0)

            act.wait_ge(stage_free, 2 + 2 * PAIRS + 1)
            for q in range(COL_COPIES):
                act.wait_ge(cols_ps, q + 1)
                n = min(4, 2 * CT - 4 * q) * P
                nc.scalar.copy(edge_cols[:, 4 * q * P:4 * q * P + n], pT[q % 2][:, 0:n]).then_inc(cols_sb, 1)
            act.wait_ge(rows_spilled, 16 * (2 * PAIRS + 1))

            act.wait_ge(fill_ready, 1)
            nc.scalar.copy(rows_flat[:, NT * P // 2:NT * P], fill[:, 0:1].to_broadcast([P, NT * P // 2])
                           ).then_inc(empty_counts, 1)
            act.wait_ge(res_biased, NT)
            nc.scalar.copy(sums_flat[:, T * CNT:], fill[:, 0:1].to_broadcast([P, (NT + 1 - T) * CNT]))
            nc.scalar.copy(sums_flat[:, 0:T * CNT], fill[:, 0:1].to_broadcast([P, T * CNT])
                           ).then_inc(sums_cleared, 1)
            act.wait_ge(fill_ready, 1)
            full = X * CAP // P
            act.dma_start(slot_table[0:full * P, :].rearrange("(p t) d -> p t d", p=P),
                          fill[:, :].unsqueeze(1).to_broadcast([P, full, ROW])).then_inc(table_filled, 16)
            act.dma_start(slot_table[full * P:X * CAP, :], fill[0:X * CAP - full * P, :]).then_inc(table_filled, 16)
            with act.Fori(0, T // 2) as i:
                for tb in range(2):
                    act.wait_ge(tile_summed, i * 2 + tb + 1)
                    for q in range(TG):
                        act.wait_ge(counts_ps1, i * (2 * TG) + tb * TG + q + 1)
                        nc.scalar.activation(counts[:, tb, :, q * GD:(q + 1) * GD].rearrange("p h d -> p d h"),
                                             pH[q % 2][:, 0:GW].rearrange("p (d h) -> p d h", d=GD), ACT.Copy,
                                             scale=1.0 / COUNT_SCALE, accum_out=lanes_now[:, tb, q:q + 1]
                                             ).then_inc(counts_taken, 1)
                    act.wait_ge(counts_taken, i * (2 * TG) + tb * TG + TG + 2)
                    act.sem_inc(act_passed, 1)
                    nc.scalar.copy(lane_edges[:, bass.ds(i * (2 * TG) + tb * TG, TG)], lanes_now[:, tb, :]
                                   ).then_inc(lanes_kept, 1)
                    act.wait_ge(tile_summed, i * 2 + tb + 2)
                    if tb == 0:
                        act.wait_ge(sums_cleared, 1)
                    act.sem_inc(act_passed, 1)
                    at = sums_from_one[:, bass.ds(i * 2 + tb, 1), :].rearrange("p a d -> p (a d)")
                    nc.scalar.activation(at[:, D:CNT], pG[:, 0:1], ACT.Copy, scale=COUNT_SCALE)
                    nc.scalar.activation(at[:, 0:D], pD[:, 0:D], ACT.Copy, scale=COUNT_SCALE).then_inc(sums_taken, 1)
            act.wait_ge(tile_summed, T + 2)
            nc.scalar.activation(sums_from_one[:, T, D:CNT], pG[:, 0:1], ACT.Copy, scale=COUNT_SCALE)
            nc.scalar.activation(sums_from_one[:, T, 0:D], pD[:, 0:D], ACT.Copy,
                                 scale=COUNT_SCALE).then_inc(sums_taken, 1)
            act.dma_start(rows[:, :, 0:D], rows_table).then_inc(back, 16)
            act.dma_start(resid, res_table).then_inc(back, 16)
            act.wait_ge(all_added, 1)
            act.dma_start(w_l_sb, w_l.rearrange("(k p) n -> p k n", p=P)).then_inc(w_l_in, 16)
            act.dma_start(gamma_sb, gamma.rearrange("(a d) -> a d", a=1).to_broadcast([P, D])).then_inc(w_l_in, 16)

            act.sem_inc(f_ps, 2)
            act.sem_inc(gate_ps, 2)
            act.wait_ge(sums_ready, 1)

            def group2(t0, nt, b, g):
                def mean(j):
                    nc.scalar.activation(stage[:, b, j, 0:D],
                                         sums[:, bass.ds(t0 + j, 1), 0:D].rearrange("p a d -> p (a d)"), ACT.Copy,
                                         scale=rdeg[:, bass.ds(t0 + j, 1)]).then_inc(mean_ready, 1)

                mean(0)
                for j in range(nt + 2):
                    if j + 1 < nt:
                        mean(j + 1)
                    if j < nt:
                        act.wait_ge(xT_ps2, t0 + j + 1)
                        act.wait_ge(f_ps, t0 + j + 1)
                        if j < 2:
                            act.wait_ge(gate_ps, t0 + 2)
                        nc.scalar.copy(xT[:, j % 2, :], pT[j % 2][:, 0:D]).then_inc(xT_sb2, 1)
                    if j > 1:
                        act.wait_ge(f_sb, t0 + j + 1)
                        v = resid[:, bass.ds(t0 + j - 2, 1), :].rearrange("p a d -> p (a d)")
                        nc.scalar.activation(v, v, ACT.Gelu).then_inc(g_sb, 1)
                for j in range(nt):
                    act.wait_ge(gT_ps, t0 + j + 1)
                    act.wait_ge(gate_ps, t0 + j + 1)
                    nc.scalar.copy(xT[:, j % 2, :], pT[j % 2][:, 0:D]).then_inc(gT_sb, 1)
                act.wait_ge(gate_ps, t0 + nt + 2)
                nc.scalar.copy(logits[:, bass.ds(t0, nt), :],
                               pG[:, 0:nt * X].rearrange("p (t e) -> p t e", e=X)).then_inc(gate_sb, 1)

            groups(act, group2)

            act.wait_ge(shifted, 1)
            nc.scalar.activation(before[:, :, :], before[:, :, :], ACT.Exp).then_inc(exped, 1)

            act.wait_ge(b1T_sb, 1)
            act.wait_ge(counts_ps, 2)
            act.sem_inc(hid_ps, 2)
            with act.Fori(0, X // 2) as i:
                for b in range(2):
                    tok0 = i * (2 * TOK_TILES) + b * TOK_TILES
                    for m in range(TOK_TILES):
                        n = P if m < TOK_TILES - 1 else TOK_LAST
                        act.wait_ge(inT_ps, tok0 + m + 1)
                        if m == 0:
                            act.wait_ge(hid_ps, i * (4 * FK) + b * 2 * FK + 2)
                        nc.scalar.copy(inT[:, :, m * P:m * P + n],
                                       pT[m % 2][:, 0:D].rearrange("p (k c) -> p k c", k=DK)[:, :, 0:n]
                                       ).then_inc(inT_sb, 1)
                    nc.scalar.copy(b1_now[:, b, :], b1_sb[:, bass.ds(i * (2 * FK) + b * FK, FK)]).then_inc(b1_set, 1)
                    act.wait_ge(b1_set, i * 2 + b + 1)
                    for h, (c0, cn) in enumerate(HALVES):
                        for f in range(FK):
                            u = h * FK + f
                            act.wait_ge(hid_ps, i * (4 * FK) + b * 2 * FK + u + 3)
                            if u == 0:
                                act.wait_ge(y_ps, tok0 + 1)
                            nc.scalar.activation(hidden[:, f, c0:c0 + cn], pH[u % 2][:, 0:cn], ACT.Relu,
                                                 bias=b1_now[:, b, f:f + 1]).then_inc(hid_sb, 1)

        @block.vector
        def _(dve):
            own = Own(dve, dve_step)
            for free, n in ((stage_free, 2), (block_done, SLOTS), (sum_added, 1), *((used, 4) for used in hots_used), (counts_taken, 2), (f_sb, 2), (y_taken, 2), (y_ps, 1),
                            (final_free, 2)):
                dve.sem_inc(free, n)

            def rsqrt(nt):
                v, y, w = var[:, 0:nt], rs[:, 0:nt], nt_[:, 0:nt]
                own(nc.vector.tensor_scalar(v, mv[:, 0:nt, 1], EPS, None, ALU.add))
                own.wait()
                own(nc.vector.tensor_scalar(w.bitcast(I32), v.bitcast(I32), 1, None, ALU.logical_shift_right))
                own.wait()
                own(nc.vector.tensor_scalar(y.bitcast(I32), w.bitcast(I32), -1.0, float(RSQRT_GUESS), ALU.mult, ALU.add))
                for _ in range(4):
                    own.wait()
                    own(nc.vector.scalar_tensor_tensor(w, y, -0.5, y, ALU.mult, ALU.mult))
                    own.wait()
                    own(nc.vector.tensor_tensor(w, w, v, ALU.mult))
                    own.wait()
                    own(nc.vector.scalar_tensor_tensor(y, w, 1.5, y, ALU.add, ALU.mult))
                own.wait()
                own(nc.vector.scalar_tensor_tensor(nmr[:, 0:nt], mv[:, 0:nt, 0], -1.0, y, ALU.mult, ALU.mult))
                own.wait()

            RSQRT_STEPS = 3 + 4 * 3 + 1

            def moments(views):
                dve.sem_inc(dve_passed, 1)
                for j, v in enumerate(views):
                    own(nc.vector.bn_stats(bn[:, j, :], v))
                own.wait_apart(dve_passed)
                for j in range(len(views)):
                    own(nc.vector.bn_aggr(mv[:, j, :], bn[:, j, :]))
                own.wait()

            def tile_rows(t):
                return rows[:, bass.ds(t, 1), 0:D].rearrange("p a d -> p (a d)")

            def tile_res(t):
                return resid[:, bass.ds(t, 1), :].rearrange("p a d -> p (a d)")

            nc.vector.memset(pad_ix[:, 0, :], 0).then_inc(pads_set, 1)
            nc.vector.memset(pad_ix[:, 1, :], NO_EDGE).then_inc(pads_set, 1)
            dve.wait_ge(chunks_in, 32)
            own(nc.vector.tensor_copy(dst_f, dst_chunks.bitcast(I32)))
            own.wait()
            for w, op in enumerate((ALU.min, ALU.max)):
                own(nc.vector.tensor_reduce(chunk_span[:, w, :], dst_f.rearrange("p (t e) -> p t e", t=CT), AX.X, op))
            own.wait()
            nc.vector.engine_nop().then_inc(spans_found, 1)
            taken = dst_chunks
            own(nc.vector.tensor_scalar(taken.bitcast(I32), src_chunks.bitcast(I32), P - 1, None, ALU.bitwise_and))
            own.wait()
            own(nc.vector.tensor_copy(lane_f, taken.bitcast(I32)))
            own.wait()
            own(nc.vector.tensor_scalar(taken.bitcast(I32), src_chunks.bitcast(I32), 7, None, ALU.logical_shift_right))
            own.wait()
            own(nc.vector.tensor_copy(src_chunks, taken.bitcast(I32)))
            own.wait()
            own(nc.vector.scalar_tensor_tensor(key_f, dst_f, float(NT), src_chunks, ALU.mult, ALU.add))
            own.wait()
            dve.wait_ge(pool_consts, 10)
            dve.wait_ge(spans_in, 16)
            def in_cols(v):
                return v.rearrange("p (t q) -> p t q", t=CT)

            def reach(r, w, op, at):
                own(nc.vector.scalar_tensor_tensor(in_cols(reached[0:GP, :]), chunk_ranges[0:GP, 1 - w, :, :],
                                                   group_edges[0:GP, w, r:r + 1], in_cols(count_up[0:GP, :]),
                                                   op, ALU.mult))
                own.wait()
                own(nc.vector.tensor_reduce(at, reached[0:GP, :], AX.X, ALU.max))
                own.wait()

            for r in range(ROUNDS):
                reach(r, 1, ALU.is_lt, group_span[0:GP, 1, r:r + 1])
            own(nc.vector.tensor_scalar(count_up, count_up, -1.0, float(NC + 1), ALU.mult, ALU.add))
            own.wait()
            for r in range(ROUNDS):
                reach(r, 0, ALU.is_ge, group_span[0:GP, 0, r:r + 1])
            lo, hi = group_span[0:GP, 0, :], group_span[0:GP, 1, :]
            own(nc.vector.tensor_scalar(lo, lo, -1.0, float(NC), ALU.mult, ALU.add))
            own(nc.vector.tensor_scalar(hi, hi, 3.0, None, ALU.add))
            own.wait()
            own(nc.vector.tensor_scalar(lo, lo, float(NC - 4), None, ALU.min))
            own.wait()
            lo_i, hi_i = four_span[0:GP, :, 0], four_span[0:GP, :, 1]
            own(nc.vector.tensor_copy(lo_i, lo))
            own(nc.vector.tensor_copy(hi_i, hi))
            own.wait()
            own(nc.vector.tensor_scalar(four_span[0:GP, :, :], four_span[0:GP, :, :], 2, None, ALU.logical_shift_right))
            own.wait()
            own(nc.vector.tensor_copy(lo, lo_i))
            own(nc.vector.tensor_copy(hi, hi_i))
            own.wait()
            own(nc.vector.scalar_tensor_tensor(hi, lo, 1.0, hi, ALU.add, ALU.max))
            own.wait()
            nc.vector.tensor_copy(hi_i, hi).then_inc(fours_found, 1)
            blocks = SLOTS * RUNS
            spans = range_row[:, :].rearrange("p (b c) -> p b c", c=2)
            own(nc.vector.memset(spans[:, :, 0], NT - 1))
            own(nc.vector.memset(spans[:, :, 1], NT))
            own.wait()
            top, back_up, seen, found = (stage_flat[0:1, k * RUNS:(k + 1) * RUNS] for k in range(4))
            at_block = stage_flat[0:1, 4 * RUNS:4 * RUNS + blocks]
            for w, op in enumerate((ALU.min, ALU.max)):
                own(nc.vector.tensor_copy(in_cols(reached[0:1, :]), chunk_ranges[0:1, w, :, :]))
                own.wait()
                own(nc.vector.tensor_reduce(at_block, reached[0:1, 0:blocks * COLS].rearrange(
                    "p (b c) -> p b c", c=COLS), AX.X, op))
                own.wait()
                own(nc.vector.tensor_copy(spans[:, 0:blocks, w], at_block))
                own.wait()
            own(nc.vector.tensor_scalar(spans[:, 0:blocks, :], spans[:, 0:blocks, :], 7, None, ALU.logical_shift_right))
            own.wait()
            own(nc.vector.tensor_scalar(spans[:, 0:blocks, 1], spans[:, 0:blocks, 1], 1.0, None, ALU.add))
            own.wait()
            nc.vector.engine_nop().then_inc(ranges_found, 1)
            dve.wait_ge(ranges_saved, 16)
            for w in range(2):
                own(nc.vector.tensor_scalar(spans[:, 0:blocks, w], spans[:, 0:blocks, w], float(T + w),
                                            float(NT - 1 + w), ALU.max, ALU.min))
            own(nc.vector.tensor_reduce(top, reached[0:1, 0:blocks * COLS].rearrange(
                "p (r c) -> p r c", r=RUNS), AX.X, ALU.max))
            own(nc.vector.tensor_scalar(back_up, count_up[0:1, 0:RUNS], -float(NC - RUNS), None, ALU.add))
            own.wait()
            own(nc.vector.scalar_tensor_tensor(seen, top, float(T * P), back_up, ALU.is_ge, ALU.mult))
            own.wait()
            own(nc.vector.tensor_reduce(found[:, 0:1], seen, AX.X, ALU.max))
            own.wait()
            own(nc.vector.tensor_scalar(found[:, 1:2], found[:, 0:1], -1.0, float(RUNS), ALU.mult, ALU.add))
            own.wait()
            own(nc.vector.tensor_scalar(found[:, 0:1], found[:, 1:2], float(RUNS - 1), None, ALU.min))
            own.wait()
            own(nc.vector.tensor_scalar(found[:, 1:2], found[:, 0:1], -1.0, float(RUNS - EARLY_RUNS), ALU.mult, ALU.add))
            own.wait()
            own(nc.vector.tensor_scalar(found[:, 1:2], found[:, 1:2], 1.0, None, ALU.max))
            own.wait()
            own(nc.vector.tensor_scalar(found[:, 2:3], found[:, 1:2], float(EARLY_RUNS), None, ALU.add))
            own.wait()
            own(nc.vector.tensor_copy(meta[:, 0:3], found[:, 0:3]))
            own.wait()
            nc.vector.engine_nop().then_inc(ranges_ready, 1)
            dve.wait_ge(x_in, 16 * 7)

            def group0(t0, nt, b, g):
                moments([tile_rows(t0 + j) for j in range(nt)])
                rsqrt(nt)
                dve.wait_ge(stage_free, g + 1)
                for j in range(nt):
                    nc.vector.tensor_scalar(stage[:, b, j, 0:D], tile_rows(t0 + j), rs[:, j:j + 1], nmr[:, j:j + 1],
                                            ALU.mult, ALU.add).then_inc(xn_ready, 1)
                dve.wait_ge(xn_ready, t0 + nt)
                v = rows[:, bass.ds(t0, nt), 0:D]
                nc.vector.tensor_tensor(v, v, stage[:, b, 0:nt, 0:D], ALU.add).then_inc(xs_ready, 1)
                dve.wait_ge(high_ready, g + 1)
                dve.sem_inc(dve_passed, 1)
                nc.vector.scalar_tensor_tensor(pieces[:, bass.ds(t0, nt), D:2 * D], stage[:, b, 0:nt, 0:D], SCALE,
                                               pieces[:, bass.ds(t0, nt), 0:D], ALU.mult, ALU.subtract
                                               ).then_inc(pieces_ready, nt)

            groups(dve, group0, own, 2 * (2 * G + RSQRT_STEPS))

            dve.wait_ge(cols_sb, COL_COPIES)
            dve.wait_ge(rows_spilled, 16 * (2 * PAIRS + 1))
            item = dve.alloc_register("dve_item")
            chunk = [dve.alloc_register(f"dve_chunk{r}") for r in range(SLOTS)]
            for r in chunk:
                dve.reg_mov(r, 0)
            dve.reg_mov(item, 0)
            summed = dve.alloc_register("dve_summed")
            dve.reg_mov(summed, T)
            dve.wait_ge(fours_in, 16)
            dve.wait_ge(fill_ready, 1 + SLOTS)
            first_run = dve.value_load(meta[0:1, 0:1], min_val=0, max_val=RUNS - 1)
            more_runs = dve.value_load(meta[0:1, 1:2], min_val=1, max_val=RUNS)
            group_fours = Ranges(dve, "dve_fours", TG // 2, NC // 4)
            block_tiles = Ranges(dve, "dve_tiles", SLOTS, NT)

            def one_hots(g, q):
                r = q % SLOTS
                with dve.Fori(*group_fours[q % (TG // 2)]) as n:
                    for h in range(4):
                        dve.reg_add(chunk[r], chunk[r], 1)
                        dve.wait_ge(hots_used[r], dve.snap(chunk[r]))
                        dve.sem_inc(dve_passed, 1)
                        nc.vector.tensor_scalar(hot[:, r, h, 0:P], lane16[:, 0:P],
                                                lane_col[:, bass.ds(n * 4 + h, 1)], None, ALU.is_equal)
                        nc.vector.tensor_scalar(hot[:, r, h, P:P + GW], lane16[:, :],
                                                key_col[:, bass.ds(n * 4 + h, 1)], group_base[:, bass.ds(g, 1)],
                                                ALU.subtract, ALU.is_equal).then_inc(hots_ready[r], 1)

            def sum_block(s, k, tiles):
                dve.wait_ge(index_in[s], k * 32 + 32)
                dve.sem_inc(dve_passed, 1)
                with dve.Fori(*tiles) as t:
                    dve.reg_add(item, item, 1)
                    n = dve.snap(item)
                    dve.wait_ge(sum_added, n)
                    dve.wait_ge(sum_ps, n)
                    v = sums[:, bass.ds(dve.snap(summed, min_val=0, max_val=NT - 1), 1), :].rearrange("p a d -> p (a d)")
                    nc.vector.tensor_tensor(v, v, pS[:, 0:CNT], ALU.add).then_inc(sum_added, 1)
                    nc.vector.tensor_scalar(dst_rel[:, :], dst_ix[:, s, :], tile_base[:, bass.ds(t, 1)], None,
                                            ALU.subtract).then_inc(rel_ready, 1)
                    dve.wait_ge(rel_ready, n)
                    nc.vector.tensor_tensor(onehot[:, :, :], lane[:, :].unsqueeze(1).to_broadcast([P, COLS, P]),
                                            dst_rel[:, :].unsqueeze(2).to_broadcast([P, COLS, P]),
                                            ALU.is_equal).then_inc(onehot_ready, 1)
                    dve.reg_mov(summed, t)

            def two_tiles(i, blocks, first):
                for tb in range(2):
                    for q in range(TG):
                        g = i * (2 * TG) + tb * TG + q
                        if q % (TG // 2) == 0:
                            group_fours.load(four_row, g)
                        one_hots(g, q)
                        if q == 0:
                            dve.wait_ge(sums_cleared, 1)
                        for n in range((tb * TG + q) * blocks, (tb * TG + q + 1) * blocks):
                            k = first + n // SLOTS
                            if n % SLOTS == 0:
                                block_tiles.load(range_row, run_of(nc, first_run, k) * SLOTS)
                            sum_block(n % SLOTS, k, block_tiles[n % SLOTS])

            two_tiles(0, HEAVY_BLOCKS, 0)
            with dve.Fori(1, T // 2) as i:
                two_tiles(i, 1, i * (2 * TG // SLOTS) + (HEAVY_RUNS - 2 * TG // SLOTS))
            with dve.Fori(0, more_runs) as k:
                block_tiles.load(range_row, run_of(nc, first_run, k + EARLY_RUNS) * SLOTS)
                for s in range(SLOTS):
                    sum_block(s, k + EARLY_RUNS, block_tiles[s])
            dve.wait_ge(sums_taken, T + 2)
            dve.wait_ge(lanes_kept, T)
            own(nc.vector.tensor_reduce(over_sb[:, 1:2], lane_edges[:, :], AX.X, ALU.max))
            own.wait()
            nc.vector.tensor_scalar(over_sb[:, 0:1], over_sb[:, 1:2], MOST / COUNT_SCALE, None, ALU.is_gt
                                    ).then_inc(over_found, 1)
            dve.wait_ge(over_ps, 1)
            own(nc.vector.tensor_scalar(over_sb[:, 1:2], pG[:, 0:1], 1.0, None, ALU.min))
            own.wait()
            own(nc.vector.tensor_scalar(over_sb[:, 2:3], over_sb[:, 1:2], -1.0, 1.0, ALU.mult, ALU.add))
            own.wait()
            own(nc.vector.tensor_scalar(over_sb[0:1, 3:4], over_sb[0:1, 1:2], float(SLOTS * RUNS - 1), 1.0,
                                        ALU.mult, ALU.add))
            own(nc.vector.tensor_scalar(over_sb[0:1, 4:5], over_sb[0:1, 2:3], float(PAD_RUNS * SLOTS - 1), None, ALU.mult))
            own.wait()
            own(nc.vector.tensor_copy(again[:, 0:1], over_sb[0:1, 4:5]))
            own(nc.vector.tensor_copy(again[:, 1:2], over_sb[0:1, 3:4]))
            dve.wait_ge(ranges_back, 16)
            for w in range(2):
                own(nc.vector.tensor_scalar(spans[:, :, w], spans[:, :, w], float(T - 1 + w), None, ALU.min))
            own.wait()
            nc.vector.engine_nop().then_inc(again_ready, 1)
            v = sums_flat[:, CNT:(T + 1) * CNT]
            dve.wait_ge(sum_added, dve.snap(item) + 1)
            dve.sem_inc(dve_passed, 1)
            own(nc.vector.tensor_scalar(v, v, over_sb[:, 2:3], None, ALU.mult))
            own.wait()
            dve.wait_ge(again_ready, 1)
            all_runs = dve.value_load(meta[0:1, 2:3], min_val=1, max_val=PAD_RUNS)
            first_block = dve.value_load(again[0:1, 0:1], min_val=0, max_val=PAD_RUNS * SLOTS - 1)
            blocks_again = dve.value_load(again[0:1, 1:2], min_val=1, max_val=SLOTS * RUNS)
            one_block = Ranges(dve, "dve_again", 1, NT)
            with dve.Fori(0, blocks_again) as j:
                one_block.load(range_row, block_of(nc, first_block, j))
                sum_block(0, all_runs + j, one_block[0])
            dve.wait_ge(sum_added, dve.snap(item) + 1)
            dve.wait_ge(sum_ps, dve.snap(item) + 1)
            v = sums[:, bass.ds(dve.snap(summed, min_val=0, max_val=NT - 1), 1), :].rearrange("p a d -> p (a d)")
            nc.vector.tensor_tensor(v, v, pS[:, 0:CNT], ALU.add).then_inc(all_added, 1)
            dve.wait_ge(all_added, 1)
            dve.wait_ge(back, 32)
            dve.wait_ge(w_l_in, 32)

            own(nc.vector.tensor_scalar(rdeg[:, :], sums[:, :, D], 1.0, None, ALU.max))
            own.wait()
            own(nc.vector.reciprocal(rdeg[:, :], rdeg[:, :]))
            own.wait()
            nc.vector.tensor_scalar(rdeg[:, :], rdeg[:, :], 1.0 / SCALE, None, ALU.mult).then_inc(sums_ready, 1)
            dve.wait_ge(sums_ready, 1)

            def group2(t0, nt, b, g):
                for j in range(nt):
                    dve.wait_ge(f_ps, t0 + j + 3)
                    nc.vector.tensor_tensor(tile_res(t0 + j), pR[j % 2][:, 0:D], tile_res(t0 + j),
                                            ALU.add).then_inc(f_sb, 1)
                dve.wait_ge(g_sb, t0 + nt)
                moments([tile_res(t0 + j) for j in range(nt)])
                rsqrt(nt)
                for j in range(nt):
                    own(nc.vector.scalar_tensor_tensor(stage[:, b, j, 0:D], tile_res(t0 + j), mv[:, j, 0:1],
                                                       gamma_sb, ALU.subtract, ALU.mult))
                own.wait()
                for j in range(nt):
                    own(nc.vector.scalar_tensor_tensor(tile_rows(t0 + j), stage[:, b, j, 0:D], rs[:, j:j + 1],
                                                       tile_rows(t0 + j), ALU.mult, ALU.add))
                own.wait()
                moments([tile_rows(t0 + j) for j in range(nt)])
                rsqrt(nt)
                own(nc.vector.tensor_copy(rows[:, bass.ds(t0, nt), RSTD], rs[:, 0:nt]))
                own(nc.vector.tensor_copy(rows[:, bass.ds(t0, nt), NMR], nmr[:, 0:nt]))
                for j in range(nt):
                    nc.vector.tensor_scalar(stage[:, b, j, 0:D], tile_rows(t0 + j), rs[:, j:j + 1], nmr[:, j:j + 1],
                                            ALU.mult, ALU.add).then_inc(x2_ready, 1)
                nc.vector.engine_nop().then_inc(x1_ready, 1)

            groups(dve, group2, own, 2 * (2 * (2 * G + RSQRT_STEPS) + 2 * G + 2))

            dve.wait_ge(gate_sb, 1 + 2 * PAIRS + 1)
            def wide(v):
                return v.unsqueeze(2).to_broadcast([P, NT, X])

            largest, best, total, where, over, keep = (small[:, k, :] for k in range(6))
            gate_b_wide = gate_b_sb[:, :].unsqueeze(1).to_broadcast([P, NT, X])
            own(nc.vector.tensor_tensor(logits[:, :, :], logits[:, :, :], gate_b_wide, ALU.add))
            own(nc.vector.tensor_scalar(descend, lane[:, 0:X].unsqueeze(1).to_broadcast([P, NT, X]), -1.0, float(X),
                                        ALU.mult, ALU.add))
            own.wait()
            own(nc.vector.tensor_reduce(largest, logits[:, :, :], AX.X, ALU.max))
            own.wait()
            nc.vector.tensor_tensor(before, logits[:, :, :], wide(largest), ALU.subtract).then_inc(shifted, 1)
            own(nc.vector.tensor_tensor(score, logits[:, :, :], wide(largest), ALU.is_equal))
            own.wait()
            own(nc.vector.tensor_tensor(score, score, descend, ALU.mult))
            own.wait()
            own(nc.vector.tensor_reduce(best, score, AX.X, ALU.max))
            own.wait()
            nc.vector.tensor_tensor(picked, descend, wide(best), ALU.is_equal).then_inc(picked_ready, 1)
            dve.wait_ge(exped, 1)
            own(nc.vector.tensor_reduce(total, before, AX.X, ALU.add))
            own.wait()
            own(nc.vector.reciprocal(rows[:, :, PROB:PROB + 1], total.unsqueeze(2)))
            own(nc.vector.tensor_copy(rows[:, :, TOKEN:TOKEN + 1].bitcast(I32), token_ix[:, :].unsqueeze(2)))
            own(nc.vector.memset(notfirst[:, :, :], 1.0))
            own.wait()
            own(nc.vector.memset(notfirst[:, :, 0:1], 0.0))
            dve.wait_ge(counts_ps, 2)
            own(nc.vector.tensor_copy(score.rearrange("p t e -> p (t e)").rearrange("p (e t) -> p e t", e=X),
                                      pR[1][:, 0:n8].rearrange("p (t e) -> p e t", e=X)))
            own.wait()
            own(nc.vector.tensor_tensor_scan(descend.rearrange("p t e -> p (t e)"),
                                             notfirst[:, :, :].rearrange("p e t -> p (e t)"),
                                             score.rearrange("p t e -> p (t e)"), 0.0, ALU.mult, ALU.add))
            own.wait()
            own(nc.vector.tensor_tensor(descend.rearrange("p t e -> p (t e)"), descend.rearrange("p t e -> p (t e)"),
                                        score.rearrange("p t e -> p (t e)"), ALU.subtract))
            own.wait()
            own(nc.vector.tensor_tensor(place, descend.rearrange("p t e -> p (t e)").rearrange("p (e t) -> p t e", e=X),
                                        pR[0][:, 0:n8].rearrange("p (t e) -> p t e", e=X), ALU.add))
            own.wait()
            own(nc.vector.tensor_tensor(place, place, picked, ALU.mult))
            own.wait()
            own(nc.vector.tensor_reduce(where, place, AX.X, ALU.add))
            own.wait()
            own(nc.vector.tensor_scalar(over, where, float(CAP), float(NOBODY), ALU.is_gt, ALU.mult))
            own(nc.vector.tensor_scalar(keep, best, -float(CAP), float(X * CAP - 1), ALU.mult, ALU.add))
            own.wait()
            own(nc.vector.tensor_tensor(keep, keep, where, ALU.add))
            own.wait()
            own(nc.vector.tensor_tensor(keep, keep, over, ALU.add))
            own.wait()
            nc.vector.tensor_copy(slot_ix[:, :], keep).then_inc(slots_ready, 1)
            own(nc.vector.memset(big, 1e4))
            own(nc.vector.memset(neg, -1e4))
            own(nc.vector.memset(zero, 0.0))
            own.wait()
            nc.vector.engine_nop().then_inc(slots_ready, 1)

            HUGE = 3.4028234e38

            def norm_rows(i, b):
                tok0 = i * (2 * TOK_TILES) + b * TOK_TILES
                dve.wait_ge(rows_in[b], i * 32 + 32)
                for m in range(TOK_TILES):
                    n = P if m < TOK_TILES - 1 else TOK_LAST
                    r = slot_rows[b]
                    dve.wait_ge(inT_sb, tok0 + m + 1)
                    nc.vector.tensor_scalar(normed[m % 2][0:n, :], r[0:n, m, 0:D], r[0:n, m, RSTD:RSTD + 1],
                                            r[0:n, m, NMR:NMR + 1], ALU.mult, ALU.add).then_inc(in_normed, 1)

            with dve.Fori(0, X // 2) as i:
                own.enter(i, 2 * TOK_TILES * 7)
                for b in range(2):
                    norm_rows(i, b)
                    tok0 = i * (2 * TOK_TILES) + b * TOK_TILES
                    dve.wait_ge(weights_in[b], i * 48 + 48)
                    for m in range(TOK_TILES):
                        n = P if m < TOK_TILES - 1 else TOK_LAST
                        r, y = slot_rows[b], final[m % 2][0:n, :]
                        dve.wait_ge(y_ps, tok0 + m + 2)
                        dve.wait_ge(final_free, tok0 + m + 1)
                        nc.vector.tensor_tensor(y, pR[m % 2][0:n, 0:D], b2_sb[b][0:n, :], ALU.add).then_inc(y_taken, 1)
                        dve.wait_ge(y_taken, tok0 + m + 3)
                        own(nc.vector.tensor_scalar(y, y, r[0:n, m, PROB:PROB + 1], None, ALU.mult))
                        own.wait()
                        own(nc.vector.tensor_tensor(mask[0][0:n, :], y, y, ALU.not_equal))
                        own(nc.vector.tensor_scalar(mask[1][0:n, :], y, HUGE, None, ALU.is_gt))
                        own(nc.vector.tensor_scalar(mask[2][0:n, :], y, -HUGE, None, ALU.is_lt))
                        for k, v in enumerate((zero, big, neg)):
                            own.wait_apart(dve_passed)
                            own(nc.vector.copy_predicated(y, mask[k][0:n, :], v[0:n, :]))
                        own.wait()
                        nc.vector.tensor_tensor(y, y, r[0:n, m, 0:D], ALU.add).then_inc(y_ready, 1)
            own.leave(X // 2)


_INS = ["x", "src", "dst", "L0_gnn_W_l", "L0_gnn_b_l", "L0_gnn_W_r", "L0_gnn_ln_gamma", "L0_gnn_ln_beta",
        "L0_ffn_gate_w", "L0_ffn_gate_b", "L0_ffn_w1", "L0_ffn_b1", "L0_ffn_w2", "L0_ffn_b2"]


def kernel(**inputs):
    import concourse.bacc as _bacc
    import numpy as _np
    from concourse import mybir as _mybir
    from concourse.bass_utils import run_bass_kernel_spmd as _run

    nc = _bacc.Bacc("TRN2", target_bir_lowering=False, num_devices=1)
    arrays, args = {}, []
    for name in _INS:
        a = _np.asarray(inputs[name])
        if name in ("L0_gnn_W_l", "L0_gnn_W_r"):
            a = a.T
        a = _np.ascontiguousarray(a)
        arrays[f"in_{name}"] = a
        args.append(nc.dram_tensor(f"in_{name}", a.shape, _mybir.dt.from_np(a.dtype), kind="ExternalInput").ap())
    args.append(nc.dram_tensor("out_rows", (N, D), F32, kind="ExternalOutput").ap())
    gnn_moe(nc, *args)
    r = _run(nc, [arrays], core_ids=[0])
    return r.results[0]["out_rows"]
```

```python
from contextlib import ExitStack

import concourse.bass as bass
from concourse import mybir

F32 = mybir.dt.float32
I32 = mybir.dt.int32
F16 = mybir.dt.float16
ALU = mybir.AluOpType
ACT = mybir.ActivationFunctionType
AX = mybir.AxisListType

P = 128
N, D = 6250, 256
E = 200000
X, F = 8, 1024
CAP = -(-5 * N // (4 * X))
EPS = 1e-5
NT = -(-N // P)
LAST = N - (NT - 1) * P
DK = D // P
FK = F // P
ROW = D + 4
PROB, TOKEN, RSTD, NMR = D, D + 1, D + 2, D + 3
NOBODY = 1 << 20

G = 8
PAIRS = (NT - 1) // (2 * G)
assert NT == PAIRS * 2 * G + 1

T = 8
assert T % 2 == 0
COLS = 6
BLOCK = P * COLS
SLOTS = 4
RUNS = -(-E // (BLOCK * SLOTS))
HEAVY = 2
HEAVY_BLOCKS = 2
HEAVY_RUNS = HEAVY * HEAVY_BLOCKS * (P // 8) // SLOTS
EARLY_RUNS = HEAVY_RUNS + (T - HEAVY) * (P // 8) // SLOTS
PAD_RUNS = RUNS + EARLY_RUNS
PADDED = PAD_RUNS * SLOTS * BLOCK
NO_EDGE = 1 << 20
PAD_P = 64
assert (PADDED - E) % PAD_P == 0
PAD_N = (PADDED - E) // PAD_P
CT = -(-E // (P * P))
NC = CT * P
GD = 8
NG = T * P // GD
TG = P // GD
GW = GD * NT
ROUNDS = -(-NG // P)
GP = NG // ROUNDS
assert NT * P + SLOTS * 2 * (P + GW) <= NT * ROW
MOST = 2048.0
assert NG == ROUNDS * GP and NC * P <= PADDED and GW <= 512
COUNT_SCALE = 16.0
CNT = D + 1
SCALE = 4096.0
GROW = 2 * D + 2

TOK_TILES = -(-CAP // P)
TOK_LAST = CAP - (TOK_TILES - 1) * P
HALVES = [(0, 512), (512, CAP - 512)]
RSQRT_GUESS = 0x5F3759DF
COL_COPIES = -(-2 * CT // 4)
SOURCES = [range(NT * u // TG, NT * (u + 1) // TG) for u in range(TG)]
assert TG == 4 * SLOTS


class Own:

    def __init__(self, eng, sem):
        self.eng, self.sem, self.n, self.off, self.per = eng, sem, 0, None, None

    def __call__(self, ins):
        ins.then_inc(self.sem, 1)
        self.n += 1
        return ins

    def wait(self):
        self.eng.wait_ge(self.sem, self.n if self.off is None else self.off + self.n)

    def wait_apart(self, passed):
        self.wait()
        self.eng.sem_inc(passed, 1)

    def enter(self, i, per):
        self.start, self.off, self.per = self.n, i * per, per

    def leave(self, trips):
        assert self.n - self.start == self.per, (self.n - self.start, self.per)
        self.n, self.off = self.start + self.per * trips, None


def groups(eng, body, own=None, per=0):
    with eng.Fori(0, PAIRS) as i:
        if own:
            own.enter(i, per)
        for b in range(2):
            body(i * (2 * G) + b * G, G, b, i * 2 + b)
    if own:
        own.leave(PAIRS)
    body(NT - 1, 1, 0, 2 * PAIRS)


class Ranges:

    def __init__(self, eng, name, count, highest):
        self.eng, self.highest = eng, highest
        self.regs = [eng.alloc_register(f"{name}{k}") for k in range(2 * count)]

    def load(self, row, first):
        self.eng.load(self.regs, row[0:1, bass.ds(first * 2, len(self.regs))])

    def __getitem__(self, k):
        lo, hi = self.regs[2 * k:2 * k + 2]
        return (self.eng.snap(lo, min_val=0, max_val=self.highest - 1),
                self.eng.snap(hi, min_val=1, max_val=self.highest))


def block_of(nc, first_block, j):
    return nc.s_assert_within(first_block + j, 0, PAD_RUNS * SLOTS - 1, skip_runtime_bounds_check_because=(
        "either the last of all blocks alone or the blocks from 0 to SLOTS * RUNS - 1"))


def run_of(nc, first_run, k):
    return nc.s_assert_within(first_run + k, 0, PAD_RUNS - 1, skip_runtime_bounds_check_because=(
        "the runs are first_run + at most max(RUNS - first_run, EARLY_RUNS + 1) - 1, with first_run < RUNS"))


def staggered(eng, ahead, body, own=None, per=0):
    ahead(0, G, 0, 0)
    with eng.Fori(0, PAIRS - 1) as i:
        if own:
            own.enter(i, per)
        for b in range(2):
            ahead(i * (2 * G) + (b + 1) * G, G, 1 - b, i * 2 + b + 1)
            body(i * (2 * G) + b * G, G, b, i * 2 + b)
    if own:
        own.leave(PAIRS - 1)
    t0, g = (PAIRS - 1) * 2 * G, 2 * (PAIRS - 1)
    for b in range(2):
        ahead(t0 + (b + 1) * G, G if b == 0 else 1, 1 - b, g + b + 1)
        body(t0 + b * G, G, b, g + b)
    body(NT - 1, 1, 0, 2 * PAIRS)


def gnn_moe(nc, x, src, dst, w_l, b_l, w_r, gamma, beta, gate_w, gate_b, w1, b1, w2, b2, out):
    ctx = ExitStack()
    with ctx:
        def sb(name, shape, dt=F32):
            return ctx.enter_context(nc.sbuf_tensor(name, shape, dt))

        def ps(name, shape):
            return ctx.enter_context(nc.psum_tensor(name, shape, F32))

        def sem(name):
            return ctx.enter_context(nc.semaphore(name))

        xn_table = nc.dram_tensor("xn_table", (N, 2 * D), F16).ap()
        slot_table = nc.dram_tensor("slot_table", (X * CAP, ROW), F32).ap()
        src_table = nc.dram_tensor("src_table", (PADDED,), I32).ap()
        dst_table = nc.dram_tensor("dst_table", (PADDED,), I32).ap()
        chunk_table = nc.dram_tensor("chunk_table", (2 * NC,), F32).ap()
        group_table = nc.dram_tensor("group_table", (NG * 2,), I32).ap()
        range_table = nc.dram_tensor("range_table", (2 * SLOTS * PAD_RUNS,), I32).ap()
        rows_table = nc.dram_tensor("rows_table", (P, NT, D), F32).ap()
        res_table = nc.dram_tensor("res_table", (P, NT, D), F32).ap()

        rows_flat = sb("rows", [P, NT * ROW])
        rows = rows_flat[:, :].rearrange("p (t d) -> p t d", t=NT)
        counts = rows_flat[:, 0:NT * P].bitcast(F16).rearrange("p (b h d) -> p b h d", b=2, h=NT)
        hot = rows_flat[:, NT * P:NT * P + SLOTS * 2 * (P + GW)].bitcast(F16).rearrange(
            "p (r h w) -> p r h w", r=SLOTS, h=4)
        res = sb("res", [P, NT * D])
        resid = res[:, :].rearrange("p (t d) -> p t d", t=NT)
        pieces = res[:, :].bitcast(F16).rearrange("p (t d) -> p t d", t=NT)
        sums_flat = sb("sums", [P, (NT + 1) * CNT])
        sums_from_one = sums_flat[:, :].rearrange("p (t d) -> p t d", t=NT + 1)
        sums = sums_from_one[:, 1:NT + 1, :]
        gath_flat = sb("gath", [P, SLOTS * COLS * GROW // 2])
        gath = gath_flat[:, :].bitcast(F16).rearrange("p (s k d) -> p s k d", s=SLOTS, k=COLS)
        res_stage = gath_flat[:, 0:2 * G * D].rearrange("p (b g d) -> p b g d", b=2, g=G)
        stage_flat = sb("stage", [P, 2 * G * ROW])
        stage = stage_flat[:, :].rearrange("p (b g d) -> p b g d", b=2, g=G)
        edge_cols = stage_flat[:, 0:2 * NC]
        lane_col, key_col = stage_flat[:, 0:NC + 3], stage_flat[:, NC:2 * NC + 3]

        pad_ix = stage_flat[0:PAD_P, 0:2 * PAD_N].bitcast(I32).rearrange("p (w n) -> p w n", w=2)
        onehot = sb("onehot", [P, COLS, P], F16)

        lane16 = sb("lane16", [P, GW], F16)
        ones16 = sb("ones16", [P, 2], F16)
        zeros16 = sb("zeros16", [P, P], F16)
        group_base = sb("group_base", [P, NG])
        group_edges = sb("group_edges", [P, 2, ROUNDS])
        group_span = sb("group_span", [P, 2, ROUNDS])
        chunks_of = sb("chunks_of", [P, ROUNDS, 2], I32)
        chunk_span = sb("chunk_span", [P, 2, CT])
        meta = sb("meta", [1, 4], I32)
        again = sb("again", [1, 2], I32)
        lane_edges = sb("lane_edges", [P, NG])
        lanes_now = sb("lanes_now", [P, 2, TG])
        over_sb = sb("over", [P, 6])
        ident = sb("ident", [P, P])
        upper = sb("upper", [P, P])
        ones = sb("ones", [P, P])
        lane = sb("lane", [P, P])
        tile_base = sb("tile_base", [P, NT])
        w_l_gamma = sb("w_l_gamma", [P, max(DK * D + D, 2 * SLOTS * PAD_RUNS)])
        w_l_sb = w_l_gamma[:, 0:DK * D].rearrange("p (k d) -> p k d", k=DK)
        gamma_sb = w_l_gamma[:, DK * D:DK * D + D]
        range_row = w_l_gamma[0:1, 0:2 * SLOTS * PAD_RUNS].bitcast(I32)
        gate_w_sb = sb("gate_w_sb", [P, DK, X])
        gate_b_sb = sb("gate_b_sb", [P, X])
        b1_rows = sb("b1_rows", [X * FK, P])
        b1_sb = sb("b1_sb", [P, X * FK])
        b1_now = sb("b1_now", [P, 2, FK])
        xT = sb("xT", [P, 2, D])
        x2T = gath_flat[:, 0:2 * D].rearrange("p (b d) -> p b d", b=2)
        src_ix = sb("src_ix", [P, SLOTS, COLS], I32)
        dst_ix = sb("dst_ix", [P, SLOTS, COLS], I32)
        bn = sb("bn", [P, G, 6])
        mv = sb("mv", [P, G, 2])
        var = sb("var", [P, G])
        rs = sb("rs", [P, G])
        nt_ = sb("nt_", [P, G])
        nmr = sb("nmr", [P, G])
        rdeg = sb("rdeg", [P, NT])
        routing = sb("routing", [P, NT * X + 6 * NT])
        logits = routing[:, 0:NT * X].rearrange("p (t e) -> p t e", e=X)
        small = routing[:, NT * X:].rearrange("p (k t) -> p k t", k=6)
        group_row = routing[0:1, 0:NG * 2].bitcast(I32)
        fill = sb("fill", [P, ROW])

        dst_chunks, src_chunks, dst_f, lane_f, key_f, count_up = (
            sums_flat[:, k * NC:(k + 1) * NC] for k in range(6))
        SPARE = 6 * NC + DK * D + 2 * D
        assert SPARE + 8 * RUNS <= (NT + 1) * CNT
        lane_key_f = sums_flat[:, 3 * NC:5 * NC]
        block_f = sums_flat[0:1, SPARE:SPARE + 8 * RUNS]
        ranges_flat, reached = sums_flat[:, 0:2 * NC], dst_f
        chunk_ranges = ranges_flat.rearrange("p (q w t) -> p w t q", w=2, q=P)
        o = 6 * NC
        w_r_sb = sums_flat[:, o:o + DK * D].rearrange("p (k d) -> p k d", k=DK)
        o += DK * D
        b_l_sb = sums_flat[:, o:o + D]
        beta_sb = sums_flat[:, o + D:o + 2 * D]
        n8 = NT * X

        def route(k):
            return stage_flat[:, k * n8:(k + 1) * n8].rearrange(
                "p (t e) -> p t e", e=X)

        picked, score, descend, before, place = (route(k) for k in range(5))
        notfirst = route(5).rearrange("p t e -> p (t e)").rearrange("p (e t) -> p e t", e=X)
        slot_ix = sb("slot_ix", [P, NT], I32)
        token_ix = sb("token_ix", [P, NT], I32)
        hidden = sums_flat[:, 0:FK * CAP].rearrange("p (f c) -> p f c", f=FK)
        inT = sums_flat[:, FK * CAP:FK * CAP + DK * CAP].rearrange("p (k c) -> p k c", k=DK)
        w1_sb = [gath_flat[:, 0:DK * F], res[:, 0:DK * F]]
        w2_sb = [gath_flat[:, DK * F:DK * F + FK * D], res[:, DK * F:DK * F + FK * D]]
        w1_sb = [w.rearrange("p (k f) -> p k f", k=DK) for w in w1_sb]
        w2_sb = [w.rearrange("p (k d) -> p k d", k=FK) for w in w2_sb]
        o = DK * F + FK * D
        b2_sb = [res[:, o + b * D:o + (b + 1) * D] for b in range(2)]
        o += 2 * D
        normed = [res[:, o + m * D:o + (m + 1) * D] for m in range(TOK_TILES)]
        o += TOK_TILES * D
        mask = [res[:, o + b * D:o + (b + 1) * D].bitcast(I32) for b in range(3)]
        o += 3 * D
        big, neg, zero = (res[:, o + b * D:o + (b + 1) * D] for b in range(3))
        o += 3 * D
        final = [res[:, o + b * D:o + (b + 1) * D] for b in range(2)]
        o += 2 * D
        slot_rows = [stage[:, b, :, :] for b in range(2)]

        pT = [ps(f"pT{b}", [P, 512]) for b in range(2)]
        pR = [ps(f"pR{b}", [P, 512]) for b in range(2)]
        pS = ps("pS", [P, 512])
        pG = ps("pG", [P, 512])
        pD = pR[0]
        pH = [ps(f"pH{b}", [P, 512]) for b in range(2)]

        x_in, consts_in, b1_in, table_filled = (sem(s) for s in (
            "x_in", "consts_in", "b1_in", "table_filled"))
        pe_passed, dve_passed = sem("pe_passed"), sem("dve_passed")
        pool_consts = sem("pool_consts")
        pool_step = sem("pool_step")
        dve_step = sem("dve_step")
        high_ready, pieces_ready = sem("high_ready"), sem("pieces_ready")
        xn_ready, xn_stored, stage_free, xs_ready, transposed0, xT_sb0, r_ps0, r_sb0, r_biased, b1T_ps, b1T_sb = (
            sem(s) for s in ("xn_ready", "xn_stored", "stage_free", "xs_ready", "transposed0", "xT_sb0", "r_ps0",
                             "r_sb0", "r_biased", "b1T_ps", "b1T_sb"))
        pads_set, padded, chunks_in, spans_found, spans_stored, spans_in, groups_found, groups_stored, groups_in = (
            sem(s) for s in ("pads_set", "padded", "chunks_in", "spans_found", "spans_stored", "spans_in", "groups_found",
                             "groups_stored", "groups_in"))
        fill_ready, rows_spilled, res_spilled, res_biased, ranges_ready = (sem(s) for s in (
            "fill_ready", "rows_spilled", "res_spilled", "res_biased", "ranges_ready"))
        cols_ps, cols_sb,  counts_ps1, counts_taken, tile_summed, sums_taken = (
            sem(s) for s in ("cols_ps", "cols_sb",  "counts_ps1",
                             "counts_taken", "tile_summed", "sums_taken"))
        lanes_kept = sem("lanes_kept")
        group_back, keys_made = sem("group_back"), sem("keys_made")
        sp_passed, ranges_found = sem("sp_passed"), sem("ranges_found")
        res_free, all_added, w_l_in = sem("res_free"), sem("all_added"), sem("w_l_in")
        ranges_saved, ranges_back, over_found, over_ps, again_ready = (sem(s) for s in (
            "ranges_saved", "ranges_back", "over_found", "over_ps", "again_ready"))
        hots_ready = [sem(f"hots_ready{r}") for r in range(SLOTS)]
        hots_used = [sem(f"hots_used{r}") for r in range(SLOTS)]
        empty_counts, back, sums_cleared, act_passed = (sem(s) for s in (
            "empty_counts", "back", "sums_cleared", "act_passed"))
        index_in = [sem(f"index_in{s}") for s in range(SLOTS)]
        gathered = [sem(f"gathered{s}") for s in range(SLOTS)]
        slot_claimed, block_done, onehot_ready, sum_ps, sum_added = (sem(s) for s in (
            "slot_claimed", "block_done", "onehot_ready", "sum_ps", "sum_added"))
        sums_ready, mean_ready, xT_ps2, xT_sb2, f_ps, g_sb, x1_ready, x1_stored, x2_ready, gT_ps, gT_sb, gate_ps, gate_sb = (
            sem(s) for s in ("sums_ready", "mean_ready", "xT_ps2", "xT_sb2", "f_ps", "g_sb", "x1_ready", "x1_stored",
                             "x2_ready", "gT_ps", "gT_sb", "gate_ps", "gate_sb"))
        shifted, exped, picked_ready, counts_ps, slots_ready, dispatched = (sem(s) for s in (
            "shifted", "exped", "picked_ready", "counts_ps", "slots_ready", "dispatched"))
        weights_in = [sem(f"weights_in{b}") for b in range(2)]
        rows_in = [sem(f"rows_in{b}") for b in range(2)]
        in_normed, inT_ps, inT_sb, hid_ps, hid_sb, y_ps, y_taken, y_ready = (sem(s) for s in (
            "in_normed", "inT_ps", "inT_sb", "hid_ps", "hid_sb", "y_ps", "y_taken", "y_ready"))
        b1_set = sem("b1_set")
        scattered = [sem(f"scattered{b}") for b in range(2)]
        scatter_claimed, final_free, tail_cleared = (sem(s) for s in ("scatter_claimed", "final_free", "tail_cleared"))

        CONSTS = 5 * 16
        block = ctx.enter_context(nc.Block())

        @block.sync
        def _(sp):
            sp.dma_start(dst_table[0:E].rearrange("(p n) -> p n", p=PAD_P), dst.rearrange("(p n) -> p n", p=PAD_P)
                         ).then_inc(padded, 16)
            sp.dma_start(src_table[0:E].rearrange("(p n) -> p n", p=PAD_P), src.rearrange("(p n) -> p n", p=PAD_P)
                         ).then_inc(padded, 16)
            sp.wait_ge(pads_set, 2)
            for w, at in enumerate((src_table, dst_table)):
                sp.dma_start(at[E:PADDED].rearrange("(p n) -> p n", p=PAD_P), pad_ix[:, w, :]).then_inc(padded, 16)
            sp.wait_ge(padded, 64)
            for at, of in ((dst_chunks, dst_table), (src_chunks, src_table)):
                sp.dma_start(at.bitcast(I32).rearrange("p (t e) -> p t e", t=CT),
                             of[0:NC * P].rearrange("(t p e) -> p t e", t=CT, p=P)).then_inc(chunks_in, 16)
            for c in range(6):
                sp.dma_start(rows[:, c * G:(c + 1) * G, 0:D],
                             x[c * G * P:(c + 1) * G * P, :].rearrange("(t p) d -> p t d", p=P)).then_inc(x_in, 16)
            sp.wait_ge(tail_cleared, 1)
            sp.dma_start(rows[0:LAST, NT - 1, 0:D], x[(NT - 1) * P:N, :]).then_inc(x_in, 16)
            sp.wait_ge(spans_found, 1)
            sp.dma_start(chunk_table.rearrange("(p w t) -> p w t", w=2, p=P), chunk_span[:, :, :]
                         ).then_inc(spans_stored, 16)
            sp.wait_ge(spans_stored, 16)
            sp.wait_ge(keys_made, 1)
            sp.dma_start(ranges_flat, chunk_table.rearrange("(a c) -> a c", a=1).to_broadcast([P, 2 * NC])
                         ).then_inc(spans_in, 16)
            def store_xn(t0, nt, b, g):
                sp.wait_ge(pieces_ready, t0 + nt)
                if nt == G:
                    sp.dma_start(xn_table[bass.ds(t0 * P, G * P), :].rearrange("(t p) d -> p t d", p=P),
                                 pieces[:, bass.ds(t0, G), :]).then_inc(xn_stored, 16)
                else:
                    sp.dma_start(xn_table[t0 * P:N, :], pieces[0:LAST, t0, :]).then_inc(xn_stored, 16)
                sp.wait_ge(transposed0, t0 + nt)
                sp.sem_inc(stage_free, 1)
                sp.wait_ge(r_biased, t0 + nt)
                sp.dma_start(rows_table[:, bass.ds(t0, nt), :], rows[:, bass.ds(t0, nt), 0:D]).then_inc(rows_spilled, 16)
                sp.wait_ge(res_biased, t0 + nt)
                sp.dma_start(res_table[:, bass.ds(t0, nt), :], res_stage[:, b, 0:nt, :]).then_inc(res_spilled, 16)
                sp.wait_ge(res_spilled, g * 16 + 16)
                sp.sem_inc(res_free, 1)

            groups(sp, store_xn)

            sp.wait_ge(groups_found, 1)
            sp.dma_start(group_table.rearrange("(r p c) -> p r c", r=ROUNDS, p=GP), chunks_of[0:GP, :, :]
                         ).then_inc(groups_stored, 16)
            sp.wait_ge(groups_stored, 16)
            sp.dma_start(group_row[:, :], group_table.rearrange("(a c) -> a c", a=1)).then_inc(groups_in, 16)

            sp.wait_ge(ranges_found, 1)
            sp.dma_start(range_table.rearrange("(a c) -> a c", a=1), range_row).then_inc(ranges_saved, 16)

            sp.wait_ge(ranges_saved, 16)
            sp.wait_ge(ranges_ready, 1)
            first_run = sp.value_load(meta[0:1, 0:1], min_val=0, max_val=RUNS - 1)
            all_runs = sp.value_load(meta[0:1, 2:3], min_val=1, max_val=PAD_RUNS)
            with sp.Fori(0, all_runs) as k:
                for s in range(SLOTS):
                    sp.wait_ge(block_done, k * SLOTS + s + 1)
                    for at, of in ((src_ix, src_table), (dst_ix, dst_table)):
                        sp.dma_start(at[:, s, :],
                                     of[bass.ds(run_of(nc, first_run, k) * (SLOTS * BLOCK) + s * BLOCK, BLOCK)
                                        ].rearrange("(p k) -> p k", k=COLS)).then_inc(index_in[s], 16)
            sp.wait_ge(block_done, all_runs * SLOTS + SLOTS)
            sp.sem_inc(sp_passed, 1)
            sp.dma_start(range_row, range_table.rearrange("(a c) -> a c", a=1)).then_inc(ranges_back, 16)
            sp.wait_ge(again_ready, 1)
            first_block = sp.value_load(again[0:1, 0:1], min_val=0, max_val=PAD_RUNS * SLOTS - 1)
            blocks_again = sp.value_load(again[0:1, 1:2], min_val=1, max_val=SLOTS * RUNS)
            with sp.Fori(0, blocks_again) as j:
                sp.wait_ge(block_done, all_runs * SLOTS + SLOTS + j)
                for at, of in ((src_ix, src_table), (dst_ix, dst_table)):
                    sp.dma_start(at[:, 0, :], of[bass.ds(block_of(nc, first_block, j) * BLOCK, BLOCK)
                                                 ].rearrange("(p k) -> p k", k=COLS)).then_inc(index_in[0], 16)

            sp.wait_ge(sums_taken, T + 2)

            def load_back(t0, nt, b, g):
                at = bass.ds(t0, nt) if nt > 1 else slice(t0, t0 + 1)
                sp.dma_start(resid[:, at, :], res_table[:, at, :]).then_inc(back, 16)
                sp.dma_start(rows[:, at, 0:D], rows_table[:, at, :]).then_inc(back, 16)
                sp.wait_ge(back, g * 32 + 32)
                sp.sem_inc(group_back, 1)

            groups(sp, load_back)

            def store_x1(t0, nt, b, g):
                sp.wait_ge(x1_ready, g + 1)
                if nt == G:
                    sp.dma_start(out[bass.ds(t0 * P, G * P), :].rearrange("(t p) d -> p t d", p=P),
                                 rows[:, bass.ds(t0, G), 0:D]).then_inc(x1_stored, 16)
                else:
                    sp.dma_start(out[t0 * P:N, :], rows[0:LAST, t0, 0:D]).then_inc(x1_stored, 16)

            groups(sp, store_x1)

            def load_weights(e, b):
                sp.dma_start(w1_sb[b], w1[e, :, :].rearrange("(k p) f -> p k f", p=P)).then_inc(weights_in[b], 16)
                sp.dma_start(w2_sb[b], w2[e, :, :].rearrange("(k p) d -> p k d", p=P)).then_inc(weights_in[b], 16)
                sp.dma_start(b2_sb[b], b2[e, :].rearrange("(a d) -> a d", a=1).to_broadcast([P, D])
                             ).then_inc(weights_in[b], 16)

            def load_rows(e, b):
                first = e * CAP
                full = (TOK_TILES - 1) * P
                sp.dma_start(slot_rows[b][:, 0:TOK_TILES - 1, :],
                             slot_table[bass.ds(first, full), :].rearrange("(t p) d -> p t d", p=P)
                             ).then_inc(rows_in[b], 16)
                sp.dma_start(slot_rows[b][0:TOK_LAST, TOK_TILES - 1, :],
                             slot_table[bass.ds(first + full, TOK_LAST), :]).then_inc(rows_in[b], 16)

            sp.wait_ge(slots_ready, 2)
            for b in range(2):
                load_weights(b, b)
            sp.wait_ge(dispatched, 16 * NT)
            for b in range(2):
                load_rows(b, b)
            with sp.Fori(1, X // 2) as i:
                for b in range(2):
                    sp.wait_ge(final_free, i * (2 * TOK_TILES) + (b - 1) * TOK_TILES + 2)
                    load_weights(i * 2 + b, b)
                    load_rows(i * 2 + b, b)

            sp.wait_ge(x1_stored, 16 * (2 * PAIRS + 1))
            for b in range(2):
                sp.wait_ge(scattered[b], 16 * X * TOK_TILES // 2)

        @block.gpsimd
        def _(pool):
            own = Own(pool, pool_step)
            nc.gpsimd.memset(rows[:, NT - 1, :], 0.0).then_inc(tail_cleared, 1)
            own(nc.gpsimd.memset(ones[:, :], 1.0))
            own(nc.gpsimd.memset(ident[:, :], 0.0))
            own.wait()
            nc.gpsimd.affine_select(out=ident[:, :], in_=ident[:, :], compare_op=ALU.not_equal, fill=1.0, base=0,
                                    pattern=[[-1, P]], channel_multiplier=1).then_inc(pool_consts, 1)
            nc.gpsimd.affine_select(out=upper[:, :], in_=ones[:, :], compare_op=ALU.is_ge, fill=0.0, base=0,
                                    pattern=[[1, P]], channel_multiplier=-1).then_inc(pool_consts, 1)
            own(nc.gpsimd.memset(ones16[:, :], 1.0))
            own(nc.gpsimd.memset(zeros16[:, :], 0.0))
            nc.gpsimd.iota(group_base[:, :], [[-GW, NG]], base=0, channel_multiplier=0,
                           allow_small_or_imprecise_dtypes=True).then_inc(pool_consts, 1)
            nc.gpsimd.iota(lane16[:, :], [[1, GW]], base=0, channel_multiplier=0,
                           allow_small_or_imprecise_dtypes=True).then_inc(pool_consts, 1)
            for w in range(2):
                nc.gpsimd.iota(group_edges[:, w, :], [[GD * GP, ROUNDS]], base=GD * w, channel_multiplier=GD,
                               allow_small_or_imprecise_dtypes=True).then_inc(pool_consts, 1)
            nc.gpsimd.iota(count_up, [[1, NC]], base=1, channel_multiplier=0,
                           allow_small_or_imprecise_dtypes=True).then_inc(pool_consts, 1)
            nc.gpsimd.iota(lane[:, :], [[1, P]], base=0, channel_multiplier=0,
                           allow_small_or_imprecise_dtypes=True).then_inc(pool_consts, 1)
            nc.gpsimd.iota(tile_base[:, :], [[P, NT]], base=0, channel_multiplier=0,
                           allow_small_or_imprecise_dtypes=True).then_inc(pool_consts, 1)
            nc.gpsimd.iota(token_ix[:, :], [[P, NT]], base=0, channel_multiplier=1).then_inc(pool_consts, 1)
            own(nc.gpsimd.memset(fill[:, :], 0.0))
            own.wait()
            nc.gpsimd.memset(fill[:, TOKEN:TOKEN + 1].bitcast(I32), NOBODY).then_inc(fill_ready, 1)

            def biases(t0, nt, b, g):
                pool.wait_ge(xs_ready, g + 1)
                v = rows[:, bass.ds(t0, nt), 0:D]
                nc.gpsimd.tensor_tensor(v, v, beta_sb[:, :].unsqueeze(1).to_broadcast([P, nt, D]),
                                        ALU.add).then_inc(r_biased, nt)
                pool.wait_ge(r_sb0, t0 + nt + 2)
                v = res_stage[:, b, 0:nt, :]
                nc.gpsimd.tensor_tensor(v, v, b_l_sb[:, :].unsqueeze(1).to_broadcast([P, nt, D]),
                                        ALU.add).then_inc(res_biased, nt)

            pool.wait_ge(consts_in, CONSTS)
            groups(pool, biases)

            pool.wait_ge(res_spilled, 16 * (2 * PAIRS + 1))
            for s in range(SLOTS):
                nc.gpsimd.memset(gath[:, s, :, 2 * D:2 * D + 1], 1.0).then_inc(fill_ready, 1)
            pool.wait_ge(xn_stored, 16 * (2 * PAIRS + 1))
            pool.wait_ge(ranges_ready, 1)
            all_runs = pool.value_load(meta[0:1, 2:3], min_val=1, max_val=PAD_RUNS)
            with pool.Fori(0, all_runs) as k:
                for s in range(SLOTS):
                    pool.wait_ge(index_in[s], k * 32 + 32)
                    pool.sem_inc(slot_claimed, 1)
                    for c in range(COLS):
                        nc.gpsimd.indirect_dma_start(
                            gath[:, s, c, 0:2 * D], None, xn_table,
                            bass.IndirectOffsetOnAxis(ap=src_ix[:, s, c:c + 1], axis=0)).then_inc(gathered[s], 16)
            pool.wait_ge(again_ready, 1)
            blocks_again = pool.value_load(again[0:1, 1:2], min_val=1, max_val=SLOTS * RUNS)
            with pool.Fori(0, blocks_again) as j:
                pool.wait_ge(index_in[0], all_runs * 32 + j * 32 + 32)
                pool.sem_inc(slot_claimed, 1)
                for c in range(COLS):
                    nc.gpsimd.indirect_dma_start(
                        gath[:, 0, c, 0:2 * D], None, xn_table,
                        bass.IndirectOffsetOnAxis(ap=src_ix[:, 0, c:c + 1], axis=0)).then_inc(gathered[0], 16)

            pool.wait_ge(slots_ready, 2)
            pool.wait_ge(table_filled, 32)
            for t in range(NT):
                n = P if t < NT - 1 else LAST
                nc.gpsimd.indirect_dma_start(
                    slot_table, bass.IndirectOffsetOnAxis(ap=slot_ix[0:n, t:t + 1], axis=0), rows[0:n, t, :], None,
                    bounds_check=X * CAP - 1, oob_is_err=False).then_inc(dispatched, 16)

            pool.wait_ge(x1_stored, 16 * (2 * PAIRS + 1))
            with pool.Fori(0, X // 2) as i:
                for b in range(2):
                    for m in range(TOK_TILES):
                        n = P if m < TOK_TILES - 1 else TOK_LAST
                        c = m % 2
                        k = b * TOK_TILES + m
                        pool.wait_ge(y_ready, i * (2 * TOK_TILES) + k + 1)
                        pool.sem_inc(scatter_claimed, 1)
                        nc.gpsimd.indirect_dma_start(
                            out, bass.IndirectOffsetOnAxis(ap=slot_rows[b][0:n, m, TOKEN:TOKEN + 1].bitcast(I32), axis=0),
                            final[c][0:n, :], None, bounds_check=N - 1, oob_is_err=False).then_inc(scattered[c], 16)
                        pool.wait_ge(scattered[c], i * (16 * TOK_TILES) + 16 * (k // 2 + 1))
                        pool.sem_inc(final_free, 1)

        @block.tensor
        def _(pe):
            def transpose_rows(at, of, n, ready, at_rows=P):
                for k in range(DK):
                    last = nc.tensor.transpose(at[:, k * P:k * P + n], of[0:n, k * P:(k + 1) * P], ident[0:n, 0:n])
                return last.then_inc(ready, 1)

            def linear(at, of, w, ready):
                for k in range(DK):
                    last = nc.tensor.matmul(at[:, 0:D], of[:, k * P:(k + 1) * P], w[:, k, :],
                                            start=(k == 0), stop=(k == DK - 1))
                return last.then_inc(ready, 1)

            pe.wait_ge(pool_consts, 10)
            pe.wait_ge(b1_in, 16)
            nc.tensor.transpose(pG[:, 0:X * FK], b1_rows[:, :], ident[0:X * FK, 0:X * FK]).then_inc(b1T_ps, 1)
            pe.wait_ge(consts_in, CONSTS)

            def transposes0(t0, j, b):
                pe.wait_ge(xn_ready, t0 + j + 1)
                pe.wait_ge(xT_sb0, t0 + j + 1)
                transpose_rows(pT[j % 2], stage[:, b, j, 0:D], P, transposed0)

            def linear0(t0, j):
                pe.wait_ge(xT_sb0, t0 + j + 3)
                pe.wait_ge(r_sb0, t0 + j + 1)
                linear(pR[j % 2], xT[:, j % 2, :], w_r_sb, r_ps0)

            def group0(t0, nt, b, g):
                for j in range(nt + 1):
                    if j < nt:
                        transposes0(t0, j, b)
                    if j > 0:
                        linear0(t0, j - 1)

            groups(pe, group0)

            for q in range(COL_COPIES):
                if q >= 2:
                    pe.wait_ge(cols_sb, q - 1)
                elif q == 0:
                    pe.wait_ge(xT_sb0, NT + 2)
                for k in range(4 * q, min(4 * q + 4, 2 * CT)):
                    last = nc.tensor.transpose(pT[q % 2][:, (k % 4) * P:(k % 4 + 1) * P],
                                               lane_key_f[:, k * P:(k + 1) * P], ident[:, :])
                last.then_inc(cols_ps, 1)

            item = pe.alloc_register("pe_item")
            chunk = [pe.alloc_register(f"pe_chunk{r}") for r in range(SLOTS)]
            for r in chunk:
                pe.reg_mov(r, 0)
            pe.reg_mov(item, 0)
            pe.wait_ge(groups_in, 16)
            pe.wait_ge(ranges_ready, 1)
            pe.wait_ge(r_sb0, NT + 2)
            pe.wait_ge(empty_counts, 1)
            first_run = pe.value_load(meta[0:1, 0:1], min_val=0, max_val=RUNS - 1)
            more_runs = pe.value_load(meta[0:1, 1:2], min_val=1, max_val=RUNS)
            group_chunks = Ranges(pe, "pe_chunks", TG // 2, NC)
            block_tiles = Ranges(pe, "pe_tiles", SLOTS, NT)

            def count_group(g, q):
                c, r = q % 2, q % SLOTS
                pe.wait_ge(counts_taken, g + 1)
                nc.tensor.matmul(pH[c][:, 0:GW], zeros16[:, :], lane16[:, :], start=True, stop=False)
                with pe.Fori(*group_chunks[q % (TG // 2)], 4):
                    for h in range(4):
                        pe.reg_add(chunk[r], chunk[r], 1)
                        pe.wait_ge(hots_ready[r], pe.snap(chunk[r]))
                        nc.tensor.matmul(pH[c][:, 0:GW], hot[:, r, h, 0:P], hot[:, r, h, P:P + GW],
                                         start=False, stop=False).then_inc(hots_used[r], 1)
                nc.tensor.matmul(pH[c][:, 0:GW], zeros16[:, :], lane16[:, :], start=False, stop=True
                                 ).then_inc(counts_ps1, 1)

            def sum_sources(b, sources):
                for h in sources:
                    first, last = h == 0, h == NT - 1
                    of = counts[:, b, h, :]
                    nc.tensor.matmul(pG[:, 0:1], of, ones16[:, 0:1], start=first, stop=last)
                    nc.tensor.matmul(pD[:, 0:D], of, pieces[:, h, D:2 * D], start=first, stop=False)
                    done = nc.tensor.matmul(pD[:, 0:D], of, pieces[:, h, 0:D], start=False, stop=last)
                if h == NT - 1:
                    done.then_inc(tile_summed, 1)

            def sum_block(s, k, tiles):
                pe.wait_ge(gathered[s], k * (16 * COLS) + 16 * COLS)
                pe.sem_inc(pe_passed, 1)
                with pe.Fori(*tiles):
                    pe.reg_add(item, item, 1)
                    pe.wait_ge(onehot_ready, pe.snap(item))
                    for c in range(COLS):
                        nc.tensor.matmul(pS[:, 0:CNT], onehot[:, c, :], gath[:, s, c, D:D + CNT],
                                         start=(c == 0), stop=False)
                        last = nc.tensor.matmul(pS[:, 0:D], onehot[:, c, :], gath[:, s, c, 0:D],
                                                start=False, stop=(c == COLS - 1))
                    last.then_inc(sum_ps, 1)
                nc.tensor.matmul(pT[0][:, 0:1], zeros16[:, :], ones16[:, 0:1], start=True, stop=True
                                 ).then_inc(block_done, 1)

            nc.tensor.matmul(pS[:, 0:CNT], zeros16[:, :], lane16[:, 0:CNT], start=True, stop=True).then_inc(sum_ps, 1)
            def two_tiles(i, blocks, first):
                for tb in range(2):
                    for q in range(TG):
                        g = i * (2 * TG) + tb * TG + q
                        if q % (TG // 2) == 0:
                            group_chunks.load(group_row, g)
                        count_group(g, q)
                        if q == 0:
                            pe.wait_ge(counts_taken, i * (2 * TG) + tb * TG + 2)
                            pe.wait_ge(sums_taken, i * 2 + tb + 1)
                        sum_sources(1 - tb, SOURCES[q])
                        for n in range((tb * TG + q) * blocks, (tb * TG + q + 1) * blocks):
                            k = first + n // SLOTS
                            if n % SLOTS == 0:
                                block_tiles.load(range_row, run_of(nc, first_run, k) * SLOTS)
                            sum_block(n % SLOTS, k, block_tiles[n % SLOTS])

            two_tiles(0, HEAVY_BLOCKS, 0)
            with pe.Fori(1, T // 2) as i:
                two_tiles(i, 1, i * (2 * TG // SLOTS) + (HEAVY_RUNS - 2 * TG // SLOTS))
            pe.wait_ge(counts_taken, NG + 2)
            pe.wait_ge(sums_taken, T + 1)
            sum_sources(1, range(NT))
            with pe.Fori(0, more_runs) as k:
                block_tiles.load(range_row, run_of(nc, first_run, k + EARLY_RUNS) * SLOTS)
                for s in range(SLOTS):
                    sum_block(s, k + EARLY_RUNS, block_tiles[s])

            pe.wait_ge(over_found, 1)
            nc.tensor.matmul(pG[:, 0:1], ones[:, :], over_sb[:, 0:1], start=True, stop=True).then_inc(over_ps, 1)
            pe.wait_ge(again_ready, 1)
            all_runs = pe.value_load(meta[0:1, 2:3], min_val=1, max_val=PAD_RUNS)
            first_block = pe.value_load(again[0:1, 0:1], min_val=0, max_val=PAD_RUNS * SLOTS - 1)
            blocks_again = pe.value_load(again[0:1, 1:2], min_val=1, max_val=SLOTS * RUNS)
            one_block = Ranges(pe, "pe_again", 1, NT)
            with pe.Fori(0, blocks_again) as j:
                one_block.load(range_row, block_of(nc, first_block, j))
                sum_block(0, all_runs + j, one_block[0])

            pe.wait_ge(w_l_in, 32)

            def linear2(t0, nt, b, g):
                pe.wait_ge(group_back, g + 1)
                for j in range(nt + 1):
                    if j < nt:
                        pe.wait_ge(xT_sb2, t0 + j + 1)
                        pe.wait_ge(mean_ready, t0 + j + 1)
                        transpose_rows(pT[j % 2], stage[:, b, j, 0:D], P, xT_ps2)
                    if j > 0:
                        pe.wait_ge(xT_sb2, t0 + j + 2)
                        pe.wait_ge(g_sb, t0 + j)
                        c = (j - 1) % 2
                        for k in range(DK):
                            nc.tensor.matmul(pR[c][:, 0:D], xT[:, c, k * P:(k + 1) * P], w_l_sb[:, k, :],
                                             start=(k == 0), stop=False)
                        nc.tensor.matmul(pR[c][:, 0:D], ident[:, :],
                                         resid[:, bass.ds(t0 + j - 1, 1), :].rearrange("p a d -> p (a d)"),
                                         start=False, stop=True).then_inc(f_ps, 1)

            def gate2(t0, nt, b, g):
                for j in range(nt + 1):
                    if j < nt:
                        pe.wait_ge(x2_ready, t0 + j + 1)
                        pe.wait_ge(gT_sb, t0 + j + 1)
                        transpose_rows(pH[j % 2], stage[:, b, j, 0:D], P, gT_ps)
                    if j > 0:
                        pe.wait_ge(gT_sb, t0 + j + 2)
                        if j == 1:
                            pe.wait_ge(gate_sb, g + 1)
                        for k in range(DK):
                            last = nc.tensor.matmul(pG[:, (j - 1) * X:j * X], x2T[:, (j - 1) % 2, k * P:(k + 1) * P],
                                                    gate_w_sb[:, k, :], start=(k == 0), stop=(k == DK - 1))
                        last.then_inc(gate_ps, 1)

            staggered(pe, linear2, gate2)

            pe.wait_ge(picked_ready, 1)
            flat = picked.rearrange("p t e -> p (t e)")
            nc.tensor.matmul(pR[0][:, 0:n8], upper[:, :], flat, start=True, stop=True).then_inc(counts_ps, 1)
            nc.tensor.matmul(pR[1][:, 0:n8], ones[:, :], flat, start=True, stop=True).then_inc(counts_ps, 1)

            def rows_of(m):
                return P if m < TOK_TILES - 1 else TOK_LAST

            def input_tile(tok0, m):
                pe.wait_ge(in_normed, tok0 + m + 1)
                pe.wait_ge(inT_sb, tok0 + m + 1)
                transpose_rows(pT[m % 2], normed[m], rows_of(m), inT_ps)

            def two_experts(i, last):
                for b in range(2):
                    tok0 = i * (2 * TOK_TILES) + b * TOK_TILES
                    pe.wait_ge(inT_sb, tok0 + TOK_TILES + 2)
                    pe.wait_ge(weights_in[b], i * 48 + 48)
                    for h, (c0, cn) in enumerate(HALVES):
                        for f in range(FK):
                            u = h * FK + f
                            pe.wait_ge(hid_sb, i * (4 * FK) + b * 2 * FK + u + 1)
                            for k in range(DK):
                                done = nc.tensor.matmul(pH[u % 2][:, 0:cn], w1_sb[b][:, k, f * P:(f + 1) * P],
                                                        inT[:, k, c0:c0 + cn], start=(k == 0), stop=(k == DK - 1))
                            done.then_inc(hid_ps, 1)
                    for m in range(TOK_TILES):
                        n = rows_of(m)
                        if not (last and b == 1):
                            input_tile(tok0 + TOK_TILES, m)
                        if m == 0:
                            pe.wait_ge(hid_sb, i * (4 * FK) + b * 2 * FK + FK + 2)
                        if m * P + n > HALVES[0][1] and m * P < HALVES[0][1] + P:
                            pe.wait_ge(hid_sb, i * (4 * FK) + b * 2 * FK + 2 * FK + 2)
                        pe.wait_ge(y_taken, tok0 + m + 1)
                        for f in range(FK):
                            done = nc.tensor.matmul(pR[m % 2][0:n, 0:D], hidden[:, f, m * P:m * P + n],
                                                    w2_sb[b][:, f, :], start=(f == 0), stop=(f == FK - 1))
                        done.then_inc(y_ps, 1)

            for m in range(TOK_TILES):
                input_tile(0, m)
            with pe.Fori(0, X // 2 - 1) as i:
                two_experts(i, False)
            two_experts(X // 2 - 1, True)

        @block.scalar
        def _(act):
            act.dma_start(w_r_sb, w_r.rearrange("(k p) n -> p k n", p=P)).then_inc(consts_in, 16)
            for at, of in ((b_l_sb, b_l), (beta_sb, beta), (gate_b_sb, gate_b)):
                act.dma_start(at[:, :], of.rearrange("(a d) -> a d", a=1).to_broadcast([P, at.shape[1]])
                              ).then_inc(consts_in, 16)
            act.dma_start(gate_w_sb[:, :, :], gate_w.rearrange("(k p) n -> p k n", p=P)).then_inc(consts_in, 16)
            act.dma_start(b1_rows[:, :], b1.rearrange("e (k p) -> (e k) p", p=P)).then_inc(b1_in, 16)
            for free, n in ((res_free, 2), (tile_summed, 1), (sums_taken, 1), (g_sb, 2), (xT_sb0, 2), (r_sb0, 2),
                            (xT_sb2, 2), (gT_sb, 2), (gate_sb, 1), (inT_sb, 2), (hid_sb, 2)):
                act.sem_inc(free, n)
            act.wait_ge(x_in, 16 * 7)
            act.wait_ge(fill_ready, 1)
            full = X * CAP // P
            act.dma_start(slot_table[0:full * P, :].rearrange("(p t) d -> p t d", p=P),
                          fill[:, :].unsqueeze(1).to_broadcast([P, full, ROW])).then_inc(table_filled, 16)
            act.dma_start(slot_table[full * P:X * CAP, :], fill[0:X * CAP - full * P, :]).then_inc(table_filled, 16)
            act.wait_ge(b1T_ps, 1)
            nc.scalar.copy(b1_sb[:, :], pG[:, 0:X * FK]).then_inc(b1T_sb, 1)

            def group0(t0, nt, b, g):
                act.wait_ge(xn_ready, t0 + nt)
                act.sem_inc(act_passed, 1)
                nc.scalar.activation(pieces[:, bass.ds(t0, nt), 0:D], stage[:, b, 0:nt, 0:D], ACT.Copy,
                                     scale=SCALE).then_inc(high_ready, 1)
                for j in range(nt + 1):
                    if j < nt:
                        act.wait_ge(transposed0, t0 + j + 1)
                        act.wait_ge(r_ps0, t0 + j + 1)
                        nc.scalar.copy(xT[:, j % 2, :], pT[j % 2][:, 0:D]).then_inc(xT_sb0, 1)
                    if j > 0:
                        act.wait_ge(r_ps0, t0 + j + 2)
                        if j == 1:
                            act.wait_ge(res_free, g + 1)
                        nc.scalar.copy(res_stage[:, b, j - 1, :],
                                       pR[(j - 1) % 2][:, 0:D]).then_inc(r_sb0, 1)

            act.sem_inc(r_ps0, 2)
            groups(act, group0)

            act.wait_ge(stage_free, 2 + 2 * PAIRS + 1)
            for q in range(COL_COPIES):
                act.wait_ge(cols_ps, q + 1)
                n = min(4, 2 * CT - 4 * q) * P
                nc.scalar.copy(edge_cols[:, 4 * q * P:4 * q * P + n], pT[q % 2][:, 0:n]).then_inc(cols_sb, 1)
            act.wait_ge(rows_spilled, 16 * (2 * PAIRS + 1))

            act.wait_ge(fill_ready, 1)
            nc.scalar.copy(rows_flat[:, NT * P // 2:NT * P], fill[:, 0:1].to_broadcast([P, NT * P // 2])
                           ).then_inc(empty_counts, 1)
            act.wait_ge(res_biased, NT)
            act.wait_ge(ranges_ready, 1)
            nc.scalar.copy(sums_flat[:, T * CNT:], fill[:, 0:1].to_broadcast([P, (NT + 1 - T) * CNT]))
            nc.scalar.copy(sums_flat[:, 0:T * CNT], fill[:, 0:1].to_broadcast([P, T * CNT])
                           ).then_inc(sums_cleared, 1)
            with act.Fori(0, T // 2) as i:
                for tb in range(2):
                    act.wait_ge(tile_summed, i * 2 + tb + 1)
                    for q in range(TG):
                        act.wait_ge(counts_ps1, i * (2 * TG) + tb * TG + q + 1)
                        nc.scalar.activation(counts[:, tb, :, q * GD:(q + 1) * GD].rearrange("p h d -> p d h"),
                                             pH[q % 2][:, 0:GW].rearrange("p (d h) -> p d h", d=GD), ACT.Copy,
                                             scale=1.0 / COUNT_SCALE, accum_out=lanes_now[:, tb, q:q + 1]
                                             ).then_inc(counts_taken, 1)
                    act.wait_ge(counts_taken, i * (2 * TG) + tb * TG + TG + 2)
                    act.sem_inc(act_passed, 1)
                    nc.scalar.copy(lane_edges[:, bass.ds(i * (2 * TG) + tb * TG, TG)], lanes_now[:, tb, :]
                                   ).then_inc(lanes_kept, 1)
                    act.wait_ge(tile_summed, i * 2 + tb + 2)
                    if tb == 0:
                        act.wait_ge(sums_cleared, 1)
                    act.sem_inc(act_passed, 1)
                    at = sums_from_one[:, bass.ds(i * 2 + tb, 1), :].rearrange("p a d -> p (a d)")
                    nc.scalar.activation(at[:, D:CNT], pG[:, 0:1], ACT.Copy, scale=COUNT_SCALE)
                    nc.scalar.activation(at[:, 0:D], pD[:, 0:D], ACT.Copy, scale=COUNT_SCALE).then_inc(sums_taken, 1)
            act.wait_ge(tile_summed, T + 2)
            nc.scalar.activation(sums_from_one[:, T, D:CNT], pG[:, 0:1], ACT.Copy, scale=COUNT_SCALE)
            nc.scalar.activation(sums_from_one[:, T, 0:D], pD[:, 0:D], ACT.Copy,
                                 scale=COUNT_SCALE).then_inc(sums_taken, 1)
            act.wait_ge(all_added, 1)
            act.dma_start(w_l_sb, w_l.rearrange("(k p) n -> p k n", p=P)).then_inc(w_l_in, 16)
            act.dma_start(gamma_sb, gamma.rearrange("(a d) -> a d", a=1).to_broadcast([P, D])).then_inc(w_l_in, 16)

            act.sem_inc(f_ps, 2)
            act.sem_inc(gate_ps, 2)
            act.wait_ge(sums_ready, 1)

            def linear2(t0, nt, b, g):
                def mean(j):
                    nc.scalar.activation(stage[:, b, j, 0:D],
                                         sums[:, bass.ds(t0 + j, 1), 0:D].rearrange("p a d -> p (a d)"), ACT.Copy,
                                         scale=rdeg[:, bass.ds(t0 + j, 1)]).then_inc(mean_ready, 1)

                mean(0)
                for j in range(nt + 2):
                    if j + 1 < nt:
                        mean(j + 1)
                    if j < nt:
                        act.wait_ge(xT_ps2, t0 + j + 1)
                        act.wait_ge(f_ps, t0 + j + 1)
                        nc.scalar.copy(xT[:, j % 2, :], pT[j % 2][:, 0:D]).then_inc(xT_sb2, 1)
                    if j > 1:
                        act.wait_ge(f_ps, t0 + j + 1)
                        act.sem_inc(act_passed, 1)
                        nc.scalar.activation(resid[:, bass.ds(t0 + j - 2, 1), :].rearrange("p a d -> p (a d)"),
                                             pR[j % 2][:, 0:D], ACT.Gelu).then_inc(g_sb, 1)

            def gate2(t0, nt, b, g):
                for j in range(nt):
                    act.wait_ge(gT_ps, t0 + j + 1)
                    act.wait_ge(gate_ps, t0 + j + 1)
                    nc.scalar.copy(x2T[:, j % 2, :], pH[j % 2][:, 0:D]).then_inc(gT_sb, 1)
                act.wait_ge(gate_ps, t0 + nt + 2)
                nc.scalar.copy(logits[:, bass.ds(t0, nt), :],
                               pG[:, 0:nt * X].rearrange("p (t e) -> p t e", e=X)).then_inc(gate_sb, 1)

            staggered(act, linear2, gate2)

            act.wait_ge(shifted, 1)
            nc.scalar.activation(before[:, :, :], before[:, :, :], ACT.Exp).then_inc(exped, 1)

            act.wait_ge(b1T_sb, 1)
            act.wait_ge(counts_ps, 2)
            act.sem_inc(hid_ps, 2)

            def input_tiles(tok0):
                for m in range(TOK_TILES):
                    n = P if m < TOK_TILES - 1 else TOK_LAST
                    act.wait_ge(inT_ps, tok0 + m + 1 + TOK_TILES)
                    nc.scalar.copy(inT[:, :, m * P:m * P + n],
                                   pT[m % 2][:, 0:D].rearrange("p (k c) -> p k c", k=DK)[:, :, 0:n]
                                   ).then_inc(inT_sb, 1)

            def two_experts(i, last):
                for b in range(2):
                    tok0 = i * (2 * TOK_TILES) + b * TOK_TILES
                    nc.scalar.copy(b1_now[:, b, :], b1_sb[:, bass.ds(i * (2 * FK) + b * FK, FK)]).then_inc(b1_set, 1)
                    act.wait_ge(b1_set, i * 2 + b + 1)
                    for h, (c0, cn) in enumerate(HALVES):
                        for f in range(FK):
                            u = h * FK + f
                            act.wait_ge(hid_ps, i * (4 * FK) + b * 2 * FK + u + 3)
                            if u == 0:
                                act.wait_ge(y_ps, tok0 + 1)
                            nc.scalar.activation(hidden[:, f, c0:c0 + cn], pH[u % 2][:, 0:cn], ACT.Relu,
                                                 bias=b1_now[:, b, f:f + 1]).then_inc(hid_sb, 1)
                    if not (last and b == 1):
                        input_tiles(tok0 + TOK_TILES)

            input_tiles(0)
            with act.Fori(0, X // 2 - 1) as i:
                two_experts(i, False)
            two_experts(X // 2 - 1, True)

        @block.vector
        def _(dve):
            own = Own(dve, dve_step)
            for free, n in ((stage_free, 2), (inT_ps, TOK_TILES), (block_done, SLOTS), (sum_added, 1),
                            *((used, 4) for used in hots_used), (counts_taken, 2), (y_taken, 2), (y_ps, 1),
                            (final_free, 2)):
                dve.sem_inc(free, n)

            def rsqrt(nt):
                v, y, w = var[:, 0:nt], rs[:, 0:nt], nt_[:, 0:nt]
                own(nc.vector.tensor_scalar(v, mv[:, 0:nt, 1], EPS, None, ALU.add))
                own.wait()
                own(nc.vector.tensor_scalar(w.bitcast(I32), v.bitcast(I32), 1, None, ALU.logical_shift_right))
                own.wait()
                own(nc.vector.tensor_scalar(y.bitcast(I32), w.bitcast(I32), -1.0, float(RSQRT_GUESS), ALU.mult, ALU.add))
                for _ in range(3):
                    own.wait()
                    own(nc.vector.scalar_tensor_tensor(w, y, -0.5, y, ALU.mult, ALU.mult))
                    own.wait()
                    own(nc.vector.tensor_tensor(w, w, v, ALU.mult))
                    own.wait()
                    own(nc.vector.scalar_tensor_tensor(y, w, 1.5, y, ALU.add, ALU.mult))
                own.wait()
                own(nc.vector.scalar_tensor_tensor(nmr[:, 0:nt], mv[:, 0:nt, 0], -1.0, y, ALU.mult, ALU.mult))
                own.wait()

            RSQRT_STEPS = 3 + 3 * 3 + 1

            def moments(views):
                dve.sem_inc(dve_passed, 1)
                for j, v in enumerate(views):
                    own(nc.vector.bn_stats(bn[:, j, :], v))
                own.wait_apart(dve_passed)
                for j in range(len(views)):
                    own(nc.vector.bn_aggr(mv[:, j, :], bn[:, j, :]))
                own.wait()

            def tile_rows(t):
                return rows[:, bass.ds(t, 1), 0:D].rearrange("p a d -> p (a d)")

            def tile_res(t):
                return resid[:, bass.ds(t, 1), :].rearrange("p a d -> p (a d)")

            nc.vector.memset(pad_ix[:, 0, :], 0).then_inc(pads_set, 1)
            nc.vector.memset(pad_ix[:, 1, :], NO_EDGE).then_inc(pads_set, 1)
            dve.wait_ge(chunks_in, 32)
            own(nc.vector.tensor_copy(dst_f, dst_chunks.bitcast(I32)))
            own.wait()
            for w, op in enumerate((ALU.min, ALU.max)):
                own(nc.vector.tensor_reduce(chunk_span[:, w, :], dst_f.rearrange("p (t e) -> p t e", t=CT), AX.X, op))
            own.wait()
            nc.vector.engine_nop().then_inc(spans_found, 1)
            taken = dst_chunks
            own(nc.vector.tensor_scalar(taken.bitcast(I32), src_chunks.bitcast(I32), P - 1, None, ALU.bitwise_and))
            own.wait()
            own(nc.vector.tensor_copy(lane_f, taken.bitcast(I32)))
            own.wait()
            own(nc.vector.tensor_scalar(taken.bitcast(I32), src_chunks.bitcast(I32), 7, None, ALU.logical_shift_right))
            own.wait()
            own(nc.vector.tensor_copy(src_chunks, taken.bitcast(I32)))
            own.wait()
            own(nc.vector.scalar_tensor_tensor(key_f, dst_f, float(NT), src_chunks, ALU.mult, ALU.add))
            own.wait()
            nc.vector.engine_nop().then_inc(keys_made, 1)
            dve.wait_ge(x_in, 16 * 7)

            def group0(t0, nt, b, g):
                moments([tile_rows(t0 + j) for j in range(nt)])
                rsqrt(nt)
                dve.wait_ge(stage_free, g + 1)
                for j in range(nt):
                    nc.vector.tensor_scalar(stage[:, b, j, 0:D], tile_rows(t0 + j), rs[:, j:j + 1], nmr[:, j:j + 1],
                                            ALU.mult, ALU.add).then_inc(xn_ready, 1)
                dve.wait_ge(xn_ready, t0 + nt)
                v = rows[:, bass.ds(t0, nt), 0:D]
                nc.vector.tensor_tensor(v, v, stage[:, b, 0:nt, 0:D], ALU.add).then_inc(xs_ready, 1)
                dve.wait_ge(high_ready, g + 1)
                dve.sem_inc(dve_passed, 1)
                nc.vector.scalar_tensor_tensor(pieces[:, bass.ds(t0, nt), D:2 * D], stage[:, b, 0:nt, 0:D], SCALE,
                                               pieces[:, bass.ds(t0, nt), 0:D], ALU.mult, ALU.subtract
                                               ).then_inc(pieces_ready, nt)

            groups(dve, group0, own, 2 * (2 * G + RSQRT_STEPS))

            dve.wait_ge(pool_consts, 10)
            dve.wait_ge(spans_in, 16)
            def in_cols(v):
                return v.rearrange("p (t q) -> p t q", t=CT)

            def reach(r, w, op, at):
                own(nc.vector.scalar_tensor_tensor(in_cols(reached[0:GP, :]), chunk_ranges[0:GP, 1 - w, :, :],
                                                   group_edges[0:GP, w, r:r + 1], in_cols(count_up[0:GP, :]),
                                                   op, ALU.mult))
                own.wait()
                own(nc.vector.tensor_reduce(at, reached[0:GP, :], AX.X, ALU.max))
                own.wait()

            for r in range(ROUNDS):
                reach(r, 1, ALU.is_lt, group_span[0:GP, 1, r:r + 1])
            own(nc.vector.tensor_scalar(count_up, count_up, -1.0, float(NC + 1), ALU.mult, ALU.add))
            own.wait()
            for r in range(ROUNDS):
                reach(r, 0, ALU.is_ge, group_span[0:GP, 0, r:r + 1])
            lo, hi = group_span[0:GP, 0, :], group_span[0:GP, 1, :]
            own(nc.vector.tensor_scalar(lo, lo, -1.0, float(NC), ALU.mult, ALU.add))
            own.wait()
            own(nc.vector.tensor_scalar(lo, lo, float(NC - 1), None, ALU.min))
            own.wait()
            own(nc.vector.scalar_tensor_tensor(hi, lo, 1.0, hi, ALU.add, ALU.max))
            own.wait()
            lo_i, hi_i = chunks_of[0:GP, :, 0], chunks_of[0:GP, :, 1]
            own(nc.vector.tensor_copy(lo_i, lo))
            own(nc.vector.tensor_copy(hi_i, hi))
            own.wait()
            nc.vector.engine_nop().then_inc(groups_found, 1)
            blocks = SLOTS * RUNS
            spans = range_row[:, :].rearrange("p (b c) -> p b c", c=2)
            own(nc.vector.memset(spans[:, :, 0], NT - 1))
            own(nc.vector.memset(spans[:, :, 1], NT))
            own.wait()
            top, back_up, seen, found = (block_f[:, k * RUNS:(k + 1) * RUNS] for k in range(4))
            at_block = block_f[:, 4 * RUNS:4 * RUNS + blocks]
            for w, op in enumerate((ALU.min, ALU.max)):
                own(nc.vector.tensor_copy(in_cols(reached[0:1, :]), chunk_ranges[0:1, w, :, :]))
                own.wait()
                own(nc.vector.tensor_reduce(at_block, reached[0:1, 0:blocks * COLS].rearrange(
                    "p (b c) -> p b c", c=COLS), AX.X, op))
                own.wait()
                own(nc.vector.tensor_copy(spans[:, 0:blocks, w], at_block))
                own.wait()
            own(nc.vector.tensor_scalar(spans[:, 0:blocks, :], spans[:, 0:blocks, :], 7, None, ALU.logical_shift_right))
            own.wait()
            own(nc.vector.tensor_scalar(spans[:, 0:blocks, 1], spans[:, 0:blocks, 1], 1.0, None, ALU.add))
            own.wait()
            nc.vector.engine_nop().then_inc(ranges_found, 1)
            dve.wait_ge(ranges_saved, 16)
            for w in range(2):
                own(nc.vector.tensor_scalar(spans[:, 0:blocks, w], spans[:, 0:blocks, w], float(T + w),
                                            float(NT - 1 + w), ALU.max, ALU.min))
            own(nc.vector.tensor_reduce(top, reached[0:1, 0:blocks * COLS].rearrange(
                "p (r c) -> p r c", r=RUNS), AX.X, ALU.max))
            own(nc.vector.tensor_scalar(back_up, count_up[0:1, 0:RUNS], -float(NC - RUNS), None, ALU.add))
            own.wait()
            own(nc.vector.scalar_tensor_tensor(seen, top, float(T * P), back_up, ALU.is_ge, ALU.mult))
            own.wait()
            own(nc.vector.tensor_reduce(found[:, 0:1], seen, AX.X, ALU.max))
            own.wait()
            own(nc.vector.tensor_scalar(found[:, 1:2], found[:, 0:1], -1.0, float(RUNS), ALU.mult, ALU.add))
            own.wait()
            own(nc.vector.tensor_scalar(found[:, 0:1], found[:, 1:2], float(RUNS - 1), None, ALU.min))
            own.wait()
            own(nc.vector.tensor_scalar(found[:, 1:2], found[:, 0:1], -1.0, float(RUNS - EARLY_RUNS), ALU.mult, ALU.add))
            own.wait()
            own(nc.vector.tensor_scalar(found[:, 1:2], found[:, 1:2], 1.0, None, ALU.max))
            own.wait()
            own(nc.vector.tensor_scalar(found[:, 2:3], found[:, 1:2], float(EARLY_RUNS), None, ALU.add))
            own.wait()
            own(nc.vector.tensor_copy(meta[:, 0:3], found[:, 0:3]))
            own.wait()
            nc.vector.engine_nop().then_inc(ranges_ready, 1)
            dve.wait_ge(cols_sb, COL_COPIES)
            own(nc.vector.memset(stage_flat[:, 2 * NC:2 * NC + 3], -1.0))
            own.wait()
            dve.wait_ge(rows_spilled, 16 * (2 * PAIRS + 1))
            item = dve.alloc_register("dve_item")
            chunk = [dve.alloc_register(f"dve_chunk{r}") for r in range(SLOTS)]
            for r in chunk:
                dve.reg_mov(r, 0)
            dve.reg_mov(item, 0)
            summed = dve.alloc_register("dve_summed")
            dve.reg_mov(summed, T)
            dve.wait_ge(groups_in, 16)
            dve.wait_ge(fill_ready, 1 + SLOTS)
            first_run = dve.value_load(meta[0:1, 0:1], min_val=0, max_val=RUNS - 1)
            more_runs = dve.value_load(meta[0:1, 1:2], min_val=1, max_val=RUNS)
            group_chunks = Ranges(dve, "dve_chunks", TG // 2, NC)
            block_tiles = Ranges(dve, "dve_tiles", SLOTS, NT)

            def one_hots(g, q):
                r = q % SLOTS
                with dve.Fori(*group_chunks[q % (TG // 2)], 4) as first:
                    for h in range(4):
                        dve.reg_add(chunk[r], chunk[r], 1)
                        dve.wait_ge(hots_used[r], dve.snap(chunk[r]))
                        dve.sem_inc(dve_passed, 1)
                        nc.vector.tensor_scalar(hot[:, r, h, 0:P], lane16[:, 0:P],
                                                lane_col[:, bass.ds(first + h, 1)], None, ALU.is_equal)
                        nc.vector.tensor_scalar(hot[:, r, h, P:P + GW], lane16[:, :],
                                                key_col[:, bass.ds(first + h, 1)], group_base[:, bass.ds(g, 1)],
                                                ALU.subtract, ALU.is_equal).then_inc(hots_ready[r], 1)

            def sum_block(s, k, tiles):
                dve.wait_ge(index_in[s], k * 32 + 32)
                dve.sem_inc(dve_passed, 1)
                with dve.Fori(*tiles) as t:
                    dve.reg_add(item, item, 1)
                    n = dve.snap(item)
                    dve.wait_ge(sum_added, n)
                    dve.wait_ge(sum_ps, n)
                    v = sums[:, bass.ds(dve.snap(summed, min_val=0, max_val=NT - 1), 1), :].rearrange("p a d -> p (a d)")
                    nc.vector.tensor_tensor(v, v, pS[:, 0:CNT], ALU.add).then_inc(sum_added, 1)
                    nc.vector.scalar_tensor_tensor(onehot[:, :, :], lane[:, :].unsqueeze(1).to_broadcast([P, COLS, P]),
                                                   tile_base[:, bass.ds(t, 1)],
                                                   dst_ix[:, s, :].unsqueeze(2).to_broadcast([P, COLS, P]),
                                                   ALU.add, ALU.is_equal).then_inc(onehot_ready, 1)
                    dve.reg_mov(summed, t)

            def two_tiles(i, blocks, first):
                for tb in range(2):
                    for q in range(TG):
                        g = i * (2 * TG) + tb * TG + q
                        if q % (TG // 2) == 0:
                            group_chunks.load(group_row, g)
                        one_hots(g, q)
                        if q == 0:
                            dve.wait_ge(sums_cleared, 1)
                        for n in range((tb * TG + q) * blocks, (tb * TG + q + 1) * blocks):
                            k = first + n // SLOTS
                            if n % SLOTS == 0:
                                block_tiles.load(range_row, run_of(nc, first_run, k) * SLOTS)
                            sum_block(n % SLOTS, k, block_tiles[n % SLOTS])

            two_tiles(0, HEAVY_BLOCKS, 0)
            with dve.Fori(1, T // 2) as i:
                two_tiles(i, 1, i * (2 * TG // SLOTS) + (HEAVY_RUNS - 2 * TG // SLOTS))
            with dve.Fori(0, more_runs) as k:
                block_tiles.load(range_row, run_of(nc, first_run, k + EARLY_RUNS) * SLOTS)
                for s in range(SLOTS):
                    sum_block(s, k + EARLY_RUNS, block_tiles[s])
            dve.wait_ge(sums_taken, T + 2)
            dve.wait_ge(lanes_kept, T)
            own(nc.vector.tensor_reduce(over_sb[:, 1:2], lane_edges[:, :], AX.X, ALU.max))
            own.wait()
            nc.vector.tensor_scalar(over_sb[:, 0:1], over_sb[:, 1:2], MOST / COUNT_SCALE, None, ALU.is_gt
                                    ).then_inc(over_found, 1)
            dve.wait_ge(over_ps, 1)
            own(nc.vector.tensor_scalar(over_sb[:, 1:2], pG[:, 0:1], 1.0, None, ALU.min))
            own.wait()
            own(nc.vector.tensor_scalar(over_sb[:, 2:3], over_sb[:, 1:2], -1.0, 1.0, ALU.mult, ALU.add))
            own.wait()
            own(nc.vector.tensor_scalar(over_sb[0:1, 3:4], over_sb[0:1, 1:2], float(SLOTS * RUNS - 1), 1.0,
                                        ALU.mult, ALU.add))
            own(nc.vector.tensor_scalar(over_sb[0:1, 4:5], over_sb[0:1, 2:3], float(PAD_RUNS * SLOTS - 1), None, ALU.mult))
            own.wait()
            own(nc.vector.tensor_copy(again[:, 0:1], over_sb[0:1, 4:5]))
            own(nc.vector.tensor_copy(again[:, 1:2], over_sb[0:1, 3:4]))
            dve.wait_ge(ranges_back, 16)
            for w in range(2):
                own(nc.vector.tensor_scalar(spans[:, :, w], spans[:, :, w], float(T - 1 + w), None, ALU.min))
            own.wait()
            nc.vector.engine_nop().then_inc(again_ready, 1)
            v = sums_flat[:, CNT:(T + 1) * CNT]
            dve.wait_ge(sum_added, dve.snap(item) + 1)
            dve.sem_inc(dve_passed, 1)
            own(nc.vector.tensor_scalar(v, v, over_sb[:, 2:3], None, ALU.mult))
            own.wait()
            dve.wait_ge(again_ready, 1)
            all_runs = dve.value_load(meta[0:1, 2:3], min_val=1, max_val=PAD_RUNS)
            first_block = dve.value_load(again[0:1, 0:1], min_val=0, max_val=PAD_RUNS * SLOTS - 1)
            blocks_again = dve.value_load(again[0:1, 1:2], min_val=1, max_val=SLOTS * RUNS)
            one_block = Ranges(dve, "dve_again", 1, NT)
            with dve.Fori(0, blocks_again) as j:
                one_block.load(range_row, block_of(nc, first_block, j))
                sum_block(0, all_runs + j, one_block[0])
            dve.wait_ge(sum_added, dve.snap(item) + 1)
            dve.wait_ge(sum_ps, dve.snap(item) + 1)
            v = sums[:, bass.ds(dve.snap(summed, min_val=0, max_val=NT - 1), 1), :].rearrange("p a d -> p (a d)")
            nc.vector.tensor_tensor(v, v, pS[:, 0:CNT], ALU.add).then_inc(all_added, 1)
            dve.wait_ge(all_added, 1)
            dve.wait_ge(w_l_in, 32)

            own(nc.vector.tensor_scalar(rdeg[:, :], sums[:, :, D], 1.0, None, ALU.max))
            own.wait()
            own(nc.vector.reciprocal(rdeg[:, :], rdeg[:, :]))
            own.wait()
            nc.vector.tensor_scalar(rdeg[:, :], rdeg[:, :], 1.0 / SCALE, None, ALU.mult).then_inc(sums_ready, 1)
            dve.wait_ge(sums_ready, 1)

            def group2(t0, nt, b, g):
                dve.wait_ge(group_back, g + 1)
                dve.wait_ge(g_sb, t0 + nt + 2)
                moments([tile_res(t0 + j) for j in range(nt)])
                rsqrt(nt)
                for j in range(nt):
                    own(nc.vector.scalar_tensor_tensor(stage[:, b, j, 0:D], tile_res(t0 + j), mv[:, j, 0:1],
                                                       gamma_sb, ALU.subtract, ALU.mult))
                own.wait()
                for j in range(nt):
                    own(nc.vector.scalar_tensor_tensor(tile_rows(t0 + j), stage[:, b, j, 0:D], rs[:, j:j + 1],
                                                       tile_rows(t0 + j), ALU.mult, ALU.add))
                own.wait()
                moments([tile_rows(t0 + j) for j in range(nt)])
                rsqrt(nt)
                own(nc.vector.tensor_copy(rows[:, bass.ds(t0, nt), RSTD], rs[:, 0:nt]))
                own(nc.vector.tensor_copy(rows[:, bass.ds(t0, nt), NMR], nmr[:, 0:nt]))
                for j in range(nt):
                    nc.vector.tensor_scalar(stage[:, b, j, 0:D], tile_rows(t0 + j), rs[:, j:j + 1], nmr[:, j:j + 1],
                                            ALU.mult, ALU.add).then_inc(x2_ready, 1)
                nc.vector.engine_nop().then_inc(x1_ready, 1)

            groups(dve, group2, own, 2 * (2 * (2 * G + RSQRT_STEPS) + 2 * G + 2))

            dve.wait_ge(gate_sb, 1 + 2 * PAIRS + 1)
            def wide(v):
                return v.unsqueeze(2).to_broadcast([P, NT, X])

            largest, best, total, where, over, keep = (small[:, k, :] for k in range(6))
            gate_b_wide = gate_b_sb[:, :].unsqueeze(1).to_broadcast([P, NT, X])
            own(nc.vector.tensor_tensor(logits[:, :, :], logits[:, :, :], gate_b_wide, ALU.add))
            own(nc.vector.tensor_scalar(descend, lane[:, 0:X].unsqueeze(1).to_broadcast([P, NT, X]), -1.0, float(X),
                                        ALU.mult, ALU.add))
            own.wait()
            own(nc.vector.tensor_reduce(largest, logits[:, :, :], AX.X, ALU.max))
            own.wait()
            nc.vector.tensor_tensor(before, logits[:, :, :], wide(largest), ALU.subtract).then_inc(shifted, 1)
            own(nc.vector.tensor_tensor(score, logits[:, :, :], wide(largest), ALU.is_equal))
            own.wait()
            own(nc.vector.tensor_tensor(score, score, descend, ALU.mult))
            own.wait()
            own(nc.vector.tensor_reduce(best, score, AX.X, ALU.max))
            own.wait()
            nc.vector.tensor_tensor(picked, descend, wide(best), ALU.is_equal).then_inc(picked_ready, 1)
            dve.wait_ge(exped, 1)
            own(nc.vector.tensor_reduce(total, before, AX.X, ALU.add))
            own.wait()
            own(nc.vector.reciprocal(rows[:, :, PROB:PROB + 1], total.unsqueeze(2)))
            own(nc.vector.tensor_copy(rows[:, :, TOKEN:TOKEN + 1].bitcast(I32), token_ix[:, :].unsqueeze(2)))
            own(nc.vector.memset(notfirst[:, :, :], 1.0))
            own.wait()
            own(nc.vector.memset(notfirst[:, :, 0:1], 0.0))
            dve.wait_ge(counts_ps, 2)
            own(nc.vector.tensor_copy(score.rearrange("p t e -> p (t e)").rearrange("p (e t) -> p e t", e=X),
                                      pR[1][:, 0:n8].rearrange("p (t e) -> p e t", e=X)))
            own.wait()
            own(nc.vector.tensor_tensor_scan(descend.rearrange("p t e -> p (t e)"),
                                             notfirst[:, :, :].rearrange("p e t -> p (e t)"),
                                             score.rearrange("p t e -> p (t e)"), 0.0, ALU.mult, ALU.add))
            own.wait()
            own(nc.vector.tensor_tensor(descend.rearrange("p t e -> p (t e)"), descend.rearrange("p t e -> p (t e)"),
                                        score.rearrange("p t e -> p (t e)"), ALU.subtract))
            own.wait()
            own(nc.vector.tensor_tensor(place, descend.rearrange("p t e -> p (t e)").rearrange("p (e t) -> p t e", e=X),
                                        pR[0][:, 0:n8].rearrange("p (t e) -> p t e", e=X), ALU.add))
            own.wait()
            own(nc.vector.tensor_tensor(place, place, picked, ALU.mult))
            own.wait()
            own(nc.vector.tensor_reduce(where, place, AX.X, ALU.add))
            own.wait()
            own(nc.vector.tensor_scalar(over, where, float(CAP), float(NOBODY), ALU.is_gt, ALU.mult))
            own(nc.vector.tensor_scalar(keep, best, -float(CAP), float(X * CAP - 1), ALU.mult, ALU.add))
            own.wait()
            own(nc.vector.tensor_tensor(keep, keep, where, ALU.add))
            own.wait()
            own(nc.vector.tensor_tensor(keep, keep, over, ALU.add))
            own.wait()
            nc.vector.tensor_copy(slot_ix[:, :], keep).then_inc(slots_ready, 1)
            own(nc.vector.memset(big, 1e4))
            own(nc.vector.memset(neg, -1e4))
            own(nc.vector.memset(zero, 0.0))
            own.wait()
            nc.vector.engine_nop().then_inc(slots_ready, 1)

            HUGE = 3.4028234e38

            def norm_rows(tok0, b, turn):
                dve.wait_ge(rows_in[b], turn)
                for m in range(TOK_TILES):
                    n = P if m < TOK_TILES - 1 else TOK_LAST
                    r = slot_rows[b]
                    dve.wait_ge(inT_ps, tok0 + m + 1)
                    nc.vector.tensor_scalar(normed[m][0:n, :], r[0:n, m, 0:D], r[0:n, m, RSTD:RSTD + 1],
                                            r[0:n, m, NMR:NMR + 1], ALU.mult, ALU.add).then_inc(in_normed, 1)

            def two_experts(i, last):
                for b in range(2):
                    tok0 = i * (2 * TOK_TILES) + b * TOK_TILES
                    if not (last and b == 1):
                        norm_rows(tok0 + TOK_TILES, 1 - b, i * 32 + (b * 32 + 32))
                    dve.wait_ge(weights_in[b], i * 48 + 48)
                    for m in range(TOK_TILES):
                        n = P if m < TOK_TILES - 1 else TOK_LAST
                        r, y = slot_rows[b], final[m % 2][0:n, :]
                        dve.wait_ge(y_ps, tok0 + m + 2)
                        dve.wait_ge(final_free, tok0 + m + 1)
                        nc.vector.tensor_tensor(y, pR[m % 2][0:n, 0:D], b2_sb[b][0:n, :], ALU.add).then_inc(y_taken, 1)
                        dve.wait_ge(y_taken, tok0 + m + 3)
                        own(nc.vector.tensor_scalar(y, y, r[0:n, m, PROB:PROB + 1], None, ALU.mult))
                        own.wait()
                        own(nc.vector.tensor_tensor(mask[0][0:n, :], y, y, ALU.not_equal))
                        own(nc.vector.tensor_scalar(mask[1][0:n, :], y, HUGE, None, ALU.is_gt))
                        own(nc.vector.tensor_scalar(mask[2][0:n, :], y, -HUGE, None, ALU.is_lt))
                        for k, v in enumerate((zero, big, neg)):
                            own.wait_apart(dve_passed)
                            own(nc.vector.copy_predicated(y, mask[k][0:n, :], v[0:n, :]))
                        own.wait()
                        nc.vector.tensor_tensor(y, y, r[0:n, m, 0:D], ALU.add).then_inc(y_ready, 1)

            norm_rows(0, 0, 32)
            with dve.Fori(0, X // 2 - 1) as i:
                own.enter(i, 2 * TOK_TILES * 7)
                two_experts(i, False)
            own.leave(X // 2 - 1)
            two_experts(X // 2 - 1, True)


_INS = ["x", "src", "dst", "L0_gnn_W_l", "L0_gnn_b_l", "L0_gnn_W_r", "L0_gnn_ln_gamma", "L0_gnn_ln_beta",
        "L0_ffn_gate_w", "L0_ffn_gate_b", "L0_ffn_w1", "L0_ffn_b1", "L0_ffn_w2", "L0_ffn_b2"]


def kernel(**inputs):
    import concourse.bacc as _bacc
    import numpy as _np
    from concourse import mybir as _mybir
    from concourse.bass_utils import run_bass_kernel_spmd as _run

    nc = _bacc.Bacc("TRN2", target_bir_lowering=False, num_devices=1)
    arrays, args = {}, []
    for name in _INS:
        a = _np.asarray(inputs[name])
        if name in ("L0_gnn_W_l", "L0_gnn_W_r"):
            a = a.T
        a = _np.ascontiguousarray(a)
        arrays[f"in_{name}"] = a
        args.append(nc.dram_tensor(f"in_{name}", a.shape, _mybir.dt.from_np(a.dtype), kind="ExternalInput").ap())
    args.append(nc.dram_tensor("out_rows", (N, D), F32, kind="ExternalOutput").ap())
    gnn_moe(nc, *args)
    r = _run(nc, [arrays], core_ids=[0])
    return r.results[0]["out_rows"]
```
